# Optimizing a Trainium2 kernel written in Bass

```python
import numpy as np
import jax
import jax.numpy as jnp

def _softmax(x, axis=-1):
    return jax.nn.softmax(x, axis=axis)

def _gelu(x):
    return jax.nn.gelu(x, approximate=True)

def _silu(x):
    return jax.nn.silu(x)

def _sigmoid(x):
    return jax.nn.sigmoid(x)

def _layernorm(x, axis=-1, eps=1e-05):
    m = jnp.mean(x, axis=axis, keepdims=True)
    v = jnp.var(x, axis=axis, keepdims=True)
    return (x - m) / jnp.sqrt(v + eps)

def _scatter_add(tgt, idx, src, axis=0):
    return tgt.at[idx].add(src)

def _segment_sum(src, seg, n):
    return jax.ops.segment_sum(src, seg, n)
kernel_name = 'mk_gnn_resnorm_d2_gnn_r32_39a6f3'

def setup_inputs(seed: int=0):
    np.random.seed(seed)
    _w = jnp.asarray

    def _rec_inputs():
        import jax
        import jax.numpy as jnp
        _gk = jax.random.key(seed)
        x = -7.329e-05 + 0.9999 * jax.random.normal(jax.random.fold_in(_gk, 1), (10000, 512), jnp.float32)
        _s = jax.random.randint(jax.random.fold_in(_gk, 2), (2500,), 0, 10000, jnp.int32)
        _d = jax.random.randint(jax.random.fold_in(_gk, 3), (2500,), 0, 10000, jnp.int32)
        _loop = jnp.arange(10000, dtype=jnp.int32)
        src = jnp.concatenate([_s, _d, _loop])
        dst = jnp.concatenate([_d, _s, _loop])
        _o = jnp.argsort(dst, stable=True)
        src = src[_o]
        dst = dst[_o]
        return (x, src, dst)
    x, src, dst = _rec_inputs()

    def _L0_gnn_setup():
        import jax, jax.numpy as jnp
        import numpy as np
        N_NODES = 3125
        N_EDGES = 25600
        D = 512
        L = 3
        LN_EPS = 1e-05
        key = jax.random.key(seed)
        ks = jax.random.split(key, 8)
        x = jax.random.normal(ks[0], (N_NODES, D), dtype=jnp.float32)
        edge_index = jax.random.randint(ks[1], (2, N_EDGES), 0, N_NODES, dtype=jnp.int32)
        scale = 1.0 / np.sqrt(D)
        W_l = jax.random.normal(ks[2], (L, D, D), dtype=jnp.float32) * scale
        W_r = jax.random.normal(ks[3], (L, D, D), dtype=jnp.float32) * scale
        b = jax.random.normal(ks[4], (L, D), dtype=jnp.float32) * 0.01
        ln_g = jnp.ones((L, D), dtype=jnp.float32)
        ln_b = jnp.zeros((L, D), dtype=jnp.float32)
        return {'x': x, 'edge_index': edge_index, 'W_l': W_l, 'W_r': W_r, 'b': b, 'ln_g': ln_g, 'ln_b': ln_b}
    _L0_gnn_all = _L0_gnn_setup()
    _L0_gnn_in = {k: v for k, v in _L0_gnn_all.items() if k in ('W_l', 'W_r', 'b', 'ln_g', 'ln_b')}
    del _L0_gnn_all

    def _L1_gnn_setup():
        import jax, jax.numpy as jnp
        import numpy as np
        N, E, DM, H, DFF = (625, 20000, 512, 8, 64)
        DK = DM // H

        def _layernorm(x, g, b, eps=1e-05):
            mu = jnp.mean(x, axis=-1, keepdims=True)
            var = jnp.mean(jnp.square(x - mu), axis=-1, keepdims=True)
            return (x - mu) * jax.lax.rsqrt(var + eps) * g + b
        key = jax.random.key(seed)
        ks = jax.random.split(key, 12)
        s = 0.02
        h = jax.random.normal(ks[0], (N, DM), dtype=jnp.float32)
        src = jax.random.randint(ks[1], (E,), 0, N, dtype=jnp.int32)
        dst = jnp.sort(jax.random.randint(ks[2], (E,), 0, N, dtype=jnp.int32))
        return {'h': h, 'src': src, 'dst': dst, 'Wq': jax.random.normal(ks[3], (DM, DM), dtype=jnp.float32) * s, 'Wk': jax.random.normal(ks[4], (DM, DM), dtype=jnp.float32) * s, 'Wv': jax.random.normal(ks[5], (DM, DM), dtype=jnp.float32) * s, 'Wo': jax.random.normal(ks[6], (DM, DM), dtype=jnp.float32) * s, 'ln1_g': jnp.ones((DM,), jnp.float32), 'ln1_b': jnp.zeros((DM,), jnp.float32), 'ln2_g': jnp.ones((DM,), jnp.float32), 'ln2_b': jnp.zeros((DM,), jnp.float32), 'W1': jax.random.normal(ks[7], (DM, DFF), dtype=jnp.float32) * s, 'b1': jnp.zeros((DFF,), jnp.float32), 'W2': jax.random.normal(ks[8], (DFF, DM), dtype=jnp.float32) * s, 'b2': jnp.zeros((DM,), jnp.float32)}
    _L1_gnn_all = _L1_gnn_setup()
    _L1_gnn_in = {k: v for k, v in _L1_gnn_all.items() if k in ('Wq', 'Wk', 'Wv', 'Wo', 'ln1_g', 'ln1_b', 'ln2_g', 'ln2_b', 'W1', 'b1', 'W2', 'b2')}
    del _L1_gnn_all
    return {'x': x, 'src': src, 'dst': dst, 'L0_gnn_W_l': _L0_gnn_in['W_l'], 'L0_gnn_W_r': _L0_gnn_in['W_r'], 'L0_gnn_b': _L0_gnn_in['b'], 'L0_gnn_ln_g': _L0_gnn_in['ln_g'], 'L0_gnn_ln_b': _L0_gnn_in['ln_b'], 'L1_gnn_Wq': _L1_gnn_in['Wq'], 'L1_gnn_Wk': _L1_gnn_in['Wk'], 'L1_gnn_Wv': _L1_gnn_in['Wv'], 'L1_gnn_Wo': _L1_gnn_in['Wo'], 'L1_gnn_ln1_g': _L1_gnn_in['ln1_g'], 'L1_gnn_ln1_b': _L1_gnn_in['ln1_b'], 'L1_gnn_ln2_g': _L1_gnn_in['ln2_g'], 'L1_gnn_ln2_b': _L1_gnn_in['ln2_b'], 'L1_gnn_W1': _L1_gnn_in['W1'], 'L1_gnn_b1': _L1_gnn_in['b1'], 'L1_gnn_W2': _L1_gnn_in['W2'], 'L1_gnn_b2': _L1_gnn_in['b2']}

def reference(x, src, dst, L0_gnn_W_l, L0_gnn_W_r, L0_gnn_b, L0_gnn_ln_g, L0_gnn_ln_b, L1_gnn_Wq, L1_gnn_Wk, L1_gnn_Wv, L1_gnn_Wo, L1_gnn_ln1_g, L1_gnn_ln1_b, L1_gnn_ln2_g, L1_gnn_ln2_b, L1_gnn_W1, L1_gnn_b1, L1_gnn_W2, L1_gnn_b2):
    import jax
    import jax.numpy as jnp

    def _L0_gnn_ref(x, edge_index, W_l, W_r, b, ln_g, ln_b):
        import jax, jax.numpy as jnp
        import numpy as np
        N_NODES = 3125
        N_EDGES = 25600
        D = 512
        L = 3
        LN_EPS = 1e-05
        src = edge_index[0]
        tgt = edge_index[1]
        n = x.shape[0]
        cnt = jax.ops.segment_sum(jnp.ones((src.shape[0],), x.dtype), tgt, num_segments=n)
        inv_cnt = (1.0 / jnp.maximum(cnt, 1.0))[:, None]
        for i in range(W_l.shape[0]):
            x_in = x
            agg = jax.ops.segment_sum(x[src], tgt, num_segments=n) * inv_cnt
            h = agg @ W_l[i].T + x @ W_r[i].T + b[i]
            mu = jnp.mean(h, axis=-1, keepdims=True)
            var = jnp.mean(jnp.square(h - mu), axis=-1, keepdims=True)
            h = (h - mu) * jax.lax.rsqrt(var + LN_EPS) * ln_g[i] + ln_b[i]
            h = jax.nn.relu(h)
            x = h + x_in
        return x

    def _L1_gnn_ref(h, src, dst, Wq, Wk, Wv, Wo, ln1_g, ln1_b, ln2_g, ln2_b, W1, b1, W2, b2):
        import jax, jax.numpy as jnp
        import numpy as np
        N, E, DM, H, DFF = (625, 20000, 512, 8, 64)
        DK = DM // H

        def _layernorm(x, g, b, eps=1e-05):
            mu = jnp.mean(x, axis=-1, keepdims=True)
            var = jnp.mean(jnp.square(x - mu), axis=-1, keepdims=True)
            return (x - mu) * jax.lax.rsqrt(var + eps) * g + b
        n = h.shape[0]
        q = (h @ Wq).reshape(n, H, DK)
        k = (h @ Wk).reshape(n, H, DK)
        v = (h @ Wv).reshape(n, H, DK)
        e = jnp.einsum('ehd,ehd->eh', k[src], q[dst]) / np.sqrt(DK).astype(np.float32)
        m = jax.ops.segment_max(e, dst, num_segments=n)
        ex = jnp.exp(e - m[dst])
        z = jax.ops.segment_sum(ex, dst, num_segments=n)
        attn = ex / z[dst]
        a = jax.ops.segment_sum(attn[:, :, None] * v[src], dst, num_segments=n)
        a = a.reshape(n, DM)
        o = a @ Wo
        x = _layernorm(h + o, ln1_g, ln1_b)
        f = jax.nn.relu(x @ W1 + b1) @ W2 + b2
        return _layernorm(x + f, ln2_g, ln2_b)
    edge_index = jnp.stack([src, dst])
    x = _layernorm(x + _L0_gnn_ref(x, edge_index, L0_gnn_W_l, L0_gnn_W_r, L0_gnn_b, L0_gnn_ln_g, L0_gnn_ln_b), axis=-1)
    x = _layernorm(x + _L1_gnn_ref(x, src, dst, L1_gnn_Wq, L1_gnn_Wk, L1_gnn_Wv, L1_gnn_Wo, L1_gnn_ln1_g, L1_gnn_ln1_b, L1_gnn_ln2_g, L1_gnn_ln2_b, L1_gnn_W1, L1_gnn_b1, L1_gnn_W2, L1_gnn_b2), axis=-1)
    return x

_drawn_inputs = setup_inputs


def setup_inputs(seed=0):
    import zlib

    import numpy as np

    out = dict(_drawn_inputs(seed))
    spreads = {'L0_gnn_ln_g': (1.0, 0.2),
     'L0_gnn_ln_b': (0.0, 0.1),
     'L1_gnn_ln1_g': (1.0, 0.2),
     'L1_gnn_ln1_b': (0.0, 0.1),
     'L1_gnn_ln2_g': (1.0, 0.2),
     'L1_gnn_ln2_b': (0.0, 0.1),
     'L1_gnn_b1': (0.0, 0.8),
     'L1_gnn_b2': (0.0, 0.1)}
    factors = {'L0_gnn_b': 8.0, 'L1_gnn_Wq': 8.0, 'L1_gnn_Wk': 8.0}
    for name, (base, spread) in spreads.items():
        noise = np.random.default_rng([zlib.crc32(name.encode()), seed]).standard_normal(out[name].shape)
        drawn = base * np.exp(spread * noise) if base else spread * noise
        out[name] = jnp.asarray(drawn.astype(out[name].dtype))
    for name, factor in factors.items():
        out[name] = (out[name] * factor).astype(out[name].dtype)
    return out
```

```python
import numpy as np
import concourse.bass as bass
from concourse import mybir
from contextlib import ExitStack

F32 = mybir.dt.float32
F32R = mybir.dt.float32r
I32 = mybir.dt.int32
ALU = mybir.AluOpType
ACT = mybir.ActivationFunctionType
AX = mybir.AxisListType

P = 128
D = 512
KC = D // P
NODES, EDGES = 10000, 15000
LAYERS, HEADS, DFF = 3, 8, 64
DK = D // HEADS
TS, CS = 8, 4
TILES = -(-NODES // (P * TS)) * TS
CHUNKS = -(-EDGES // (P * CS)) * CS
NP, EP = TILES * P, CHUNKS * P
TT, CT = TILES // TS, CHUNKS // CS
AW = D + HEADS
SKIP = 1 << 15
EPS = 1e-5
FAR = 1.0e38


def in_turns(eng, turns, slots, stages):
    most = max(lag for _, lag in stages)

    def turn(i, guard):
        for s in range(slots):
            for stage, lag in stages:
                at = (s - lag) // slots
                if guard and not 0 <= i + at < turns:
                    continue
                stage(i + at if guard or at else i, (s - lag) % slots)

    first = 1 + -(-most // slots)
    for i in range(first):
        turn(i, True)
    with eng.Fori(first, turns) as i:
        turn(i, False)
    for i in range(turns, turns + -(-most // slots)):
        turn(i, True)


def wait(eng, semaphore, count):
    if not isinstance(count, int) or count > 0:
        eng.wait_ge(semaphore, count)


def build(nc, t, out):
    ctx = ExitStack()
    with ctx:
        def sem(name):
            return ctx.enter_context(nc.semaphore(name))

        def ring(name, n):
            return [sem(f"{name}{i}") for i in range(n)]

        def dram(name, shape, dt=F32):
            return nc.dram_tensor(name, shape, dt, kind="Internal").ap()

        xs = dram("xs", [NP, D])
        agg = dram("agg", [NP, AW])
        lrows = dram("lrows", [CHUNKS, AW])
        hs = dram("hs", [NP, D])
        qs = dram("qs", [NP, D])
        ks = dram("ks", [NP, D])
        vs = dram("vs", [NP, D])
        ends_m = dram("ends_m", [CHUNKS, 2 * HEADS])

        top = [nc.sbuf_base]

        def sb(name, shape, dt=F32):
            size = int(np.prod(shape[1:])) * mybir.dt.size(dt)
            top[0] = -(-top[0] // 32) * 32
            tensor = nc.alloc_sbuf_tensor_at(name, shape, dt, offset=top[0])
            top[0] += size
            return tensor

        ident = sb("ident", [P, P])
        dst_bc = sb("dst_bc", [P, EP], I32)
        src_i = sb("src_i", [P, CHUNKS], I32)
        dst_i = sb("dst_i", [P, CHUNKS], I32)
        dst_f = sb("dst_f", [P, CHUNKS])
        nxt_i = sb("nxt_i", [P, CHUNKS], I32)
        same = sb("same", [P, CHUNKS])
        put_i = sb("put_i", [P, CHUNKS], I32)
        get_now = sb("get_now", [P, CS], I32)
        get_now2 = sb("get_now2", [P, CS], I32)
        put_now = sb("put_now", [P, CS], I32)
        ends_i = sb("ends_i", [CHUNKS, 4], I32)
        ends_f = sb("ends_f", [CHUNKS, 4])
        first_bc = sb("first_bc", [CHUNKS, CHUNKS], I32)
        last_bc = sb("last_bc", [CHUNKS, CHUNKS], I32)
        carry_m = sb("carry_m", [CHUNKS, CHUNKS])
        back_m = sb("back_m", [CHUNKS, CHUNKS])
        fixt = sb("fixt", [CHUNKS, 2])
        fix_i = sb("fix_i", [CHUNKS, 1], I32)
        ones_x = sb("ones_x", [P, HEADS], F32R)
        onesf = sb("onesf", [P, P])
        drow = sb("drow", [CHUNKS, P], I32)
        e_all = sb("e_all", [P, CHUNKS, HEADS])
        shared = top[0]

        G = sb("G", [P, CS, D])
        Ghi = sb("Ghi", [P, CS, D], F32R)
        Glo = sb("Glo", [P, CS, D], F32R)
        E = sb("E", [P, CS, P], F32R)
        O = sb("O", [P, CS, AW])
        lr = sb("lr", [CHUNKS, AW])
        fx = sb("fx", [CHUNKS, AW])
        fy = sb("fy", [CHUNKS, AW])
        edges_end = top[0]
        weights = shared + 62 * 1024

        top[0] = shared
        xin = sb("xin", [P, TS, D])
        ain = sb("ain", [P, 4, AW])
        inv = sb("inv", [P, 4, 2])
        an = sb("an", [P, 2, D])
        xhi = sb("xhi", [P, 2, D], F32R)
        xlo = sb("xlo", [P, 2, D], F32R)
        ahi = sb("ahi", [P, 2, D], F32R)
        alo = sb("alo", [P, 2, D], F32R)
        h = sb("h", [P, 2, D])
        st = sb("st", [P, 2, 6])
        mv = sb("mv", [P, 2, 2])
        sd = sb("sd", [P, 2, 3])
        hn = sb("hn", [P, 2, D])
        y = sb("y", [P, 4, D])
        assert top[0] <= weights, top
        top[0] = weights
        wraw = sb("wraw", [P, 2, KC, D])
        whi = sb("whi", [P, 2, KC, D], F32R)
        wlo = sb("wlo", [P, 2, KC, D], F32R)
        rows_bc = sb("rows_bc", [P, 5, D])
        rows_end = top[0]

        top[0] = shared
        a_x3 = sb("a_x3", [P, 4, D])
        a_x0 = sb("a_x0", [P, 4, D])
        a_sum = sb("a_sum", [P, 4, D])
        a_h = sb("a_h", [P, 4, D])
        a_hi = sb("a_hi", [P, 2, D], F32R)
        a_lo = sb("a_lo", [P, 2, D], F32R)
        a_q = sb("a_q", [P, 4, D])
        a_k = sb("a_k", [P, 4, D])
        a_st = sb("a_st", [P, 2, 6])
        a_mv = sb("a_mv", [P, 2, 2])
        a_sd = sb("a_sd", [P, 2, 3])
        assert top[0] <= weights

        top[0] = shared
        b_k = sb("b_k", [P, CS, D])
        b_q = sb("b_q", [P, CS, D])
        b_kq = sb("b_kq", [P, 2, D])
        v_h = sb("v_h", [P, TS, D])
        v_t = sb("v_t", [P, 2, D])
        v_o = sb("v_o", [P, 4, D])
        values_end = top[0]
        wv = wraw[:, 0]
        top[0] = weights + 4 * KC * D * 2
        m_e = sb("m_e", [CHUNKS, HEADS, P])
        m_f = sb("m_f", [CHUNKS, HEADS, P])
        m_new = sb("m_new", [CHUNKS, HEADS, P])
        m_end = sb("m_end", [CHUNKS, HEADS, P])
        m_t = sb("m_t", [CHUNKS, HEADS, P])
        m_row = sb("m_row", [CHUNKS, 3, P])
        m_first = sb("m_first", [CHUNKS, P])
        m_last = sb("m_last", [CHUNKS, P])
        m_prev = sb("m_prev", [CHUNKS, CHUNKS])
        m_next = sb("m_next", [CHUNKS, CHUNKS])
        m_ends = sb("m_ends", [CHUNKS, CHUNKS, 2, HEADS])
        m_ce = sb("m_ce", [CHUNKS, 2, HEADS])
        m_c = sb("m_c", [CHUNKS, 2, HEADS])
        assert top[0] <= weights + 24 * KC * D
        top[0] = weights + 8 * KC * D
        Gx = sb("Gx", [P, CS, D])
        top[0] = max(edges_end, values_end)
        ex = sb("ex", [P, CHUNKS, HEADS])
        ex_hi = sb("ex_hi", [P, CHUNKS, HEADS], F32R)
        ex_lo = sb("ex_lo", [P, CHUNKS, HEADS], F32R)
        assert top[0] <= weights
        assert top[0] <= nc.sbuf_usable_end, (top, nc.sbuf_usable_end)

        top[0] = shared
        d_a = sb("d_a", [P, 4, AW])
        d_z = sb("d_z", [P, 4, 2, HEADS])
        d_h = sb("d_h", [P, TS, D])
        d_n = sb("d_n", [P, 2, D])
        d_hi = sb("d_hi", [P, 2, D], F32R)
        d_lo = sb("d_lo", [P, 2, D], F32R)
        d_s1 = sb("d_s1", [P, 2, D])
        d_y = sb("d_y", [P, TS, D])
        d_yt = sb("d_yt", [P, 2, D])
        d_f = sb("d_f", [DFF, 2, P])
        d_st = sb("d_st", [P, 6, 6])
        d_mv = sb("d_mv", [P, 6, 2])
        d_sd = sb("d_sd", [P, 6, 3])
        d_end = top[0]
        top[0] = weights + 4 * KC * D
        d_s2 = sb("d_s2", [P, 2, D])
        d_n2 = sb("d_n2", [P, 2, D])
        assert top[0] <= weights + 8 * KC * D
        top[0] = weights + 12 * KC * D
        d_s3 = sb("d_s3", [P, 2, D])
        w1 = sb("w1", [P, KC, DFF])
        w2 = sb("w2", [DFF, D])
        b1c = sb("b1c", [DFF, 1])
        assert top[0] <= weights + 16 * KC * D
        top[0] = weights + 20 * KC * D
        d_o = sb("d_o", [P, 4, D])
        assert top[0] <= weights + 24 * KC * D
        assert d_end <= weights, (d_end, weights)
        top[0] = rows_end
        d_h2 = sb("d_h2", [P, 4, D])
        assert top[0] <= nc.sbuf_usable_end

        bank = [ctx.enter_context(nc.psum_tensor(f"bank{i}", [P, 512], F32)) for i in range(8)]

        idx_in, tables, zero_set, zeroed, prep = map(sem, ("idx_in", "tables", "zero_set", "zeroed", "prep"))
        pool_go, dve_go = sem("pool_go"), sem("dve_go")
        w_in, w_hi, w_lo = map(sem, ("w_in", "w_hi", "w_lo"))
        r_in = sem("r_in")
        gathered, scattered, lrow_out = ring("gathered", CS), ring("scattered", CS), ring("lrow_out", CS)
        get_set, put_set, hi_done, lo_done, eq_done, summed, out_main, out_extra = map(
            sem, ("get_set", "put_set", "hi_done", "lo_done", "eq_done", "summed", "out_main", "out_extra"))
        lr_in, carried, fix_in, fixed, fix_out = map(sem, ("lr_in", "carried", "fix_in", "fixed", "fix_out"))
        ring8, ring4, store4 = ring("ring8", 8), ring("ring4", 4), ring("store4", 4)
        inv_max, inv_done, an_done, tposed, nhi, nlo, mm_done, h_done = map(
            sem, ("inv_max", "inv_done", "an_done", "tposed", "nhi", "nlo", "mm_done", "h_done"))
        bn, ag, var_d, sd_done, rc, rs_done, nrm, g_mul, g_add, y_done = map(
            sem, ("bn", "ag", "var_d", "sd_done", "rc", "rs_done", "nrm", "g_mul", "g_add", "y_done"))
        h_out, qk_out = ring("h_out", 4), ring("qk_out", 4)
        a_add, q_ev, k_ev = map(sem, ("a_add", "q_ev", "k_ev"))
        kq_in = ring("kq_in", CS)
        v_tp, v_ev, v_mm, v_out, b_mul, b_red = map(sem, ("v_tp", "v_ev", "v_mm", "v_out", "b_mul", "b_red"))
        m_step, m_pe, m_act, ends_out, ends_in = map(sem, ("m_step", "m_pe", "m_act", "ends_out", "ends_in"))
        gx_done, ex_split = sem("gx_done"), sem("ex_split")
        h2_in = ring("h2_in", 4)
        f_tp, f_t, f_1, f_r, f_2 = map(sem, ("f_tp", "f_t", "f_1", "f_r", "f_2"))
        s2_done, s3_done, o_done, nrm2, g_mul2, g_add2 = map(
            sem, ("s2_done", "s3_done", "o_done", "nrm2", "g_mul2", "g_add2"))
        ln2 = [sem(f"ln2_{n}") for n in ("bn", "ag", "var", "sd", "rc", "rs")]
        ln3 = [sem(f"ln3_{n}") for n in ("bn", "ag", "var", "sd", "rc", "rs")]
        ln1 = [bn, ag, var_d, sd_done, rc, rs_done]

        A0, D0 = LAYERS * TILES, (LAYERS + 1) * TILES
        R8_V, R8_D = LAYERS * TT, (LAYERS + 1) * TT
        R4_A = LAYERS * 2 * TT * 16
        R4_D = R4_A + 2 * TT * 32
        ST_V, ST_D = LAYERS * 2 * TT, (LAYERS + 1) * 2 * TT

        def rows(i, s):
            return bass.ds((i * TS + s) * P, P)

        block = ctx.enter_context(nc.Block())

        @block.sync
        def _(eng):
            for tile, name in ((src_i, "src_cols"), (dst_i, "dst_cols"), (nxt_i, "next_cols"), (ends_i, "ends"),
                               (drow, "dst_rows")):
                eng.dma_start(tile[:, :], t[name]).then_inc(idx_in, 16)
            eng.dma_start(first_bc[:, :], t["first_row"].broadcast_to([CHUNKS, CHUNKS])).then_inc(idx_in, 16)
            eng.dma_start(last_bc[:, :], t["last_row"].broadcast_to([CHUNKS, CHUNKS])).then_inc(idx_in, 16)
            eng.dma_start(dst_bc[:, :], t["dst_row"].broadcast_to([P, EP])).then_inc(idx_in, 16)
            eng.wait_ge(zero_set, 1)
            agg_flat = agg.rearrange("(p r) w -> p (r w)", p=P)
            for r in range(TILES // CS):
                eng.dma_start(agg_flat[:, r * CS * AW:(r + 1) * CS * AW],
                              O[:, :, :].rearrange("p s w -> p (s w)")).then_inc(zeroed, 16)

            def carries(a):
                def save_last_row(i, s):
                    g = (a * CT + i) * CS + s
                    eng.wait_ge(out_main, g + 1)
                    eng.wait_ge(out_extra, g + 1)
                    eng.dma_start(lrows[bass.ds(i * CS + s, 1), :], O[P - 1:P, s, :]).then_inc(lrow_out[s], 16)

                in_turns(eng, CT, CS, [(save_last_row, 0)])
                for s in range(CS):
                    eng.wait_ge(lrow_out[s], 16 * CT * (a + 1))
                eng.dma_start(lr[:, :], lrows).then_inc(lr_in, 16)
                eng.wait_ge(fix_out, 16 * (a + 1))

            for l in range(LAYERS):
                wait(eng, mm_done, l * TILES)
                for k, name in enumerate(("L0_WlT", "L0_WrT")):
                    eng.dma_start(wraw[:, k], t[name][l].rearrange("(k p) n -> p k n", p=P)).then_inc(w_in, 16)
                wait(eng, y_done, l * TILES)
                for k, name in enumerate(("L0_gnn_b", "L0_gnn_ln_g", "L0_gnn_ln_b")):
                    eng.dma_start(rows_bc[:, k], t[name][l:l + 1, :].broadcast_to([P, D])).then_inc(r_in, 16)
                carries(l)

                def load(i, s):
                    g = (l * TT + i) * TS + s
                    wait(eng, y_done, g - 7)
                    eng.dma_start(xin[:, s, :], (t["x"] if l == 0 else xs)[rows(i, s), :]).then_inc(ring8[s], 16)
                    wait(eng, an_done, g - 3)
                    eng.dma_start(ain[:, s % 4, :], agg[rows(i, s), :]).then_inc(ring4[s % 4], 16)

                def store(i, s):
                    g = (l * TT + i) * TS + s
                    eng.wait_ge(y_done, g + 1)
                    eng.dma_start(xs[rows(i, s), :], y[:, s % 4, :]).then_inc(store4[s % 4], 16)

                in_turns(eng, TT, TS, [(load, 0), (store, 8)])
                for s in range(4):
                    eng.wait_ge(store4[s], 16 * 2 * TT * (l + 1))

            eng.wait_ge(mm_done, A0)
            for k, name in enumerate(("L1_gnn_Wq", "L1_gnn_Wk")):
                eng.dma_start(wraw[:, k], t[name].rearrange("(k p) n -> p k n", p=P)).then_inc(w_in, 16)

            def a_load(i, s):
                g = i * TS + s
                wait(eng, a_add, g - 3)
                eng.dma_start(a_x3[:, s % 4, :], xs[rows(i, s), :]).then_inc(ring4[s % 4], 16)
                eng.dma_start(a_x0[:, s % 4, :], t["x"][rows(i, s), :]).then_inc(ring4[s % 4], 16)

            def a_store_h(i, s):
                eng.wait_ge(nrm, A0 + i * TS + s + 1)
                eng.dma_start(hs[rows(i, s), :], a_h[:, s % 4, :]).then_inc(h_out[s % 4], 16)

            def a_store_qk(i, s):
                g = i * TS + s
                eng.wait_ge(q_ev, g + 1)
                eng.dma_start(qs[rows(i, s), :], a_q[:, s % 4, :]).then_inc(qk_out[s % 4], 16)
                eng.wait_ge(k_ev, g + 1)
                eng.dma_start(ks[rows(i, s), :], a_k[:, s % 4, :]).then_inc(qk_out[s % 4], 16)

            in_turns(eng, TT, TS, [(a_load, 0), (a_store_h, 6), (a_store_qk, 9)])
            for s in range(4):
                eng.wait_ge(qk_out[s], 32 * 2 * TT)
                eng.wait_ge(h_out[s], 16 * 2 * TT)

            eng.dma_start(wv, t["L1_gnn_Wv"].rearrange("(k p) n -> p k n", p=P)).then_inc(w_in, 16)

            def v_load(i, s):
                wait(eng, v_tp, i * TS + s - 7)
                eng.dma_start(v_h[:, s, :], hs[rows(i, s), :]).then_inc(ring8[s], 16)

            def v_store(i, s):
                eng.wait_ge(v_out, i * TS + s + 1)
                eng.dma_start(vs[rows(i, s), :], v_o[:, s % 4, :]).then_inc(store4[s % 4], 16)

            in_turns(eng, TT, TS, [(v_load, 0), (v_store, 10)])

            eng.wait_ge(m_step, 14)
            eng.dma_start(ends_m, m_ce[:, :, :].rearrange("p a h -> p (a h)")).then_inc(ends_out, 16)
            eng.wait_ge(ends_out, 16)
            eng.dma_start(m_ends[:, :, :, :].rearrange("p c a h -> p (c a h)"),
                          ends_m.rearrange("c w -> (c w)").unsqueeze(0).broadcast_to([CHUNKS, 2 * CHUNKS * HEADS])
                          ).then_inc(ends_in, 16)

            eng.wait_ge(v_mm, TILES)
            eng.dma_start(wraw[:, 0], t["L1_gnn_Wo"].rearrange("(k p) n -> p k n", p=P)).then_inc(w_in, 16)
            for k, name in enumerate(("L1_gnn_ln1_g", "L1_gnn_ln1_b", "L1_gnn_ln2_g", "L1_gnn_ln2_b", "L1_gnn_b2")):
                eng.dma_start(rows_bc[:, k], t[name].broadcast_to([P, D])).then_inc(r_in, 16)
            carries(3)
            eng.dma_start(w1[:, :, :], t["L1_gnn_W1"].rearrange("(k p) n -> p k n", p=P)).then_inc(r_in, 16)
            eng.dma_start(w2[:, :], t["L1_gnn_W2"]).then_inc(r_in, 16)
            eng.dma_start(b1c[:, :], t["b1_col"]).then_inc(r_in, 16)

            def d_load(i, s):
                g = i * TS + s
                wait(eng, an_done, A0 + g - 3)
                eng.dma_start(d_a[:, s % 4, :], agg[rows(i, s), :]).then_inc(ring4[s % 4], 16)
                wait(eng, h_done, A0 + g - 7)
                eng.dma_start(d_h[:, s, :], hs[rows(i, s), :]).then_inc(ring8[s], 16)

            def d_load_again(i, s):
                wait(eng, s3_done, i * TS + s - 3)
                eng.dma_start(d_h2[:, s % 4, :], hs[rows(i, s), :]).then_inc(h2_in[s % 4], 16)

            def d_store(i, s):
                eng.wait_ge(o_done, i * TS + s + 1)
                eng.dma_start(out[rows(i, s), :], d_o[:, s % 4, :]).then_inc(store4[s % 4], 16)

            in_turns(eng, TT, TS, [(d_load, 0), (d_load_again, 10), (d_store, 15)])
            for s in range(4):
                eng.wait_ge(store4[s], 16 * (ST_D + 2 * TT))

        @block.gpsimd
        def _(eng):
            last_row = eng.to_reg(NP - 1)
            eng.memset(O[:, :, :], 0.0).then_inc(zero_set, 1)
            eng.memset(ident[:, :], 0.0).then_inc(prep, 1)
            eng.wait_ge(prep, 1)
            eng.affine_select(out=ident[:, :], in_=ident[:, :], compare_op=ALU.not_equal, fill=1.0,
                              base=0, pattern=[[-1, P]], channel_multiplier=1).then_inc(prep, 1)
            eng.memset(onesf[:, :], 1.0).then_inc(prep, 1)
            eng.wait_ge(tables, 7)
            eng.affine_select(out=carry_m[:, :], in_=carry_m[:, :], compare_op=ALU.is_gt, fill=0.0,
                              base=0, pattern=[[1, CHUNKS]], channel_multiplier=-1).then_inc(prep, 1)
            eng.affine_select(out=back_m[:, :], in_=back_m[:, :], compare_op=ALU.is_gt, fill=0.0,
                              base=0, pattern=[[-1, CHUNKS]], channel_multiplier=1).then_inc(prep, 1)

            def aggregate(a, source):
                def gather(i, s):
                    g = (a * CT + i) * CS + s
                    free = gx_done if a == 3 else lo_done
                    wait(eng, free, i * CS + s - 3 if a == 3 else g - 3)
                    eng.tensor_copy(get_now[:, s:s + 1], src_i[:, bass.ds(i * CS + s, 1)]).then_inc(get_set, 1)
                    eng.wait_ge(get_set, g + 1 + (2 * CHUNKS if a == 3 else 0))
                    eng.sem_inc(pool_go, 1)
                    eng.indirect_dma_start(
                        out=G[:, s, :], out_offset=None, in_=source,
                        in_offset=bass.IndirectOffsetOnAxis(ap=get_now[:, s:s + 1], axis=0),
                    ).then_inc(gathered[s], 16)

                def scatter(i, s):
                    g = (a * CT + i) * CS + s
                    wait(eng, scattered[s], 16 * (a * CT + i))
                    eng.tensor_copy(put_now[:, s:s + 1], put_i[:, bass.ds(i * CS + s, 1)]).then_inc(put_set, 1)
                    eng.wait_ge(put_set, g + 1)
                    eng.wait_ge(out_main, g + 1)
                    eng.wait_ge(out_extra, g + 1)
                    eng.sem_inc(pool_go, 1)
                    eng.indirect_dma_start(
                        out=agg, out_offset=bass.IndirectOffsetOnAxis(ap=put_now[:, s:s + 1], axis=0),
                        in_=O[:, s, :], in_offset=None, bounds_check=last_row, oob_is_err=False,
                    ).then_inc(scattered[s], 16)

                in_turns(eng, CT, CS, [(gather, 0), (scatter, CS)])
                for s in range(CS):
                    eng.wait_ge(scattered[s], 16 * CT * (a + 1))
                eng.indirect_dma_start(
                    out=fx[:, :], out_offset=None, in_=agg,
                    in_offset=bass.IndirectOffsetOnAxis(ap=ends_i[:, 0:1], axis=0)).then_inc(fix_in, 16)
                eng.wait_ge(fixed, 2 * (a + 1))
                eng.indirect_dma_start(
                    out=agg, out_offset=bass.IndirectOffsetOnAxis(ap=fix_i[:, 0:1], axis=0),
                    in_=fy[:, :], in_offset=None, bounds_check=last_row, oob_is_err=False).then_inc(fix_out, 16)
                eng.wait_ge(fix_out, 16 * (a + 1))

            for l in range(LAYERS):
                if l == 0:
                    eng.wait_ge(zeroed, 16 * (TILES // CS))
                for s in range(4):
                    wait(eng, store4[s], 16 * 2 * TT * l)
                aggregate(l, t["x"] if l == 0 else xs)
                eng.wait_ge(r_in, 16 * 3 * (l + 1))

                def affine(i, s):
                    g = (l * TT + i) * TS + s
                    eng.wait_ge(nrm, g + 1)
                    eng.tensor_tensor(hn[:, s % 2, :], hn[:, s % 2, :], rows_bc[:, 1, :], ALU.mult).then_inc(g_mul, 1)
                    eng.wait_ge(g_mul, g + 1)
                    eng.tensor_tensor(hn[:, s % 2, :], hn[:, s % 2, :], rows_bc[:, 2, :], ALU.add).then_inc(g_add, 1)

                in_turns(eng, TT, TS, [(affine, 0)])

            for s in range(4):
                eng.wait_ge(store4[s], 16 * 2 * TT * LAYERS)

            def a_sums(i, s):
                g = i * TS + s
                eng.wait_ge(ring4[s % 4], R4_A + 32 * (2 * i + s // 4 + 1))
                wait(eng, nrm, A0 + g - 3)
                eng.tensor_tensor(a_sum[:, s % 4, :], a_x3[:, s % 4, :], a_x0[:, s % 4, :], ALU.add).then_inc(a_add, 1)

            in_turns(eng, TT, TS, [(a_sums, 0)])

            for s in range(4):
                eng.wait_ge(qk_out[s], 32 * 2 * TT)

            def gather_kq(i, s):
                g = i * CS + s
                wait(eng, b_mul, g - 3)
                eng.tensor_copy(get_now[:, s:s + 1], src_i[:, bass.ds(g, 1)]).then_inc(get_set, 1)
                eng.tensor_copy(get_now2[:, s:s + 1], dst_i[:, bass.ds(g, 1)]).then_inc(get_set, 1)
                eng.wait_ge(get_set, 3 * CHUNKS + 2 * g + 2)
                eng.sem_inc(pool_go, 1)
                for tile, row, source in ((b_k, get_now, ks), (b_q, get_now2, qs)):
                    eng.indirect_dma_start(
                        out=tile[:, s, :], out_offset=None, in_=source,
                        in_offset=bass.IndirectOffsetOnAxis(ap=row[:, s:s + 1], axis=0)).then_inc(kq_in[s], 16)

            in_turns(eng, CT, CS, [(gather_kq, 0)])
            for s in range(4):
                eng.wait_ge(store4[s], 16 * (ST_V + 2 * TT))
            eng.wait_ge(b_mul, CHUNKS)
            aggregate(3, vs)
            eng.wait_ge(r_in, 16 * (3 * LAYERS + 8))

            def attention(i, s):
                g = A0 + i * TS + s
                eng.wait_ge(inv_done, g + 1)
                wait(eng, tposed, g + TILES - 1)
                eng.tensor_tensor(d_n[:, s % 2, :].rearrange("p (h d) -> p h d", h=HEADS),
                                  d_a[:, s % 4, 0:D].rearrange("p (h d) -> p h d", h=HEADS),
                                  d_z[:, s % 4, 1, :].unsqueeze(2).broadcast_to([P, HEADS, DK]),
                                  ALU.mult).then_inc(an_done, 1)

            def affine1(i, s):
                g = i * TS + s
                eng.wait_ge(nrm, D0 + g + 1)
                eng.tensor_tensor(d_y[:, s, :], d_y[:, s, :], rows_bc[:, 0, :], ALU.mult).then_inc(g_mul, 1)
                eng.wait_ge(g_mul, A0 + g + 1)
                eng.tensor_tensor(d_y[:, s, :], d_y[:, s, :], rows_bc[:, 1, :], ALU.add).then_inc(g_add, 1)

            def affine2(i, s):
                g = i * TS + s
                eng.wait_ge(nrm2, g + 1)
                eng.tensor_tensor(d_n2[:, s % 2, :], d_n2[:, s % 2, :], rows_bc[:, 2, :], ALU.mult).then_inc(g_mul2, 1)
                eng.wait_ge(g_mul2, g + 1)
                eng.tensor_tensor(d_n2[:, s % 2, :], d_n2[:, s % 2, :], rows_bc[:, 3, :], ALU.add).then_inc(g_add2, 1)

            in_turns(eng, TT, TS, [(attention, 1), (affine1, 5), (affine2, 10)])

        @block.tensor
        def _(eng):
            eng.wait_ge(prep, 5)

            def aggregate(a):
                def segment_sums(i, s):
                    g = (a * CT + i) * CS + s
                    eng.wait_ge(eq_done, g + 1)
                    eng.wait_ge(hi_done, g + 1)
                    wait(eng, out_main, g - 3)
                    eng.matmul(bank[s][:, 0:D], E[:, s, :], Ghi[:, s, :], start=True, stop=False)
                    eng.wait_ge(lo_done, g + 1)
                    eng.matmul(bank[s][:, 0:D], E[:, s, :], Glo[:, s, :], start=False, stop=True)
                    wait(eng, out_extra, g - 3)
                    if a < 3:
                        last = eng.matmul(bank[4 + s][:, 0:HEADS], E[:, s, :], ones_x[:, :], start=True, stop=True)
                    else:
                        c = bass.ds(i * CS + s, 1)
                        eng.matmul(bank[4 + s][:, 0:HEADS], E[:, s, :], ex_hi[:, c, :].rearrange("p c h -> p (c h)"), start=True, stop=False)
                        last = eng.matmul(bank[4 + s][:, 0:HEADS], E[:, s, :], ex_lo[:, c, :].rearrange("p c h -> p (c h)"), start=False, stop=True)
                    last.then_inc(summed, 1)

                in_turns(eng, CT, CS, [(segment_sums, 0)])
                eng.wait_ge(out_main, CHUNKS * (a + 1))
                eng.wait_ge(out_extra, CHUNKS * (a + 1))
                eng.wait_ge(lr_in, 16 * (a + 1))
                eng.matmul(bank[0][0:CHUNKS, 0:D], carry_m[:, :], lr[:, 0:D], start=True, stop=True).then_inc(carried, 1)
                eng.matmul(bank[4][0:CHUNKS, 0:HEADS], carry_m[:, :], lr[:, D:AW], start=True, stop=True).then_inc(carried, 1)
                eng.wait_ge(fixed, 2 * (a + 1))

            def transpose4(into, tile):
                for k in range(KC):
                    last = eng.transpose(into[:, k * P:(k + 1) * P], tile[:, k * P:(k + 1) * P], ident[:, :])
                return last

            def product3(into, terms):
                step, steps = 0, len(terms) * KC * 3
                for hi, lo, w in terms:
                    for k in range(KC):
                        b = slice(k * P, (k + 1) * P)
                        for left, right in ((hi, whi), (hi, wlo), (lo, whi)):
                            last = eng.matmul(into, left[:, b], right[:, w, k, :], start=step == 0, stop=step == steps - 1)
                            step += 1
                return last

            for l in range(LAYERS):
                aggregate(l)
                eng.wait_ge(w_hi, 2 * (l + 1))
                eng.wait_ge(w_lo, 2 * (l + 1))

                def transposes(i, s):
                    g = (l * TT + i) * TS + s
                    o = s % 2
                    wait(eng, nlo, g - 1)
                    eng.wait_ge(ring8[s], 16 * (l * TT + i + 1))
                    transpose4(bank[o], xin[:, s, :])
                    eng.wait_ge(an_done, g + 1)
                    transpose4(bank[2 + o], an[:, o, :]).then_inc(tposed, 1)

                def products(i, s):
                    g = (l * TT + i) * TS + s
                    o = s % 2
                    wait(eng, h_done, g - 1)
                    eng.wait_ge(nlo, g + 1)
                    product3(bank[4 + o][:, :], [(ahi[:, o, :], alo[:, o, :], 0),
                                                 (xhi[:, o, :], xlo[:, o, :], 1)]).then_inc(mm_done, 1)

                in_turns(eng, TT, TS, [(transposes, 2), (products, 3)])

            eng.wait_ge(w_hi, 2 * LAYERS + 2)
            eng.wait_ge(w_lo, 2 * LAYERS + 2)

            def a_transposes(i, s):
                g = A0 + i * TS + s
                wait(eng, nlo, g - 1)
                eng.wait_ge(nrm, g + 1)
                transpose4(bank[s % 2], a_h[:, s % 4, :]).then_inc(tposed, 1)

            def a_products(i, s):
                g = i * TS + s
                o = s % 2
                eng.wait_ge(nlo, A0 + g + 1)
                wait(eng, q_ev, g - 1)
                product3(bank[2 + o][:, :], [(a_hi[:, o, :], a_lo[:, o, :], 0)])
                wait(eng, k_ev, g - 1)
                product3(bank[4 + o][:, :], [(a_hi[:, o, :], a_lo[:, o, :], 1)]).then_inc(mm_done, 1)

            in_turns(eng, TT, TS, [(a_transposes, 3), (a_products, 4)])

            eng.wait_ge(w_in, 16 * (2 * LAYERS + 3))
            eng.wait_ge(k_ev, TILES)
            eng.wait_ge(q_ev, TILES)

            def v_transposes(i, s):
                g = i * TS + s
                wait(eng, v_ev, g - 1)
                eng.wait_ge(ring8[s], 16 * (R8_V + i + 1))
                transpose4(bank[s % 2], v_h[:, s, :]).then_inc(v_tp, 1)

            def v_products(i, s):
                g = i * TS + s
                wait(eng, v_out, g - 1)
                eng.wait_ge(v_ev, g + 1)
                for k in range(KC):
                    last = eng.matmul(bank[2 + s % 2][:, :], v_t[:, s % 2, k * P:(k + 1) * P], wv[:, k, :],
                                      start=k == 0, stop=k == KC - 1)
                last.then_inc(v_mm, 1)

            in_turns(eng, TT, TS, [(v_transposes, 0), (v_products, 1)])

            eng.wait_ge(b_red, CHUNKS)
            for n in range(HEADS):
                eng.transpose(bank[4 + n // 4][0:CHUNKS, (n % 4) * P:(n % 4 + 1) * P], e_all[:, :, n],
                              ident[:, :]).then_inc(m_pe, 1)
            eng.wait_ge(m_step, 22)
            for n in range(HEADS):
                eng.transpose(bank[6 + n // 4][:, (n % 4) * CHUNKS:(n % 4 + 1) * CHUNKS], m_e[:, n, :],
                              ident[0:CHUNKS, 0:CHUNKS]).then_inc(m_pe, 1)
            eng.wait_ge(m_step, 24)
            eng.wait_ge(ex_split, 1)

            aggregate(3)

            eng.wait_ge(w_hi, 2 * LAYERS + 3)
            eng.wait_ge(w_lo, 2 * LAYERS + 3)
            eng.wait_ge(r_in, 16 * (3 * LAYERS + 8))

            def d_transposes(i, s):
                g = i * TS + s
                wait(eng, nlo, D0 + g - 1)
                eng.wait_ge(an_done, A0 + g + 1)
                transpose4(bank[s % 2], d_n[:, s % 2, :]).then_inc(tposed, 1)

            def d_products(i, s):
                g = i * TS + s
                o = s % 2
                wait(eng, h_done, A0 + g - 1)
                eng.wait_ge(nlo, D0 + g + 1)
                product3(bank[2 + o][:, :], [(d_hi[:, o, :], d_lo[:, o, :], 0)]).then_inc(mm_done, 1)

            def f_transposes(i, s):
                g = i * TS + s
                wait(eng, f_t, g)
                eng.wait_ge(g_add, A0 + g + 1)
                transpose4(bank[4], d_y[:, s, :]).then_inc(f_tp, 1)

            def f_first(i, s):
                g = i * TS + s
                wait(eng, f_r, g)
                eng.wait_ge(f_t, g + 1)
                for k in range(KC):
                    last = eng.matmul(bank[5][0:DFF, 0:P], w1[:, k, :], d_yt[:, s % 2, k * P:(k + 1) * P],
                                      start=k == 0, stop=k == KC - 1)
                last.then_inc(f_1, 1)

            def f_second(i, s):
                g = i * TS + s
                wait(eng, s2_done, g - 1)
                eng.matmul(bank[6 + s % 2][:, :], onesf[0:1, :], rows_bc[0:1, 4, :], start=True, stop=False)
                eng.wait_ge(f_r, g + 1)
                eng.matmul(bank[6 + s % 2][:, :], d_f[:, s % 2, :], w2[:, :], start=False, stop=True).then_inc(f_2, 1)

            in_turns(eng, TT, TS, [(d_transposes, 2), (f_transposes, 6), (f_first, 7), (f_second, 8), (d_products, 3)])

        @block.scalar
        def _(eng):
            def aggregate(a):
                def split_hi(i, s):
                    g = (a * CT + i) * CS + s
                    if a == 3:
                        eng.wait_ge(gx_done, i * CS + s + 1)
                    else:
                        eng.wait_ge(gathered[s], 16 * (a * CT + i + 1))
                    wait(eng, summed, g - 3)
                    eng.activation(Ghi[:, s, :], (Gx if a == 3 else G)[:, s, :], ACT.Copy).then_inc(hi_done, 1)

                def take_sums(i, s):
                    g = (a * CT + i) * CS + s
                    eng.wait_ge(summed, g + 1)
                    wait(eng, scattered[s], 16 * (a * CT + i))
                    wait(eng, lrow_out[s], 16 * (a * CT + i))
                    eng.activation(O[:, s, 0:D], bank[s][:, 0:D], ACT.Copy).then_inc(out_main, 1)

                in_turns(eng, CT, CS, [(split_hi, 0), (take_sums, 2)])

            def deviation(i, s, sems, base, sd_t, mv_t, n):
                eng.wait_ge(sems[2], base + i * TS + s + 1)
                eng.activation(sd_t[:, n, 0:1], mv_t[:, n, 1:2], ACT.Sqrt).then_inc(sems[3], 1)

            for l in range(LAYERS):
                eng.wait_ge(w_in, 32 * (l + 1))
                for w in range(2):
                    eng.activation(whi[:, w], wraw[:, w], ACT.Copy).then_inc(w_hi, 1)
                aggregate(l)

                def mean(i, s):
                    g = (l * TT + i) * TS + s
                    eng.wait_ge(inv_done, g + 1)
                    wait(eng, tposed, g - 1)
                    eng.activation(an[:, s % 2, :], ain[:, s % 4, 0:D], ACT.Copy, scale=inv[:, s % 4, 1:2]).then_inc(an_done, 1)

                def split_nodes(i, s):
                    g = (l * TT + i) * TS + s
                    o = s % 2
                    eng.wait_ge(tposed, g + 1)
                    wait(eng, mm_done, g - 1)
                    eng.activation(xhi[:, o, :], bank[o][:, :], ACT.Copy)
                    eng.activation(ahi[:, o, :], bank[2 + o][:, :], ACT.Copy).then_inc(nhi, 1)

                def normalise(i, s):
                    g = (l * TT + i) * TS + s
                    o = s % 2
                    eng.wait_ge(rs_done, g + 1)
                    wait(eng, y_done, g - 1)
                    eng.activation(hn[:, o, :], h[:, o, :], ACT.Identity, bias=sd[:, o, 2:3],
                                   scale=sd[:, o, 1:2]).then_inc(nrm, 1)

                in_turns(eng, TT, TS, [(normalise, 5), (mean, 1), (split_nodes, 2),
                                       (lambda i, s: deviation(i, s, ln1, l * TILES, sd, mv, s % 2), 4)])

            eng.wait_ge(w_in, 16 * (2 * LAYERS + 2))
            for w in range(2):
                eng.activation(whi[:, w], wraw[:, w], ACT.Copy).then_inc(w_hi, 1)

            def a_normalise(i, s):
                g = i * TS + s
                eng.wait_ge(rs_done, A0 + g + 1)
                wait(eng, tposed, A0 + g - 3)
                wait(eng, h_out[s % 4], 16 * (2 * i + s // 4))
                eng.activation(a_h[:, s % 4, :], a_sum[:, s % 4, :], ACT.Identity, bias=a_sd[:, s % 2, 2:3],
                               scale=a_sd[:, s % 2, 1:2]).then_inc(nrm, 1)

            def a_split(i, s):
                g = A0 + i * TS + s
                eng.wait_ge(tposed, g + 1)
                wait(eng, mm_done, g - 1)
                eng.activation(a_hi[:, s % 2, :], bank[s % 2][:, :], ACT.Copy).then_inc(nhi, 1)

            def take_q(i, s):
                g = i * TS + s
                eng.wait_ge(mm_done, A0 + g + 1)
                wait(eng, qk_out[s % 4], 32 * (2 * i + s // 4))
                eng.activation(a_q[:, s % 4, :], bank[2 + s % 2][:, :], ACT.Copy).then_inc(q_ev, 1)

            in_turns(eng, TT, TS, [(a_normalise, 2), (a_split, 3), (take_q, 5),
                                   (lambda i, s: deviation(i, s, ln1, A0, a_sd, a_mv, s % 2), 1)])

            def v_take(i, s):
                g = i * TS + s
                eng.wait_ge(v_tp, g + 1)
                wait(eng, v_mm, g - 1)
                eng.activation(v_t[:, s % 2, :], bank[s % 2][:, :], ACT.Copy).then_inc(v_ev, 1)

            def v_finish(i, s):
                eng.wait_ge(v_mm, i * TS + s + 1)
                wait(eng, store4[s % 4], 16 * (ST_V + 2 * i + s // 4))
                eng.activation(v_o[:, s % 4, :], bank[2 + s % 2][:, :], ACT.Copy).then_inc(v_out, 1)

            in_turns(eng, TT, TS, [(v_take, 0), (v_finish, 2)])

            eng.wait_ge(m_step, 24)
            eng.activation(ex[:, :, :], e_all[:, :, :], ACT.Exp, scale=1.0 / DK ** 0.5).then_inc(m_act, 1)
            eng.wait_ge(m_act, 1)
            eng.activation(ex_hi[:, :, :], ex[:, :, :], ACT.Copy).then_inc(m_act, 1)
            aggregate(3)
            eng.wait_ge(w_in, 16 * (2 * LAYERS + 4))
            eng.wait_ge(fix_out, 16 * 4)
            eng.activation(whi[:, 0], wraw[:, 0], ACT.Copy).then_inc(w_hi, 1)

            def d_split(i, s):
                g = D0 + i * TS + s
                eng.wait_ge(tposed, g + 1)
                wait(eng, mm_done, g - 1)
                eng.activation(d_hi[:, s % 2, :], bank[s % 2][:, :], ACT.Copy).then_inc(nhi, 1)

            def d_norm1(i, s):
                g = i * TS + s
                eng.wait_ge(rs_done, D0 + g + 1)
                wait(eng, s2_done, g - 7)
                eng.activation(d_y[:, s, :], d_s1[:, s % 2, :], ACT.Identity, bias=d_sd[:, s % 2, 2:3],
                               scale=d_sd[:, s % 2, 1:2]).then_inc(nrm, 1)

            def f_take(i, s):
                g = i * TS + s
                eng.wait_ge(f_tp, g + 1)
                wait(eng, f_1, g - 1)
                eng.activation(d_yt[:, s % 2, :], bank[4][:, :], ACT.Copy).then_inc(f_t, 1)

            def f_relu(i, s):
                g = i * TS + s
                eng.wait_ge(f_1, g + 1)
                wait(eng, f_2, g - 1)
                eng.activation(d_f[:, s % 2, :], bank[5][0:DFF, 0:P], ACT.Relu, bias=b1c[:, 0:1]).then_inc(f_r, 1)

            def d_norm2(i, s):
                g = i * TS + s
                eng.wait_ge(ln2[5], g + 1)
                wait(eng, s3_done, g - 1)
                eng.activation(d_n2[:, s % 2, :], d_s2[:, s % 2, :], ACT.Identity, bias=d_sd[:, 2 + s % 2, 2:3],
                               scale=d_sd[:, 2 + s % 2, 1:2]).then_inc(nrm2, 1)

            def d_norm3(i, s):
                g = i * TS + s
                eng.wait_ge(ln3[5], g + 1)
                wait(eng, store4[s % 4], 16 * (ST_D + 2 * i + s // 4))
                eng.activation(d_o[:, s % 4, :], d_s3[:, s % 2, :], ACT.Identity, bias=d_sd[:, 4 + s % 2, 2:3],
                               scale=d_sd[:, 4 + s % 2, 1:2]).then_inc(o_done, 1)

            in_turns(eng, TT, TS, [
                (d_norm1, 5), (d_norm2, 10), (d_norm3, 12), (d_split, 2), (f_take, 6), (f_relu, 7),
                (lambda i, s: deviation(i, s, ln1, D0, d_sd, d_mv, s % 2), 4),
                (lambda i, s: deviation(i, s, ln2, 0, d_sd, d_mv, 2 + s % 2), 9),
                (lambda i, s: deviation(i, s, ln3, 0, d_sd, d_mv, 4 + s % 2), 11)])

        @block.vector
        def _(eng):
            eng.wait_ge(idx_in, 16 * 8)
            eng.tensor_copy(dst_f[:, :], dst_i[:, :]).then_inc(tables, 1)
            eng.tensor_tensor(same[:, :], dst_i[:, :], nxt_i[:, :], ALU.is_equal).then_inc(tables, 1)
            eng.tensor_copy(ends_f[:, :], ends_i[:, :]).then_inc(tables, 1)
            eng.wait_ge(tables, 3)
            eng.scalar_tensor_tensor(out=put_i[:, :], in0=same[:, :], scalar=float(SKIP), in1=dst_f[:, :],
                                     op0=ALU.mult, op1=ALU.add).then_inc(tables, 1)
            eng.tensor_tensor(fixt[:, 0:1], ends_f[:, 0:1], ends_f[:, 2:3], ALU.is_equal).then_inc(m_step, 1)
            eng.tensor_tensor(fixt[:, 1:2], ends_f[:, 0:1], ends_f[:, 3:4], ALU.is_equal).then_inc(m_step, 1)
            eng.wait_ge(m_step, 2)
            eng.scalar_tensor_tensor(out=fixt[:, 1:2], in0=fixt[:, 1:2], scalar=-1.0, in1=fixt[:, 0:1],
                                     op0=ALU.add, op1=ALU.mult).then_inc(m_step, 1)
            eng.wait_ge(m_step, 3)
            eng.tensor_scalar(fixt[:, 0:1], fixt[:, 1:2], float(SKIP), float(SKIP), ALU.mult, ALU.add).then_inc(m_step, 1)
            eng.wait_ge(m_step, 4)
            eng.tensor_tensor(fix_i[:, :], fixt[:, 0:1], ends_f[:, 0:1], ALU.add).then_inc(tables, 1)
            eng.tensor_scalar(carry_m[:, :], first_bc[:, :], ends_f[:, 1:2], None, ALU.is_equal).then_inc(tables, 1)
            eng.tensor_scalar(back_m[:, :], last_bc[:, :], ends_f[:, 0:1], None, ALU.is_equal).then_inc(tables, 1)
            eng.wait_ge(prep, 3)
            eng.tensor_copy(ones_x[:, :], onesf[:, 0:HEADS]).then_inc(m_step, 1)

            def weights_lo(n, count):
                for w in range(count):
                    eng.wait_ge(w_hi, n + w + 1)
                    eng.tensor_tensor(wlo[:, w], wraw[:, w], whi[:, w].bitcast(F32), ALU.subtract).then_inc(w_lo, 1)

            def aggregate(a):
                def equal_edges(i, s):
                    g = (a * CT + i) * CS + s
                    c = i * CS + s
                    wait(eng, summed, g - 3)
                    eng.tensor_scalar(E[:, s, :], dst_bc[:, bass.ds(c * P, P)], dst_f[:, bass.ds(c, 1)], None,
                                      ALU.is_equal).then_inc(eq_done, 1)

                def weigh(i, s):
                    c = i * CS + s
                    eng.wait_ge(gathered[s], 16 * (a * CT + i + 1))
                    wait(eng, lo_done, a * CHUNKS + c - 3)
                    eng.tensor_tensor(Gx[:, s, :].rearrange("p (h d) -> p h d", h=HEADS),
                                      G[:, s, :].rearrange("p (h d) -> p h d", h=HEADS),
                                      ex[:, bass.ds(c, 1), :].rearrange("p c h -> p (c h)").unsqueeze(2).broadcast_to([P, HEADS, DK]),
                                      ALU.mult).then_inc(gx_done, 1)

                def split_lo(i, s):
                    g = (a * CT + i) * CS + s
                    eng.wait_ge(hi_done, g + 1)
                    eng.tensor_tensor(Glo[:, s, :], (Gx if a == 3 else G)[:, s, :], Ghi[:, s, :].bitcast(F32),
                                      ALU.subtract).then_inc(lo_done, 1)

                def take_extra(i, s):
                    g = (a * CT + i) * CS + s
                    eng.wait_ge(summed, g + 1)
                    wait(eng, scattered[s], 16 * (a * CT + i))
                    wait(eng, lrow_out[s], 16 * (a * CT + i))
                    eng.tensor_copy(O[:, s, D:AW], bank[4 + s][:, 0:HEADS]).then_inc(out_extra, 1)

                stages = [(equal_edges, 0), (split_lo, 0), (take_extra, 2)]
                if a == 3:
                    stages = [(weigh, 0), (equal_edges, 1), (split_lo, 1), (take_extra, 3)]
                in_turns(eng, CT, CS, stages)
                eng.wait_ge(fix_in, 16 * (a + 1))
                eng.wait_ge(carried, 2 * (a + 1))
                eng.tensor_tensor(fy[:, 0:D], fx[:, 0:D], bank[0][0:CHUNKS, 0:D], ALU.add).then_inc(fixed, 1)
                eng.tensor_tensor(fy[:, D:AW], fx[:, D:AW], bank[4][0:CHUNKS, 0:HEADS], ALU.add).then_inc(fixed, 1)

            def moments(g, sems, tile, st_t, mv_t):
                eng.bn_stats(st_t, tile).then_inc(sems[0], 1)
                eng.wait_ge(sems[0], g + 1)
                eng.sem_inc(dve_go, 1)
                eng.bn_aggr(mv_t, st_t).then_inc(sems[1], 1)
                eng.wait_ge(sems[1], g + 1)
                eng.tensor_scalar(mv_t[:, 1:2], mv_t[:, 1:2], EPS, None, ALU.add).then_inc(sems[2], 1)

            def shift(g, sems, mv_t, sd_t):
                eng.wait_ge(sems[3], g + 1)
                eng.reciprocal(sd_t[:, 1:2], sd_t[:, 0:1]).then_inc(sems[4], 1)
                eng.wait_ge(sems[4], g + 1)
                eng.tensor_scalar(sd_t[:, 2:3], mv_t[:, 0:1], sd_t[:, 1:2], -1.0, ALU.mult, ALU.mult).then_inc(sems[5], 1)

            for l in range(LAYERS):
                weights_lo(2 * l, 2)
                aggregate(l)
                eng.wait_ge(r_in, 16 * 3 * (l + 1))

                def inverse_count(i, s):
                    g = (l * TT + i) * TS + s
                    eng.wait_ge(ring4[s % 4], 16 * (2 * (l * TT + i) + s // 4 + 1))
                    eng.tensor_scalar(inv[:, s % 4, 0:1], ain[:, s % 4, D:D + 1], 1.0, None, ALU.max).then_inc(inv_max, 1)
                    eng.wait_ge(inv_max, g + 1)
                    eng.reciprocal(inv[:, s % 4, 1:2], inv[:, s % 4, 0:1]).then_inc(inv_done, 1)

                def split_nodes_lo(i, s):
                    g = (l * TT + i) * TS + s
                    o = s % 2
                    eng.wait_ge(nhi, g + 1)
                    eng.tensor_tensor(xlo[:, o, :], bank[o][:, :], xhi[:, o, :].bitcast(F32), ALU.subtract)
                    eng.tensor_tensor(alo[:, o, :], bank[2 + o][:, :], ahi[:, o, :].bitcast(F32), ALU.subtract).then_inc(nlo, 1)

                def statistics(i, s):
                    g = (l * TT + i) * TS + s
                    o = s % 2
                    eng.wait_ge(mm_done, g + 1)
                    wait(eng, nrm, g - 1)
                    eng.tensor_tensor(h[:, o, :], bank[4 + o][:, :], rows_bc[:, 0, :], ALU.add).then_inc(h_done, 1)
                    eng.wait_ge(h_done, g + 1)
                    moments(g, ln1, h[:, o, :], st[:, o, :], mv[:, o, :])

                def shifts(i, s):
                    shift((l * TT + i) * TS + s, ln1, mv[:, s % 2, :], sd[:, s % 2, :])

                def residual(i, s):
                    g = (l * TT + i) * TS + s
                    eng.wait_ge(g_add, g + 1)
                    wait(eng, store4[s % 4], 16 * (2 * (l * TT + i) + s // 4))
                    eng.scalar_tensor_tensor(out=y[:, s % 4, :], in0=hn[:, s % 2, :], scalar=0.0, in1=xin[:, s, :],
                                             op0=ALU.max, op1=ALU.add).then_inc(y_done, 1)

                in_turns(eng, TT, TS, [(shifts, 5), (inverse_count, 0), (split_nodes_lo, 2), (statistics, 4), (residual, 6)])

            weights_lo(2 * LAYERS, 2)

            def a_statistics(i, s):
                g = i * TS + s
                eng.wait_ge(a_add, g + 1)
                wait(eng, nrm, A0 + g - 1)
                moments(A0 + g, ln1, a_sum[:, s % 4, :], a_st[:, s % 2, :], a_mv[:, s % 2, :])

            def a_shifts(i, s):
                shift(A0 + i * TS + s, ln1, a_mv[:, s % 2, :], a_sd[:, s % 2, :])

            def a_split_lo(i, s):
                g = A0 + i * TS + s
                eng.wait_ge(nhi, g + 1)
                eng.tensor_tensor(a_lo[:, s % 2, :], bank[s % 2][:, :], a_hi[:, s % 2, :].bitcast(F32), ALU.subtract).then_inc(nlo, 1)

            def take_k(i, s):
                g = i * TS + s
                eng.wait_ge(mm_done, A0 + g + 1)
                wait(eng, qk_out[s % 4], 32 * (2 * i + s // 4))
                eng.tensor_copy(a_k[:, s % 4, :], bank[4 + s % 2][:, :]).then_inc(k_ev, 1)

            in_turns(eng, TT, TS, [(a_shifts, 2), (a_split_lo, 3), (a_statistics, 1), (take_k, 5)])

            def score(i, s):
                g = i * CS + s
                eng.wait_ge(kq_in[s], 32 * (i + 1))
                eng.tensor_tensor(b_kq[:, s % 2, :], b_k[:, s, :], b_q[:, s, :], ALU.mult).then_inc(b_mul, 1)
                eng.wait_ge(b_mul, g + 1)
                eng.sem_inc(dve_go, 1)
                eng.tensor_reduce(e_all[:, bass.ds(g, 1), :].rearrange("p c h -> p (c h)"),
                                  b_kq[:, s % 2, :].rearrange("p (h d) -> p h d", h=HEADS), AX.X, ALU.add).then_inc(b_red, 1)

            in_turns(eng, CT, CS, [(score, 0)])

            eng.wait_ge(mm_done, D0)
            eng.memset(m_row[:, :, :], 0.0).then_inc(m_step, 1)
            eng.wait_ge(m_step, 6)
            eng.tensor_tensor(m_row[:, 0, 1:P], drow[:, 1:P], drow[:, 0:P - 1], ALU.is_equal)
            eng.tensor_tensor(m_row[:, 1, 0:P - 1], drow[:, 1:P], drow[:, 0:P - 1], ALU.is_equal).then_inc(m_step, 1)
            eng.wait_ge(m_step, 7)
            for k, tile in enumerate((m_new, m_end)):
                eng.tensor_scalar(tile[:, :, :], m_row[:, k:k + 1, :].broadcast_to([CHUNKS, HEADS, P]), -1.0, FAR, ALU.add, ALU.mult)
            for k, tile in enumerate((m_first, m_last)):
                eng.tensor_scalar(m_t[:, k, :], drow[:, :], ends_f[:, k:k + 1], None, ALU.is_equal).then_inc(m_step, 1)
                eng.wait_ge(m_step, 8 + k)
                eng.tensor_scalar(tile[:, :], m_t[:, k, :], -1.0, FAR, ALU.add, ALU.mult)
            eng.tensor_scalar(m_prev[:, :], back_m[:, :], -1.0, FAR, ALU.add, ALU.mult)
            eng.tensor_scalar(m_next[:, :], carry_m[:, :], -1.0, FAR, ALU.add, ALU.mult).then_inc(m_step, 1)
            eng.wait_ge(m_pe, HEADS)
            eng.tensor_copy(m_e[:, 0:4, :].rearrange("p h e -> p (h e)"), bank[4][0:CHUNKS, :])
            eng.tensor_copy(m_e[:, 4:8, :].rearrange("p h e -> p (h e)"), bank[5][0:CHUNKS, :]).then_inc(m_step, 1)
            eng.wait_ge(m_step, 11)
            flat = [x[:, :, :].rearrange("p h e -> p (h e)") for x in (m_new, m_e, m_f, m_end)]
            eng.tensor_tensor_scan(flat[2], flat[0], flat[1], -FAR, ALU.add, ALU.max).then_inc(m_step, 1)
            eng.wait_ge(m_step, 12)
            eng.tensor_tensor_scan(flat[1][:, ::-1], flat[3][:, ::-1], flat[2][:, ::-1], -FAR, ALU.add, ALU.max).then_inc(m_step, 1)
            eng.wait_ge(m_step, 13)
            eng.tensor_copy(m_ce[:, 0, :], m_f[:, :, P - 1])
            eng.tensor_copy(m_ce[:, 1, :], m_e[:, :, 0]).then_inc(m_step, 1)
            eng.wait_ge(ends_in, 16)
            for k, mask in enumerate((m_prev, m_next)):
                eng.tensor_tensor(m_ends[:, :, k], m_ends[:, :, k], mask[:, :].unsqueeze(2).broadcast_to([CHUNKS, CHUNKS, HEADS]),
                                  ALU.add).then_inc(m_step, 1)
                eng.wait_ge(m_step, 15 + 2 * k)
                eng.tensor_reduce(m_c[:, k, :], m_ends[:, :, k].rearrange("p c h -> p h c"), AX.X, ALU.max).then_inc(m_step, 1)
            eng.wait_ge(m_step, 18)
            for k, mask in enumerate((m_first, m_last)):
                eng.tensor_tensor(m_t[:, :, :], mask[:, :].unsqueeze(1).broadcast_to([CHUNKS, HEADS, P]),
                                  m_c[:, k, :].unsqueeze(2).broadcast_to([CHUNKS, HEADS, P]), ALU.add).then_inc(m_step, 1)
                eng.wait_ge(m_step, 19 + 2 * k)
                eng.tensor_tensor(m_e[:, :, :], m_e[:, :, :], m_t[:, :, :], ALU.max).then_inc(m_step, 1)
                eng.wait_ge(m_step, 20 + 2 * k)
            eng.wait_ge(m_pe, 2 * HEADS)
            for k in range(2):
                half = e_all[:, :, 4 * k:4 * k + 4].rearrange("p c h -> p h c")
                eng.tensor_tensor(half, half, bank[6 + k][:, 0:4 * CHUNKS].rearrange("p (h c) -> p h c", h=4), ALU.subtract).then_inc(m_step, 1)
            eng.wait_ge(m_act, 2)
            eng.tensor_tensor(ex_lo[:, :, :], ex[:, :, :], ex_hi[:, :, :].bitcast(F32), ALU.subtract).then_inc(ex_split, 1)
            aggregate(3)
            eng.wait_ge(r_in, 16 * (3 * LAYERS + 8))
            weights_lo(2 * LAYERS + 2, 1)

            def inverse_weight(i, s):
                g = A0 + i * TS + s
                eng.wait_ge(ring4[s % 4], R4_D + 16 * (2 * i + s // 4 + 1))
                eng.tensor_scalar(d_z[:, s % 4, 0, :], d_a[:, s % 4, D:AW], 1e-30, None, ALU.max).then_inc(inv_max, 1)
                eng.wait_ge(inv_max, g + 1)
                eng.reciprocal(d_z[:, s % 4, 1, :], d_z[:, s % 4, 0, :]).then_inc(inv_done, 1)

            def d_split_lo(i, s):
                eng.wait_ge(nhi, D0 + i * TS + s + 1)
                eng.tensor_tensor(d_lo[:, s % 2, :], bank[s % 2][:, :], d_hi[:, s % 2, :].bitcast(F32), ALU.subtract).then_inc(nlo, 1)

            def d_stats1(i, s):
                g = i * TS + s
                o = s % 2
                eng.wait_ge(mm_done, D0 + g + 1)
                eng.wait_ge(ring8[s], 16 * (R8_D + i + 1))
                wait(eng, nrm, D0 + g - 1)
                eng.tensor_tensor(d_s1[:, o, :], bank[2 + o][:, :], d_h[:, s, :], ALU.add).then_inc(h_done, 1)
                eng.wait_ge(h_done, A0 + g + 1)
                moments(D0 + g, ln1, d_s1[:, o, :], d_st[:, o, :], d_mv[:, o, :])

            def d_stats2(i, s):
                g = i * TS + s
                o = s % 2
                eng.wait_ge(f_2, g + 1)
                wait(eng, nrm2, g - 1)
                eng.tensor_tensor(d_s2[:, o, :], bank[6 + o][:, :], d_y[:, s, :], ALU.add).then_inc(s2_done, 1)
                eng.wait_ge(s2_done, g + 1)
                moments(g, ln2, d_s2[:, o, :], d_st[:, 2 + o, :], d_mv[:, 2 + o, :])

            def d_stats3(i, s):
                g = i * TS + s
                o = s % 2
                eng.wait_ge(g_add2, g + 1)
                eng.wait_ge(h2_in[s % 4], 16 * (2 * i + s // 4 + 1))
                wait(eng, o_done, g - 1)
                eng.tensor_tensor(d_s3[:, o, :], d_n2[:, o, :], d_h2[:, s % 4, :], ALU.add).then_inc(s3_done, 1)
                eng.wait_ge(s3_done, g + 1)
                moments(g, ln3, d_s3[:, o, :], d_st[:, 4 + o, :], d_mv[:, 4 + o, :])

            in_turns(eng, TT, TS, [
                (lambda i, s: shift(D0 + i * TS + s, ln1, d_mv[:, s % 2, :], d_sd[:, s % 2, :]), 5),
                (lambda i, s: shift(i * TS + s, ln2, d_mv[:, 2 + s % 2, :], d_sd[:, 2 + s % 2, :]), 10),
                (lambda i, s: shift(i * TS + s, ln3, d_mv[:, 4 + s % 2, :], d_sd[:, 4 + s % 2, :]), 12),
                (inverse_weight, 0), (d_split_lo, 2), (d_stats1, 4), (d_stats2, 9), (d_stats3, 11)])


_SAME = ["L0_gnn_b", "L0_gnn_ln_g", "L0_gnn_ln_b", "L1_gnn_Wq", "L1_gnn_Wk", "L1_gnn_Wv", "L1_gnn_Wo",
         "L1_gnn_W1", "L1_gnn_W2"]
_ROWS = ["L1_gnn_ln1_g", "L1_gnn_ln1_b", "L1_gnn_ln2_g", "L1_gnn_ln2_b", "L1_gnn_b2"]


def kernel(**inputs):
    import concourse.bacc as bacc
    from concourse.bass_utils import run_bass_kernel_spmd

    a = {k: np.asarray(v) for k, v in inputs.items()}
    x = np.zeros((NP, D), np.float32)
    x[:NODES] = a["x"]
    src = np.zeros(EP, np.int32)
    src[:EDGES] = a["src"]
    dst = np.full(EP, NODES, np.int32)
    dst[:EDGES] = a["dst"]
    around = np.full(EP + 2, -1, np.int32)
    around[1:-1] = dst
    first = np.arange(CHUNKS) * P
    last = first + P - 1
    arrays = {
        "x": x,
        "src_cols": np.ascontiguousarray(src.reshape(CHUNKS, P).T),
        "dst_cols": np.ascontiguousarray(dst.reshape(CHUNKS, P).T),
        "next_cols": np.ascontiguousarray(around[2:].reshape(CHUNKS, P).T),
        "dst_rows": dst.reshape(CHUNKS, P),
        "dst_row": dst.reshape(1, EP),
        "first_row": np.ascontiguousarray(dst[first]).reshape(1, CHUNKS),
        "last_row": np.ascontiguousarray(dst[last]).reshape(1, CHUNKS),
        "ends": np.ascontiguousarray(np.stack([dst[first], dst[last], around[first], around[last + 2]], 1)),
        "L0_WlT": np.ascontiguousarray(a["L0_gnn_W_l"].transpose(0, 2, 1)),
        "L0_WrT": np.ascontiguousarray(a["L0_gnn_W_r"].transpose(0, 2, 1)),
        "b1_col": np.ascontiguousarray(a["L1_gnn_b1"]).reshape(DFF, 1),
    }
    for name in _SAME:
        arrays[name] = np.ascontiguousarray(a[name])
    for name in _ROWS:
        arrays[name] = np.ascontiguousarray(a[name]).reshape(1, D)
    nc = bacc.Bacc("TRN2", target_bir_lowering=False, num_devices=1)
    t = {n: nc.dram_tensor("in_" + n, v.shape, mybir.dt.from_np(v.dtype), kind="ExternalInput").ap()
         for n, v in arrays.items()}
    out = nc.dram_tensor("out", (NP, D), F32, kind="ExternalOutput").ap()
    build(nc, t, out)
    r = run_bass_kernel_spmd(nc, [{"in_" + n: v for n, v in arrays.items()}], core_ids=[0])
    return np.ascontiguousarray(r.results[0]["out"][:NODES])
```

```python
import numpy as np
import concourse.bass as bass
from concourse import mybir
from contextlib import ExitStack

F32 = mybir.dt.float32
F32R = mybir.dt.float32r
I32 = mybir.dt.int32
ALU = mybir.AluOpType
ACT = mybir.ActivationFunctionType
AX = mybir.AxisListType

P = 128
D = 512
KC = D // P
NODES, EDGES = 10000, 15000
LAYERS, HEADS, DFF = 3, 8, 64
DK = D // HEADS
TS, CB = 8, 12
CS = 4
CU = CB // CS
TT = max(-(-NODES // (P * TS)), -(-EDGES // (P * CB)))
TILES, CHUNKS = TT * TS, TT * CB
NP, EP = TILES * P, CHUNKS * P
AW = D + HEADS
SKIP = 1 << 15
EPS = 1e-5
FAR = 1.0e38


def in_turns(eng, units, stages):
    stages = [(stage, lag, rate[0] if rate else 1) for stage, lag, *rate in stages]
    late = max(-(-lag // (units * rate)) for _, lag, rate in stages)

    def turn(i, guard):
        for unit in range(units):
            for j in range(max(rate for _, _, rate in stages)):
                for stage, lag, rate in stages:
                    at, item = divmod(unit * rate + j - lag, units * rate)
                    if j >= rate or (guard and not 0 <= i + at < TT):
                        continue
                    stage(i + at if guard or at else i, item)

    for i in range(1 + late):
        turn(i, True)
    with eng.Fori(1 + late, TT) as i:
        turn(i, False)
    for i in range(TT, TT + late):
        turn(i, True)


def wait(eng, semaphore, count):
    if not isinstance(count, int) or count > 0:
        eng.wait_ge(semaphore, count)


def build(nc, t, out):
    ctx = ExitStack()
    with ctx:
        def sem(name):
            return ctx.enter_context(nc.semaphore(name))

        def ring(name, n):
            return [sem(f"{name}{i}") for i in range(n)]

        def dram(name, shape, dt=F32):
            return nc.dram_tensor(name, shape, dt, kind="Internal").ap()

        xs = dram("xs", [NP, D])
        agg = dram("agg", [NP, AW])
        lrows = dram("lrows", [CHUNKS, AW])
        hs = dram("hs", [NP, D])
        qs = dram("qs", [NP, D])
        ks = dram("ks", [NP, D])
        vs = dram("vs", [NP, D])
        zs = dram("zs", [NP, D])
        ends_m = dram("ends_m", [CHUNKS, 2 * HEADS])

        top = [nc.sbuf_base]

        def sb(name, shape, dt=F32):
            size = int(np.prod(shape[1:])) * mybir.dt.size(dt)
            top[0] = -(-top[0] // 32) * 32
            tensor = nc.alloc_sbuf_tensor_at(name, shape, dt, offset=top[0])
            top[0] += size
            return tensor

        ident = sb("ident", [P, P])
        dst_bc = sb("dst_bc", [P, EP], I32)
        src_i = sb("src_i", [P, CHUNKS], I32)
        dst_i = sb("dst_i", [P, CHUNKS], I32)
        dst_f = sb("dst_f", [P, CHUNKS])
        nxt_i = sb("nxt_i", [P, CHUNKS], I32)
        same = sb("same", [P, CHUNKS])
        put_i = sb("put_i", [P, CHUNKS], I32)
        get_now = sb("get_now", [P, CB], I32)
        get_now2 = sb("get_now2", [P, CB], I32)
        put_now = sb("put_now", [P, CB], I32)
        inv_n = sb("inv_n", [P, TILES])
        eps = sb("eps", [P, 1])
        ends_i = sb("ends_i", [CHUNKS, 4], I32)
        ends_f = sb("ends_f", [CHUNKS, 4])
        first_bc = sb("first_bc", [CHUNKS, CHUNKS], I32)
        last_bc = sb("last_bc", [CHUNKS, CHUNKS], I32)
        carry_m = sb("carry_m", [CHUNKS, CHUNKS])
        back_m = sb("back_m", [CHUNKS, CHUNKS])
        fixt = sb("fixt", [CHUNKS, 2])
        fix_i = sb("fix_i", [CHUNKS, 1], I32)
        ones_r = sb("ones_r", [P, P], F32R)
        onesf = sb("onesf", [P, P])
        drow = sb("drow", [CHUNKS, P], I32)
        e_all = sb("e_all", [P, CHUNKS, HEADS])
        shared = top[0]

        G = sb("G", [P, CS, D])
        Ghi = sb("Ghi", [P, CS, D], F32R)
        Glo = sb("Glo", [P, CS, D], F32R)
        E = sb("E", [P, CS, P], F32R)
        O = sb("O", [P, CS, AW])
        lr = sb("lr", [CHUNKS, AW])
        fx = sb("fx", [CHUNKS, AW])
        fy = sb("fy", [CHUNKS, AW])
        edges_end = top[0]
        zx = sb("zx", [P, 4, D])
        zhi = sb("zhi", [P, 2, D], F32R)
        zlo = sb("zlo", [P, 2, D], F32R)
        zo = sb("zo", [P, 4, D])
        weights = shared + 66 * 1024
        assert top[0] <= weights

        top[0] = shared
        xin = sb("xin", [P, 4, D])
        ain = sb("ain", [P, 4, AW])
        zin = sb("zin", [P, 4, D])
        inv = sb("inv", [P, 2])
        an = sb("an", [P, 2, D])
        ahi = sb("ahi", [P, 2, D], F32R)
        alo = sb("alo", [P, 2, D], F32R)
        h = sb("h", [P, 2, D])
        st = sb("st", [P, 2, 6])
        mv = sb("mv", [P, 2, 2])
        sd = sb("sd", [P, 2, 3])
        hn = sb("hn", [P, 4, D])
        y = sb("y", [P, 4, D])
        assert top[0] <= weights, top
        top[0] = weights
        wraw = sb("wraw", [P, 2, KC, D])
        whi = sb("whi", [P, 2, KC, D], F32R)
        wlo = sb("wlo", [P, 2, KC, D], F32R)
        rows_bc = sb("rows_bc", [P, 5, D])
        rows_end = top[0]

        top[0] = shared
        a_x3 = sb("a_x3", [P, 4, D])
        a_x0 = sb("a_x0", [P, 4, D])
        a_sum = sb("a_sum", [P, 4, D])
        a_h = sb("a_h", [P, 4, D])
        a_hi = sb("a_hi", [P, 2, D], F32R)
        a_lo = sb("a_lo", [P, 2, D], F32R)
        a_q = sb("a_q", [P, 4, D])
        a_k = sb("a_k", [P, 4, D])
        a_st = sb("a_st", [P, 2, 6])
        a_mv = sb("a_mv", [P, 2, 2])
        a_sd = sb("a_sd", [P, 2, 3])
        assert top[0] <= weights

        top[0] = shared
        b_k = sb("b_k", [P, CS, D])
        b_q = sb("b_q", [P, CS, D])
        b_kq = sb("b_kq", [P, 2, D])
        v_h = sb("v_h", [P, TS, D])
        v_hi = sb("v_hi", [P, 2, D], F32R)
        v_lo = sb("v_lo", [P, 2, D], F32R)
        v_o = sb("v_o", [P, 4, D])
        values_end = top[0]
        top[0] = weights + 4 * KC * D * 2
        m_e = sb("m_e", [CHUNKS, HEADS, P])
        m_f = sb("m_f", [CHUNKS, HEADS, P])
        m_new = sb("m_new", [CHUNKS, HEADS, P])
        m_end = sb("m_end", [CHUNKS, HEADS, P])
        m_t = sb("m_t", [CHUNKS, HEADS, P])
        m_row = sb("m_row", [CHUNKS, 3, P])
        m_first = sb("m_first", [CHUNKS, P])
        m_last = sb("m_last", [CHUNKS, P])
        m_prev = sb("m_prev", [CHUNKS, CHUNKS])
        m_next = sb("m_next", [CHUNKS, CHUNKS])
        m_ends = sb("m_ends", [CHUNKS, CHUNKS, 2, HEADS])
        m_ce = sb("m_ce", [CHUNKS, 2, HEADS])
        m_c = sb("m_c", [CHUNKS, 2, HEADS])
        assert top[0] <= weights + 24 * KC * D
        top[0] = weights + 8 * KC * D
        Gx = sb("Gx", [P, CS, D])
        top[0] = max(edges_end, values_end)
        ex = sb("ex", [P, CHUNKS, HEADS])
        ex_hi = sb("ex_hi", [P, CHUNKS, HEADS], F32R)
        ex_lo = sb("ex_lo", [P, CHUNKS, HEADS], F32R)
        assert top[0] <= weights
        assert top[0] <= nc.sbuf_usable_end, (top, nc.sbuf_usable_end)

        top[0] = shared
        d_a = sb("d_a", [P, 4, AW])
        d_z = sb("d_z", [P, 4, 2, HEADS])
        d_h = sb("d_h", [P, 4, D])
        d_n = sb("d_n", [P, 2, D])
        d_hi = sb("d_hi", [P, 2, D], F32R)
        d_lo = sb("d_lo", [P, 2, D], F32R)
        d_s1 = sb("d_s1", [P, 2, D])
        d_y = sb("d_y", [P, TS, D])
        d_yt = sb("d_yt", [P, 2, D])
        d_f = sb("d_f", [DFF, 2, P])
        d_st = sb("d_st", [P, 6, 6])
        d_mv = sb("d_mv", [P, 6, 2])
        d_sd = sb("d_sd", [P, 6, 3])
        d_n2 = sb("d_n2", [P, 4, D])
        b2_hi = sb("b2_hi", [1, D], F32R)
        b2_lo = sb("b2_lo", [1, D], F32R)
        d_end = top[0]
        top[0] = weights + 4 * KC * D
        d_s2 = sb("d_s2", [P, 2, D])
        assert top[0] <= weights + 8 * KC * D
        top[0] = weights + 12 * KC * D
        d_s3 = sb("d_s3", [P, 2, D])
        w1 = sb("w1", [P, KC, DFF])
        w2 = sb("w2", [DFF, D])
        b1c = sb("b1c", [DFF, 1])
        assert top[0] <= weights + 16 * KC * D
        top[0] = weights + 20 * KC * D
        d_o = sb("d_o", [P, 4, D])
        assert top[0] <= weights + 24 * KC * D
        assert d_end <= weights, (d_end, weights)
        top[0] = rows_end
        d_h2 = sb("d_h2", [P, 4, D])
        top[0] = rows_end
        zero = sb("zero", [P, 4, AW])
        assert top[0] <= nc.sbuf_usable_end

        bank = [ctx.enter_context(nc.psum_tensor(f"bank{i}", [P, 512], F32)) for i in range(8)]

        idx_in, tables, zero_set, zeroed, prep = map(sem, ("idx_in", "tables", "zero_set", "zeroed", "prep"))
        src_in, eps_set = sem("src_in"), sem("eps_set")
        pool_go, dve_go = sem("pool_go"), sem("dve_go")
        w_in, w_hi, w_lo = map(sem, ("w_in", "w_hi", "w_lo"))
        r_in = sem("r_in")
        gathered, scattered, lrow_out = ring("gathered", CS), ring("scattered", CS), ring("lrow_out", CS)
        z_in, z_out, zr_in = ring("z_in", 4), ring("z_out", 4), ring("zr_in", 4)
        b_in, z_tp, z_hi, z_lo, z_mm, z_ev, get2_set = map(
            sem, ("b_in", "z_tp", "z_hi", "z_lo", "z_mm", "z_ev", "get2_set"))
        get_set, put_set, hi_done, lo_done, eq_done, summed, out_main, out_extra = map(
            sem, ("get_set", "put_set", "hi_done", "lo_done", "eq_done", "summed", "out_main", "out_extra"))
        lr_in, carried, fix_in, fixed, fix_out = map(sem, ("lr_in", "carried", "fix_in", "fixed", "fix_out"))
        ring8, ring4, store4 = ring("ring8", 8), ring("ring4", 4), ring("store4", 4)
        xr_in = ring("xr_in", 4)
        inv_max, inv_done, an_done, tposed, nhi, nlo, mm_done, h_done = map(
            sem, ("inv_max", "inv_done", "an_done", "tposed", "nhi", "nlo", "mm_done", "h_done"))
        bn, ag, var_d, sd_done, rc, rs_done, nrm, g_mul, g_add, y_done = map(
            sem, ("bn", "ag", "var_d", "sd_done", "rc", "rs_done", "nrm", "g_mul", "g_add", "y_done"))
        h_out, qk_out = ring("h_out", 4), ring("qk_out", 4)
        a_add, q_ev, k_ev = map(sem, ("a_add", "q_ev", "k_ev"))
        kq_in = ring("kq_in", CS)
        v_tp, v_hid, v_lod, v_mm, v_out, b_mul, b_red = map(sem, ("v_tp", "v_hid", "v_lod", "v_mm", "v_out", "b_mul", "b_red"))
        m_step, m_pe, m_act, ends_out, ends_in = map(sem, ("m_step", "m_pe", "m_act", "ends_out", "ends_in"))
        gx_done, ex_split, b2_split = sem("gx_done"), sem("ex_split"), sem("b2_split")
        h2_in = ring("h2_in", 4)
        f_tp, f_t, f_1, f_r, f_2 = map(sem, ("f_tp", "f_t", "f_1", "f_r", "f_2"))
        s2_done, s3_done, o_done, nrm2, g_mul2, g_add2 = map(
            sem, ("s2_done", "s3_done", "o_done", "nrm2", "g_mul2", "g_add2"))
        ln2 = [sem(f"ln2_{n}") for n in ("bn", "ag", "var", "sd", "rc", "rs")]
        ln3 = [sem(f"ln3_{n}") for n in ("bn", "ag", "var", "sd", "rc", "rs")]
        ln1 = [bn, ag, var_d, sd_done, rc, rs_done]

        A0, D0 = LAYERS * TILES, (LAYERS + 1) * TILES
        XR_D = LAYERS * 2 * TT
        R4_A = LAYERS * 2 * TT * 16
        R4_D = R4_A + 2 * TT * 32
        ST_V, ST_D = LAYERS * 2 * TT, (LAYERS + 1) * 2 * TT

        def rows(i, s):
            return bass.ds((i * TS + s) * P, P)

        block = ctx.enter_context(nc.Block())

        @block.sync
        def _(eng):
            eng.dma_start(src_i[:, :], t["src_cols"]).then_inc(src_in, 16)
            for tile, name in ((dst_i, "dst_cols"), (nxt_i, "next_cols"), (ends_i, "ends"),
                               (drow, "dst_rows")):
                eng.dma_start(tile[:, :], t[name]).then_inc(idx_in, 16)
            eng.dma_start(first_bc[:, :], t["first_row"].broadcast_to([CHUNKS, CHUNKS])).then_inc(idx_in, 16)
            eng.dma_start(last_bc[:, :], t["last_row"].broadcast_to([CHUNKS, CHUNKS])).then_inc(idx_in, 16)
            eng.dma_start(dst_bc[:, :], t["dst_row"].broadcast_to([P, EP])).then_inc(idx_in, 16)
            eng.wait_ge(zero_set, 1)
            agg_flat = agg.rearrange("(p r) w -> p (r w)", p=P)
            for r in range(TILES // CS):
                eng.dma_start(agg_flat[:, r * CS * AW:(r + 1) * CS * AW],
                              zero[:, :, :].rearrange("p s w -> p (s w)")).then_inc(zeroed, 16)

            def save_last_row(a, i, s):
                g = (a * TT + i) * CB + s
                eng.wait_ge(out_main, g + 1)
                eng.wait_ge(out_extra, g + 1)
                eng.dma_start(lrows[bass.ds(i * CB + s, 1), :], O[P - 1:P, s % CS, :]).then_inc(lrow_out[s % CS], 16)

            def carries(a):
                for s in range(CS):
                    eng.wait_ge(lrow_out[s], 16 * CU * TT * (a + 1))
                eng.dma_start(lr[:, :], lrows).then_inc(lr_in, 16)
                eng.wait_ge(fix_out, 16 * (a + 1))

            def load_right(l):
                eng.dma_start(wraw[:, 1], t["L0_WrT"][l].rearrange("(k p) n -> p k n", p=P)).then_inc(b_in, 16)
                eng.dma_start(rows_bc[:, 0], t["L0_gnn_b"][l:l + 1, :].broadcast_to([P, D])).then_inc(b_in, 16)

            load_right(0)
            for l in range(LAYERS):
                x_now = t["x"] if l == 0 else xs
                wait(eng, mm_done, l * TILES)
                eng.dma_start(wraw[:, 0], t["L0_WlT"][l].rearrange("(k p) n -> p k n", p=P)).then_inc(w_in, 16)
                wait(eng, y_done, l * TILES)
                for k, name in ((1, "L0_gnn_ln_g"), (2, "L0_gnn_ln_b")):
                    eng.dma_start(rows_bc[:, k], t[name][l:l + 1, :].broadcast_to([P, D])).then_inc(r_in, 16)

                def z_load(i, s):
                    g = (l * TT + i) * TS + s
                    wait(eng, z_tp, g - 3)
                    eng.dma_start(zx[:, s % 4, :], x_now[rows(i, s), :]).then_inc(z_in[s % 4], 16)

                def z_store(i, s):
                    eng.wait_ge(z_ev, (l * TT + i) * TS + s + 1)
                    eng.dma_start(zs[rows(i, s), :], zo[:, s % 4, :]).then_inc(z_out[s % 4], 16)

                in_turns(eng, 4, [(lambda i, s: save_last_row(l, i, s), 6, 3), (z_load, 0, 2), (z_store, 7, 2)])
                carries(l)
                for s in range(4):
                    eng.wait_ge(z_out[s], 16 * 2 * TT * (l + 1))
                if l < LAYERS - 1:
                    load_right(l + 1)

                def load(i, s):
                    g = (l * TT + i) * TS + s
                    wait(eng, an_done, g - 3)
                    eng.dma_start(ain[:, s % 4, :], agg[rows(i, s), :]).then_inc(ring4[s % 4], 16)

                def store(i, s):
                    g = (l * TT + i) * TS + s
                    eng.wait_ge(y_done, g + 1)
                    eng.dma_start(xs[rows(i, s), :], y[:, s % 4, :]).then_inc(store4[s % 4], 16)

                def load_x(i, s):
                    wait(eng, y_done, (l * TT + i) * TS + s - 3)
                    eng.dma_start(xin[:, s % 4, :], x_now[rows(i, s), :]).then_inc(xr_in[s % 4], 16)

                def load_z(i, s):
                    wait(eng, h_done, (l * TT + i) * TS + s - 3)
                    eng.dma_start(zin[:, s % 4, :], zs[rows(i, s), :]).then_inc(zr_in[s % 4], 16)

                in_turns(eng, TS, [(load, 0), (load_z, 5), (load_x, 8), (store, 12)])
                for s in range(4):
                    eng.wait_ge(store4[s], 16 * 2 * TT * (l + 1))

            eng.wait_ge(mm_done, A0)
            for k, name in enumerate(("L1_gnn_Wq", "L1_gnn_Wk")):
                eng.dma_start(wraw[:, k], t[name].rearrange("(k p) n -> p k n", p=P)).then_inc(w_in, 16)

            def a_load(i, s):
                g = i * TS + s
                wait(eng, a_add, g - 3)
                eng.dma_start(a_x3[:, s % 4, :], xs[rows(i, s), :]).then_inc(ring4[s % 4], 16)
                eng.dma_start(a_x0[:, s % 4, :], t["x"][rows(i, s), :]).then_inc(ring4[s % 4], 16)

            def a_store_h(i, s):
                eng.wait_ge(nrm, A0 + i * TS + s + 1)
                eng.dma_start(hs[rows(i, s), :], a_h[:, s % 4, :]).then_inc(h_out[s % 4], 16)

            def a_store_qk(i, s):
                g = i * TS + s
                eng.wait_ge(q_ev, g + 1)
                eng.dma_start(qs[rows(i, s), :], a_q[:, s % 4, :]).then_inc(qk_out[s % 4], 16)
                eng.wait_ge(k_ev, g + 1)
                eng.dma_start(ks[rows(i, s), :], a_k[:, s % 4, :]).then_inc(qk_out[s % 4], 16)

            in_turns(eng, TS, [(a_load, 0), (a_store_h, 6), (a_store_qk, 11)])
            for s in range(4):
                eng.wait_ge(qk_out[s], 32 * 2 * TT)
                eng.wait_ge(h_out[s], 16 * 2 * TT)

            eng.dma_start(wraw[:, 0], t["L1_gnn_Wv"].rearrange("(k p) n -> p k n", p=P)).then_inc(w_in, 16)

            def v_load(i, s):
                wait(eng, v_tp, i * TS + s - 7)
                eng.dma_start(v_h[:, s, :], hs[rows(i, s), :]).then_inc(ring8[s], 16)

            def v_store(i, s):
                eng.wait_ge(v_out, i * TS + s + 1)
                eng.dma_start(vs[rows(i, s), :], v_o[:, s % 4, :]).then_inc(store4[s % 4], 16)

            in_turns(eng, TS, [(v_load, 0), (v_store, 10)])

            eng.wait_ge(m_step, 14)
            eng.dma_start(ends_m, m_ce[:, :, :].rearrange("p a h -> p (a h)")).then_inc(ends_out, 16)
            eng.wait_ge(ends_out, 16)
            eng.dma_start(m_ends[:, :, :, :].rearrange("p c a h -> p (c a h)"),
                          ends_m.rearrange("c w -> (c w)").unsqueeze(0).broadcast_to([CHUNKS, 2 * CHUNKS * HEADS])
                          ).then_inc(ends_in, 16)

            eng.wait_ge(v_mm, TILES)
            eng.dma_start(wraw[:, 0], t["L1_gnn_Wo"].rearrange("(k p) n -> p k n", p=P)).then_inc(w_in, 16)
            for k, name in enumerate(("L1_gnn_ln1_g", "L1_gnn_ln1_b", "L1_gnn_ln2_g", "L1_gnn_ln2_b", "L1_gnn_b2")):
                eng.dma_start(rows_bc[:, k], t[name].broadcast_to([P, D])).then_inc(r_in, 16)
            in_turns(eng, CB, [(lambda i, s: save_last_row(3, i, s), 0)])
            carries(3)
            eng.dma_start(w1[:, :, :], t["L1_gnn_W1"].rearrange("(k p) n -> p k n", p=P)).then_inc(r_in, 16)
            eng.dma_start(w2[:, :], t["L1_gnn_W2"]).then_inc(r_in, 16)
            eng.dma_start(b1c[:, :], t["b1_col"]).then_inc(r_in, 16)

            def d_load(i, s):
                g = i * TS + s
                wait(eng, an_done, A0 + g - 3)
                eng.dma_start(d_a[:, s % 4, :], agg[rows(i, s), :]).then_inc(ring4[s % 4], 16)

            def d_load_h(i, s):
                wait(eng, h_done, A0 + i * TS + s - 3)
                eng.dma_start(d_h[:, s % 4, :], hs[rows(i, s), :]).then_inc(xr_in[s % 4], 16)

            def d_load_again(i, s):
                wait(eng, s3_done, i * TS + s - 3)
                eng.dma_start(d_h2[:, s % 4, :], hs[rows(i, s), :]).then_inc(h2_in[s % 4], 16)

            def d_store(i, s):
                eng.wait_ge(o_done, i * TS + s + 1)
                eng.dma_start(out[rows(i, s), :], d_o[:, s % 4, :]).then_inc(store4[s % 4], 16)

            in_turns(eng, TS, [(d_load, 0), (d_load_h, 5), (d_load_again, 16), (d_store, 21)])
            for s in range(4):
                eng.wait_ge(store4[s], 16 * (ST_D + 2 * TT))

        @block.gpsimd
        def _(eng):
            last_row = eng.to_reg(NP - 1)
            eng.memset(zero[:, :, :], 0.0).then_inc(zero_set, 1)
            eng.memset(ident[:, :], 0.0).then_inc(prep, 1)
            eng.wait_ge(src_in, 16)
            eng.wait_ge(prep, 1)
            eng.affine_select(out=ident[:, :], in_=ident[:, :], compare_op=ALU.not_equal, fill=1.0,
                              base=0, pattern=[[-1, P]], channel_multiplier=1).then_inc(prep, 1)
            eng.memset(onesf[:, :], 1.0).then_inc(prep, 1)
            eng.wait_ge(tables, 7)
            eng.affine_select(out=carry_m[:, :], in_=carry_m[:, :], compare_op=ALU.is_gt, fill=0.0,
                              base=0, pattern=[[1, CHUNKS]], channel_multiplier=-1).then_inc(prep, 1)
            eng.affine_select(out=back_m[:, :], in_=back_m[:, :], compare_op=ALU.is_gt, fill=0.0,
                              base=0, pattern=[[-1, CHUNKS]], channel_multiplier=1).then_inc(prep, 1)

            def aggregate(a, source):
                def gather(i, s):
                    g = (a * TT + i) * CB + s
                    n = (LAYERS + 1 if a == 3 else a) * TT + i
                    free = gx_done if a == 3 else lo_done
                    wait(eng, free, i * CB + s - 3 if a == 3 else g - 3)
                    if s % CS == 0:
                        eng.tensor_copy(get_now[:, s:s + CS], src_i[:, bass.ds(i * CB + s, CS)]).then_inc(get_set, 1)
                        eng.wait_ge(get_set, n * CU + s // CS + 1)
                    eng.sem_inc(pool_go, 1)
                    eng.indirect_dma_start(
                        out=G[:, s % CS, :], out_offset=None, in_=source,
                        in_offset=bass.IndirectOffsetOnAxis(ap=get_now[:, s:s + 1], axis=0),
                    ).then_inc(gathered[s % CS], 16)

                def scatter(i, s):
                    g = (a * TT + i) * CB + s
                    if a == 0 and isinstance(i, int) and i + s == 0:
                        eng.wait_ge(zeroed, 16 * (TILES // CS))
                    if s % CS == 0:
                        for k in range(CS):
                            wait(eng, scattered[k], 16 * ((a * TT + i) * CU + s // CS - CU + 1))
                        eng.tensor_copy(put_now[:, s:s + CS], put_i[:, bass.ds(i * CB + s, CS)]).then_inc(put_set, 1)
                        eng.wait_ge(put_set, (a * TT + i) * CU + s // CS + 1)
                    eng.wait_ge(out_main, g + 1)
                    eng.wait_ge(out_extra, g + 1)
                    eng.sem_inc(pool_go, 1)
                    eng.indirect_dma_start(
                        out=agg, out_offset=bass.IndirectOffsetOnAxis(ap=put_now[:, s:s + 1], axis=0),
                        in_=O[:, s % CS, :], in_offset=None, bounds_check=last_row, oob_is_err=False,
                    ).then_inc(scattered[s % CS], 16)

                in_turns(eng, CB, [(gather, 0), (scatter, CS)])
                for s in range(CS):
                    eng.wait_ge(scattered[s], 16 * CU * TT * (a + 1))
                eng.indirect_dma_start(
                    out=fx[:, :], out_offset=None, in_=agg,
                    in_offset=bass.IndirectOffsetOnAxis(ap=ends_i[:, 0:1], axis=0)).then_inc(fix_in, 16)
                eng.wait_ge(fixed, 2 * (a + 1))
                eng.indirect_dma_start(
                    out=agg, out_offset=bass.IndirectOffsetOnAxis(ap=fix_i[:, 0:1], axis=0),
                    in_=fy[:, :], in_offset=None, bounds_check=last_row, oob_is_err=False).then_inc(fix_out, 16)
                eng.wait_ge(fix_out, 16 * (a + 1))

            for l in range(LAYERS):
                for s in range(4):
                    wait(eng, store4[s], 16 * 2 * TT * l)
                aggregate(l, t["x"] if l == 0 else xs)
                eng.wait_ge(r_in, 16 * 2 * (l + 1))

                def affine(i, s):
                    g = (l * TT + i) * TS + s
                    eng.wait_ge(nrm, g + 1)
                    eng.tensor_tensor(hn[:, s % 4, :], hn[:, s % 4, :], rows_bc[:, 1, :], ALU.mult).then_inc(g_mul, 1)
                    eng.wait_ge(g_mul, g + 1)
                    eng.tensor_tensor(hn[:, s % 4, :], hn[:, s % 4, :], rows_bc[:, 2, :], ALU.add).then_inc(g_add, 1)

                in_turns(eng, TS, [(affine, 0)])

            for s in range(4):
                eng.wait_ge(store4[s], 16 * 2 * TT * LAYERS)

            def a_sums(i, s):
                g = i * TS + s
                eng.wait_ge(ring4[s % 4], R4_A + 32 * (2 * i + s // 4 + 1))
                wait(eng, nrm, A0 + g - 3)
                eng.tensor_tensor(a_sum[:, s % 4, :], a_x3[:, s % 4, :], a_x0[:, s % 4, :], ALU.add).then_inc(a_add, 1)

            in_turns(eng, TS, [(a_sums, 0)])

            for s in range(4):
                eng.wait_ge(qk_out[s], 32 * 2 * TT)

            def gather_kq(i, s):
                g = i * CB + s
                wait(eng, b_mul, g - 3)
                if s % CS == 0:
                    eng.tensor_copy(get_now[:, s:s + CS], src_i[:, bass.ds(g, CS)]).then_inc(get_set, 1)
                    eng.tensor_copy(get_now2[:, s:s + CS], dst_i[:, bass.ds(g, CS)]).then_inc(get2_set, 1)
                    eng.wait_ge(get_set, (LAYERS * TT + i) * CU + s // CS + 1)
                    eng.wait_ge(get2_set, i * CU + s // CS + 1)
                eng.sem_inc(pool_go, 1)
                for tile, row, source in ((b_k, get_now, ks), (b_q, get_now2, qs)):
                    eng.indirect_dma_start(
                        out=tile[:, s % CS, :], out_offset=None, in_=source,
                        in_offset=bass.IndirectOffsetOnAxis(ap=row[:, s:s + 1], axis=0)).then_inc(kq_in[s % CS], 16)

            in_turns(eng, CB, [(gather_kq, 0)])
            for s in range(4):
                eng.wait_ge(store4[s], 16 * (ST_V + 2 * TT))
            eng.wait_ge(b_mul, CHUNKS)
            aggregate(3, vs)
            eng.wait_ge(r_in, 16 * (2 * LAYERS + 8))

            def attention(i, s):
                g = i * TS + s
                eng.wait_ge(inv_done, TILES + g + 1)
                wait(eng, tposed, D0 + g - 1)
                eng.tensor_tensor(d_n[:, s % 2, :].rearrange("p (h d) -> p h d", h=HEADS),
                                  d_a[:, s % 4, 0:D].rearrange("p (h d) -> p h d", h=HEADS),
                                  d_z[:, s % 4, 1, :].unsqueeze(2).broadcast_to([P, HEADS, DK]),
                                  ALU.mult).then_inc(an_done, 1)

            def gain1(i, s):
                eng.wait_ge(nrm, D0 + i * TS + s + 1)
                eng.tensor_tensor(d_y[:, s, :], d_y[:, s, :], rows_bc[:, 0, :], ALU.mult).then_inc(g_mul, 1)

            def offset1(i, s):
                eng.wait_ge(g_mul, A0 + i * TS + s + 1)
                eng.tensor_tensor(d_y[:, s, :], d_y[:, s, :], rows_bc[:, 1, :], ALU.add).then_inc(g_add, 1)

            def gain2(i, s):
                eng.wait_ge(nrm2, i * TS + s + 1)
                eng.tensor_tensor(d_n2[:, s % 4, :], d_n2[:, s % 4, :], rows_bc[:, 2, :], ALU.mult).then_inc(g_mul2, 1)

            def offset2(i, s):
                eng.wait_ge(g_mul2, i * TS + s + 1)
                eng.tensor_tensor(d_n2[:, s % 4, :], d_n2[:, s % 4, :], rows_bc[:, 3, :], ALU.add).then_inc(g_add2, 1)

            in_turns(eng, TS, [(gain1, 7), (gain2, 15), (offset1, 7), (offset2, 15), (attention, 1)])

        @block.tensor
        def _(eng):
            eng.wait_ge(prep, 5)

            def segment_sums(a, i, s):
                g = (a * TT + i) * CB + s
                o = s % 2
                eng.wait_ge(eq_done, g + 1)
                eng.wait_ge(hi_done, g + 1)
                wait(eng, out_main, g - 1)
                eng.matmul(bank[o][:, 0:D], E[:, s % CS, :], Ghi[:, s % CS, :], start=True, stop=False)
                eng.wait_ge(lo_done, g + 1)
                eng.matmul(bank[o][:, 0:D], E[:, s % CS, :], Glo[:, s % CS, :], start=False, stop=True)
                wait(eng, out_extra, g - 1)
                if a < 3:
                    last = eng.matmul(bank[2 + o][:, 0:HEADS], E[:, s % CS, :], ones_r[:, 0:HEADS], start=True, stop=True)
                else:
                    c = bass.ds(i * CB + s, 1)
                    eng.matmul(bank[2 + o][:, 0:HEADS], E[:, s % CS, :], ex_hi[:, c, :].rearrange("p c h -> p (c h)"), start=True, stop=False)
                    last = eng.matmul(bank[2 + o][:, 0:HEADS], E[:, s % CS, :], ex_lo[:, c, :].rearrange("p c h -> p (c h)"), start=False, stop=True)
                last.then_inc(summed, 1)

            def carry(a):
                eng.wait_ge(out_main, CHUNKS * (a + 1))
                eng.wait_ge(out_extra, CHUNKS * (a + 1))
                eng.wait_ge(lr_in, 16 * (a + 1))
                eng.matmul(bank[0][0:CHUNKS, 0:D], carry_m[:, :], lr[:, 0:D], start=True, stop=True).then_inc(carried, 1)
                eng.matmul(bank[2][0:CHUNKS, 0:HEADS], carry_m[:, :], lr[:, D:AW], start=True, stop=True).then_inc(carried, 1)
                eng.wait_ge(fixed, 2 * (a + 1))

            def transpose4(into, tile):
                for k in range(KC):
                    last = eng.transpose(into[:, k * P:(k + 1) * P], tile[:, k * P:(k + 1) * P], ident[:, :])
                return last

            def product3(into, terms):
                step, steps = 0, len(terms) * KC * 3
                for hi, lo, w in terms:
                    for k in range(KC):
                        b = slice(k * P, (k + 1) * P)
                        for left, right in ((hi, whi), (hi, wlo), (lo, whi)):
                            last = eng.matmul(into, left[:, b], right[:, w, k, :], start=step == 0, stop=step == steps - 1)
                            step += 1
                return last

            for l in range(LAYERS):
                eng.wait_ge(w_hi, 2 * l + 1)
                eng.wait_ge(w_lo, 2 * l + 1)

                def z_transposes(i, s):
                    g = (l * TT + i) * TS + s
                    wait(eng, z_lo, g - 1)
                    eng.wait_ge(z_in[s % 4], 16 * (2 * (l * TT + i) + s // 4 + 1))
                    transpose4(bank[4 + s % 2], zx[:, s % 4, :]).then_inc(z_tp, 1)

                def z_products(i, s):
                    g = (l * TT + i) * TS + s
                    o = s % 2
                    wait(eng, z_ev, g - 1)
                    eng.wait_ge(z_lo, g + 1)
                    product3(bank[6 + o][:, :], [(zhi[:, o, :], zlo[:, o, :], 1)]).then_inc(z_mm, 1)

                in_turns(eng, 4, [(lambda i, s: segment_sums(l, i, s), 1, 3), (z_transposes, 0, 2), (z_products, 2, 2)])
                carry(l)
                eng.wait_ge(w_hi, 2 * l + 2)
                eng.wait_ge(w_lo, 2 * l + 2)

                def transposes(i, s):
                    g = (l * TT + i) * TS + s
                    o = s % 2
                    wait(eng, nlo, g - 1)
                    eng.wait_ge(an_done, g + 1)
                    transpose4(bank[2 + o], an[:, o, :]).then_inc(tposed, 1)

                def products(i, s):
                    g = (l * TT + i) * TS + s
                    o = s % 2
                    wait(eng, h_done, g - 1)
                    eng.wait_ge(nlo, g + 1)
                    product3(bank[o][:, :], [(ahi[:, o, :], alo[:, o, :], 0)]).then_inc(mm_done, 1)

                in_turns(eng, TS, [(transposes, 2), (products, 4)])

            eng.wait_ge(w_hi, 2 * LAYERS + 2)
            eng.wait_ge(w_lo, 2 * LAYERS + 2)

            def a_transposes(i, s):
                g = A0 + i * TS + s
                wait(eng, nlo, g - 1)
                eng.wait_ge(nrm, g + 1)
                transpose4(bank[s % 2], a_h[:, s % 4, :]).then_inc(tposed, 1)

            def a_products(i, s):
                g = i * TS + s
                o = s % 2
                eng.wait_ge(nlo, A0 + g + 1)
                wait(eng, q_ev, g - 1)
                product3(bank[2 + o][:, :], [(a_hi[:, o, :], a_lo[:, o, :], 0)])
                wait(eng, k_ev, g - 1)
                product3(bank[4 + o][:, :], [(a_hi[:, o, :], a_lo[:, o, :], 1)]).then_inc(mm_done, 1)

            in_turns(eng, TS, [(a_transposes, 3), (a_products, 5)])

            eng.wait_ge(w_lo, 2 * LAYERS + 3)
            eng.wait_ge(k_ev, TILES)
            eng.wait_ge(q_ev, TILES)

            def v_transposes(i, s):
                g = i * TS + s
                wait(eng, v_lod, g - 1)
                eng.wait_ge(ring8[s], 16 * (i + 1))
                transpose4(bank[s % 2], v_h[:, s, :]).then_inc(v_tp, 1)

            def v_products(i, s):
                g = i * TS + s
                wait(eng, v_out, g - 1)
                eng.wait_ge(v_lod, g + 1)
                product3(bank[2 + s % 2][:, :], [(v_hi[:, s % 2, :], v_lo[:, s % 2, :], 0)]).then_inc(v_mm, 1)

            in_turns(eng, TS, [(v_transposes, 0), (v_products, 2)])

            eng.wait_ge(b_red, CHUNKS)
            for n in range(HEADS):
                eng.transpose(bank[4 + n // 4][0:CHUNKS, (n % 4) * P:(n % 4 + 1) * P], e_all[:, :, n],
                              ident[:, :]).then_inc(m_pe, 1)
            eng.wait_ge(m_step, 22)
            for n in range(HEADS):
                eng.transpose(bank[6 + n // 4][:, (n % 4) * CHUNKS:(n % 4 + 1) * CHUNKS], m_e[:, n, :],
                              ident[0:CHUNKS, 0:CHUNKS]).then_inc(m_pe, 1)
            eng.wait_ge(m_step, 24)
            eng.wait_ge(ex_split, 1)

            in_turns(eng, CB, [(lambda i, s: segment_sums(3, i, s), 0)])
            carry(3)

            eng.wait_ge(w_hi, 2 * LAYERS + 4)
            eng.wait_ge(w_lo, 2 * LAYERS + 4)
            eng.wait_ge(r_in, 16 * (2 * LAYERS + 8))

            def d_transposes(i, s):
                g = i * TS + s
                wait(eng, nlo, D0 + g - 1)
                eng.wait_ge(an_done, A0 + g + 1)
                transpose4(bank[s % 2], d_n[:, s % 2, :]).then_inc(tposed, 1)

            def d_products(i, s):
                g = i * TS + s
                o = s % 2
                wait(eng, h_done, A0 + g - 1)
                eng.wait_ge(nlo, D0 + g + 1)
                product3(bank[2 + o][:, :], [(d_hi[:, o, :], d_lo[:, o, :], 0)]).then_inc(mm_done, 1)

            def f_transposes(i, s):
                g = i * TS + s
                wait(eng, f_t, g)
                eng.wait_ge(g_add, A0 + g + 1)
                transpose4(bank[4], d_y[:, s, :]).then_inc(f_tp, 1)

            def f_first(i, s):
                g = i * TS + s
                wait(eng, f_r, g)
                eng.wait_ge(f_t, g + 1)
                for k in range(KC):
                    last = eng.matmul(bank[5][0:DFF, 0:P], w1[:, k, :], d_yt[:, s % 2, k * P:(k + 1) * P],
                                      start=k == 0, stop=k == KC - 1)
                last.then_inc(f_1, 1)

            def f_second(i, s):
                g = i * TS + s
                wait(eng, s2_done, g - 1)
                eng.matmul(bank[6 + s % 2][:, :], ones_r[0:1, :], b2_hi[:, :], start=True, stop=False)
                eng.matmul(bank[6 + s % 2][:, :], ones_r[0:1, :], b2_lo[:, :], start=False, stop=False)
                eng.wait_ge(f_r, g + 1)
                eng.matmul(bank[6 + s % 2][:, :], d_f[:, s % 2, :], w2[:, :], start=False, stop=True).then_inc(f_2, 1)

            eng.wait_ge(b2_split, 2)
            in_turns(eng, TS, [(f_second, 12), (d_transposes, 2), (d_products, 4), (f_first, 10), (f_transposes, 8)])

        @block.scalar
        def _(eng):
            eng.wait_ge(eps_set, 1)
            def split_hi(a, i, s):
                g = (a * TT + i) * CB + s
                if a == 3:
                    eng.wait_ge(gx_done, i * CB + s + 1)
                else:
                    eng.wait_ge(gathered[s % CS], 16 * ((a * TT + i) * CU + s // CS + 1))
                wait(eng, summed, g - 3)
                eng.activation(Ghi[:, s % CS, :], (Gx if a == 3 else G)[:, s % CS, :], ACT.Copy).then_inc(hi_done, 1)

            def take_sums(a, i, s):
                g = (a * TT + i) * CB + s
                eng.wait_ge(summed, g + 1)
                wait(eng, scattered[s % CS], 16 * ((a * TT + i) * CU + s // CS))
                wait(eng, lrow_out[s % CS], 16 * ((a * TT + i) * CU + s // CS))
                eng.activation(O[:, s % CS, 0:D], bank[s % 2][:, 0:D], ACT.Copy).then_inc(out_main, 1)

            def deviation(i, s, sems, base, sd_t, mv_t, n):
                eng.wait_ge(sems[1], base + i * TS + s + 1)
                eng.activation(sd_t[:, n, 0:1], mv_t[:, n, 1:2], ACT.Sqrt, bias=eps[:, 0:1]).then_inc(sems[3], 1)

            for l in range(LAYERS):
                eng.wait_ge(b_in, 32 * (l + 1))
                eng.activation(whi[:, 1], wraw[:, 1], ACT.Copy).then_inc(w_hi, 1)

                def z_split(i, s):
                    g = (l * TT + i) * TS + s
                    eng.wait_ge(z_tp, g + 1)
                    wait(eng, z_mm, g - 1)
                    eng.activation(zhi[:, s % 2, :], bank[4 + s % 2][:, :], ACT.Copy).then_inc(z_hi, 1)

                in_turns(eng, 4, [(lambda i, s: split_hi(l, i, s), 0, 3), (z_split, 1, 2),
                                  (lambda i, s: take_sums(l, i, s), 2, 3)])
                eng.wait_ge(w_in, 16 * (l + 1))
                eng.activation(whi[:, 0], wraw[:, 0], ACT.Copy).then_inc(w_hi, 1)

                def mean(i, s):
                    g = (l * TT + i) * TS + s
                    if l == 0:
                        eng.wait_ge(inv_done, g + 1)
                    eng.wait_ge(ring4[s % 4], 16 * (2 * (l * TT + i) + s // 4 + 1))
                    wait(eng, tposed, g - 1)
                    eng.activation(an[:, s % 2, :], ain[:, s % 4, 0:D], ACT.Copy, scale=inv_n[:, bass.ds(i * TS + s, 1)]).then_inc(an_done, 1)

                def split_nodes(i, s):
                    g = (l * TT + i) * TS + s
                    o = s % 2
                    eng.wait_ge(tposed, g + 1)
                    wait(eng, mm_done, g - 1)
                    eng.activation(ahi[:, o, :], bank[2 + o][:, :], ACT.Copy).then_inc(nhi, 1)

                def normalise(i, s):
                    g = (l * TT + i) * TS + s
                    o = s % 2
                    eng.wait_ge(rs_done, g + 1)
                    wait(eng, y_done, g - 3)
                    eng.activation(hn[:, s % 4, :], h[:, o, :], ACT.Identity, bias=sd[:, o, 2:3],
                                   scale=sd[:, o, 1:2]).then_inc(nrm, 1)

                in_turns(eng, TS, [(split_nodes, 3), (mean, 1), (normalise, 6),
                                   (lambda i, s: deviation(i, s, ln1, l * TILES, sd, mv, s % 2), 5)])

            eng.wait_ge(w_in, 16 * (LAYERS + 2))
            for w in range(2):
                eng.activation(whi[:, w], wraw[:, w], ACT.Copy).then_inc(w_hi, 1)

            def a_normalise(i, s):
                g = i * TS + s
                eng.wait_ge(rs_done, A0 + g + 1)
                wait(eng, tposed, A0 + g - 3)
                wait(eng, h_out[s % 4], 16 * (2 * i + s // 4))
                eng.activation(a_h[:, s % 4, :], a_sum[:, s % 4, :], ACT.Identity, bias=a_sd[:, s % 2, 2:3],
                               scale=a_sd[:, s % 2, 1:2]).then_inc(nrm, 1)

            def a_split(i, s):
                g = A0 + i * TS + s
                eng.wait_ge(tposed, g + 1)
                wait(eng, mm_done, g - 1)
                eng.activation(a_hi[:, s % 2, :], bank[s % 2][:, :], ACT.Copy).then_inc(nhi, 1)

            def take_q(i, s):
                g = i * TS + s
                eng.wait_ge(mm_done, A0 + g + 1)
                wait(eng, qk_out[s % 4], 32 * (2 * i + s // 4))
                eng.activation(a_q[:, s % 4, :], bank[2 + s % 2][:, :], ACT.Copy).then_inc(q_ev, 1)

            in_turns(eng, TS, [(a_split, 4), (take_q, 6), (a_normalise, 2),
                                   (lambda i, s: deviation(i, s, ln1, A0, a_sd, a_mv, s % 2), 1)])

            eng.wait_ge(w_in, 16 * (LAYERS + 3))
            eng.wait_ge(mm_done, D0)
            eng.activation(whi[:, 0], wraw[:, 0], ACT.Copy).then_inc(w_hi, 1)

            def v_split(i, s):
                g = i * TS + s
                eng.wait_ge(v_tp, g + 1)
                wait(eng, v_mm, g - 1)
                eng.activation(v_hi[:, s % 2, :], bank[s % 2][:, :], ACT.Copy).then_inc(v_hid, 1)

            def v_finish(i, s):
                eng.wait_ge(v_mm, i * TS + s + 1)
                wait(eng, store4[s % 4], 16 * (ST_V + 2 * i + s // 4))
                eng.activation(v_o[:, s % 4, :], bank[2 + s % 2][:, :], ACT.Copy).then_inc(v_out, 1)

            in_turns(eng, TS, [(v_split, 1), (v_finish, 3)])

            eng.wait_ge(m_step, 24)
            eng.activation(ex[:, :, :], e_all[:, :, :], ACT.Exp, scale=1.0 / DK ** 0.5).then_inc(m_act, 1)
            eng.wait_ge(m_act, 1)
            eng.activation(ex_hi[:, :, :], ex[:, :, :], ACT.Copy).then_inc(m_act, 1)
            in_turns(eng, CB, [(lambda i, s: split_hi(3, i, s), 0), (lambda i, s: take_sums(3, i, s), 2 - 1)])
            eng.wait_ge(w_in, 16 * (LAYERS + 4))
            eng.wait_ge(fix_out, 16 * 4)
            eng.wait_ge(r_in, 16 * (2 * LAYERS + 8))
            eng.activation(whi[:, 0], wraw[:, 0], ACT.Copy).then_inc(w_hi, 1)

            def d_split(i, s):
                g = D0 + i * TS + s
                eng.wait_ge(tposed, g + 1)
                wait(eng, mm_done, g - 1)
                eng.activation(d_hi[:, s % 2, :], bank[s % 2][:, :], ACT.Copy).then_inc(nhi, 1)

            def d_norm1(i, s):
                g = i * TS + s
                eng.wait_ge(rs_done, D0 + g + 1)
                wait(eng, s2_done, g - 7)
                eng.activation(d_y[:, s, :], d_s1[:, s % 2, :], ACT.Identity, bias=d_sd[:, s % 2, 2:3],
                               scale=d_sd[:, s % 2, 1:2]).then_inc(nrm, 1)

            def f_take(i, s):
                g = i * TS + s
                eng.wait_ge(f_tp, g + 1)
                wait(eng, f_1, g - 1)
                eng.activation(d_yt[:, s % 2, :], bank[4][:, :], ACT.Copy).then_inc(f_t, 1)

            def f_relu(i, s):
                g = i * TS + s
                eng.wait_ge(f_1, g + 1)
                wait(eng, f_2, g - 1)
                eng.activation(d_f[:, s % 2, :], bank[5][0:DFF, 0:P], ACT.Relu, bias=b1c[:, 0:1]).then_inc(f_r, 1)

            def d_norm2(i, s):
                g = i * TS + s
                eng.wait_ge(ln2[5], g + 1)
                wait(eng, s3_done, g - 3)
                eng.activation(d_n2[:, s % 4, :], d_s2[:, s % 2, :], ACT.Identity, bias=d_sd[:, 2 + s % 2, 2:3],
                               scale=d_sd[:, 2 + s % 2, 1:2]).then_inc(nrm2, 1)

            def d_norm3(i, s):
                g = i * TS + s
                eng.wait_ge(ln3[5], g + 1)
                wait(eng, store4[s % 4], 16 * (ST_D + 2 * i + s // 4))
                eng.activation(d_o[:, s % 4, :], d_s3[:, s % 2, :], ACT.Identity, bias=d_sd[:, 4 + s % 2, 2:3],
                               scale=d_sd[:, 4 + s % 2, 1:2]).then_inc(o_done, 1)

            eng.activation(b2_hi[:, :], rows_bc[0:1, 4, :], ACT.Copy).then_inc(b2_split, 1)
            in_turns(eng, TS, [
                (f_take, 9), (f_relu, 11), (d_split, 3), (d_norm1, 6), (d_norm2, 14), (d_norm3, 17),
                (lambda i, s: deviation(i, s, ln1, D0, d_sd, d_mv, s % 2), 5),
                (lambda i, s: deviation(i, s, ln2, 0, d_sd, d_mv, 2 + s % 2), 13),
                (lambda i, s: deviation(i, s, ln3, 0, d_sd, d_mv, 4 + s % 2), 16)])

        @block.vector
        def _(eng):
            eng.memset(eps[:, :], EPS).then_inc(eps_set, 1)
            eng.wait_ge(idx_in, 16 * 7)
            eng.tensor_copy(dst_f[:, :], dst_i[:, :]).then_inc(tables, 1)
            eng.tensor_tensor(same[:, :], dst_i[:, :], nxt_i[:, :], ALU.is_equal).then_inc(tables, 1)
            eng.tensor_copy(ends_f[:, :], ends_i[:, :]).then_inc(tables, 1)
            eng.wait_ge(tables, 3)
            eng.scalar_tensor_tensor(out=put_i[:, :], in0=same[:, :], scalar=float(SKIP), in1=dst_f[:, :],
                                     op0=ALU.mult, op1=ALU.add).then_inc(tables, 1)
            eng.tensor_tensor(fixt[:, 0:1], ends_f[:, 0:1], ends_f[:, 2:3], ALU.is_equal).then_inc(m_step, 1)
            eng.tensor_tensor(fixt[:, 1:2], ends_f[:, 0:1], ends_f[:, 3:4], ALU.is_equal).then_inc(m_step, 1)
            eng.wait_ge(m_step, 2)
            eng.scalar_tensor_tensor(out=fixt[:, 1:2], in0=fixt[:, 1:2], scalar=-1.0, in1=fixt[:, 0:1],
                                     op0=ALU.add, op1=ALU.mult).then_inc(m_step, 1)
            eng.wait_ge(m_step, 3)
            eng.tensor_scalar(fixt[:, 0:1], fixt[:, 1:2], float(SKIP), float(SKIP), ALU.mult, ALU.add).then_inc(m_step, 1)
            eng.wait_ge(m_step, 4)
            eng.tensor_tensor(fix_i[:, :], fixt[:, 0:1], ends_f[:, 0:1], ALU.add).then_inc(tables, 1)
            eng.tensor_scalar(carry_m[:, :], first_bc[:, :], ends_f[:, 1:2], None, ALU.is_equal).then_inc(tables, 1)
            eng.tensor_scalar(back_m[:, :], last_bc[:, :], ends_f[:, 0:1], None, ALU.is_equal).then_inc(tables, 1)
            eng.wait_ge(prep, 3)
            eng.tensor_copy(ones_r[:, :], onesf[:, :]).then_inc(m_step, 1)

            def weights_lo(n, halves):
                for k, w in enumerate(halves):
                    eng.wait_ge(w_hi, n + k + 1)
                    eng.tensor_tensor(wlo[:, w], wraw[:, w], whi[:, w].bitcast(F32), ALU.subtract).then_inc(w_lo, 1)

            def equal_edges(a, i, s):
                g = (a * TT + i) * CB + s
                c = i * CB + s
                wait(eng, summed, g - 3)
                eng.tensor_scalar(E[:, s % CS, :], dst_bc[:, bass.ds(c * P, P)], dst_f[:, bass.ds(c, 1)], None,
                                  ALU.is_equal).then_inc(eq_done, 1)

            def weigh(i, s):
                c = i * CB + s
                eng.wait_ge(gathered[s % CS], 16 * ((3 * TT + i) * CU + s // CS + 1))
                wait(eng, lo_done, 3 * CHUNKS + c - 3)
                eng.tensor_tensor(Gx[:, s % CS, :].rearrange("p (h d) -> p h d", h=HEADS),
                                  G[:, s % CS, :].rearrange("p (h d) -> p h d", h=HEADS),
                                  ex[:, bass.ds(c, 1), :].rearrange("p c h -> p (c h)").unsqueeze(2).broadcast_to([P, HEADS, DK]),
                                  ALU.mult).then_inc(gx_done, 1)

            def split_lo(a, i, s):
                g = (a * TT + i) * CB + s
                eng.wait_ge(hi_done, g + 1)
                eng.tensor_tensor(Glo[:, s % CS, :], (Gx if a == 3 else G)[:, s % CS, :], Ghi[:, s % CS, :].bitcast(F32),
                                  ALU.subtract).then_inc(lo_done, 1)

            def take_extra(a, i, s):
                g = (a * TT + i) * CB + s
                eng.wait_ge(summed, g + 1)
                wait(eng, scattered[s % CS], 16 * ((a * TT + i) * CU + s // CS))
                wait(eng, lrow_out[s % CS], 16 * ((a * TT + i) * CU + s // CS))
                eng.tensor_copy(O[:, s % CS, D:AW], bank[2 + s % 2][:, 0:HEADS]).then_inc(out_extra, 1)

            def fix(a):
                eng.wait_ge(fix_in, 16 * (a + 1))
                eng.wait_ge(carried, 2 * (a + 1))
                eng.tensor_tensor(fy[:, 0:D], fx[:, 0:D], bank[0][0:CHUNKS, 0:D], ALU.add).then_inc(fixed, 1)
                eng.tensor_tensor(fy[:, D:AW], fx[:, D:AW], bank[2][0:CHUNKS, 0:HEADS], ALU.add).then_inc(fixed, 1)

            def norm_steps(base, sems, tile, st_t, mv_t, sd_t):
                def moments(i, s):
                    eng.bn_stats(st_t(s), tile(s)).then_inc(sems[0], 1)

                def mean_variance(i, s):
                    eng.wait_ge(sems[0], base + i * TS + s + 1)
                    eng.sem_inc(dve_go, 1)
                    eng.bn_aggr(mv_t(s), st_t(s)).then_inc(sems[1], 1)

                def invert(i, s):
                    eng.wait_ge(sems[3], base + i * TS + s + 1)
                    eng.reciprocal(sd_t(s)[:, 1:2], sd_t(s)[:, 0:1]).then_inc(sems[4], 1)

                def shift(i, s):
                    eng.wait_ge(sems[4], base + i * TS + s + 1)
                    eng.tensor_scalar(sd_t(s)[:, 2:3], mv_t(s)[:, 0:1], sd_t(s)[:, 1:2], -1.0, ALU.mult, ALU.mult).then_inc(sems[5], 1)

                return moments, mean_variance, invert, shift

            for l in range(LAYERS):
                weights_lo(2 * l, (1,))

                def z_split_lo(i, s):
                    eng.wait_ge(z_hi, (l * TT + i) * TS + s + 1)
                    eng.tensor_tensor(zlo[:, s % 2, :], bank[4 + s % 2][:, :], zhi[:, s % 2, :].bitcast(F32), ALU.subtract).then_inc(z_lo, 1)

                def z_take(i, s):
                    g = (l * TT + i) * TS + s
                    eng.wait_ge(z_mm, g + 1)
                    wait(eng, z_out[s % 4], 16 * (2 * (l * TT + i) + s // 4))
                    eng.tensor_tensor(zo[:, s % 4, :], bank[6 + s % 2][:, :], rows_bc[:, 0, :], ALU.add).then_inc(z_ev, 1)

                eng.wait_ge(b_in, 32 * (l + 1))
                in_turns(eng, 4, [(lambda i, s: equal_edges(l, i, s), 0, 3), (z_take, 3, 2),
                                  (lambda i, s: split_lo(l, i, s), 0, 3), (lambda i, s: take_extra(l, i, s), 2, 3),
                                  (z_split_lo, 1, 2)])
                fix(l)
                weights_lo(2 * l + 1, (0,))
                eng.wait_ge(r_in, 16 * 2 * (l + 1))

                def inverse_count(i, s):
                    g = i * TS + s
                    eng.wait_ge(ring4[s % 4], 16 * (2 * i + s // 4 + 1))
                    o = s % 2
                    wait(eng, inv_done, g - 1)
                    eng.tensor_scalar(inv[:, o:o + 1], ain[:, s % 4, D:D + 1], 1.0, None, ALU.max).then_inc(inv_max, 1)
                    eng.wait_ge(inv_max, g + 1)
                    eng.reciprocal(inv_n[:, bass.ds(g, 1)], inv[:, o:o + 1]).then_inc(inv_done, 1)

                def split_nodes_lo(i, s):
                    g = (l * TT + i) * TS + s
                    o = s % 2
                    eng.wait_ge(nhi, g + 1)
                    eng.tensor_tensor(alo[:, o, :], bank[2 + o][:, :], ahi[:, o, :].bitcast(F32), ALU.subtract).then_inc(nlo, 1)

                def add_right(i, s):
                    g = (l * TT + i) * TS + s
                    o = s % 2
                    eng.wait_ge(mm_done, g + 1)
                    eng.wait_ge(zr_in[s % 4], 16 * (2 * (l * TT + i) + s // 4 + 1))
                    wait(eng, nrm, g - 1)
                    eng.tensor_tensor(h[:, o, :], bank[o][:, :], zin[:, s % 4, :], ALU.add).then_inc(h_done, 1)

                moments, mean_variance, invert, shift = norm_steps(
                    l * TILES, ln1, lambda s: h[:, s % 2, :], lambda s: st[:, s % 2, :],
                    lambda s: mv[:, s % 2, :], lambda s: sd[:, s % 2, :])

                def moments_of_sum(i, s):
                    eng.wait_ge(h_done, (l * TT + i) * TS + s + 1)
                    moments(i, s)

                def residual(i, s):
                    g = (l * TT + i) * TS + s
                    eng.wait_ge(g_add, g + 1)
                    eng.wait_ge(xr_in[s % 4], 16 * (2 * (l * TT + i) + s // 4 + 1))
                    wait(eng, store4[s % 4], 16 * (2 * (l * TT + i) + s // 4))
                    eng.scalar_tensor_tensor(out=y[:, s % 4, :], in0=hn[:, s % 4, :], scalar=0.0, in1=xin[:, s % 4, :],
                                             op0=ALU.max, op1=ALU.add).then_inc(y_done, 1)

                in_turns(eng, TS, [(invert, 6), (add_right, 5), (shift, 6), (moments_of_sum, 5), (residual, 8)]
                         + [(inverse_count, 0)] * (l == 0) + [(mean_variance, 5), (split_nodes_lo, 3)])

            weights_lo(2 * LAYERS, (0, 1))

            moments, mean_variance, invert, shift = norm_steps(
                A0, ln1, lambda s: a_sum[:, s % 4, :], lambda s: a_st[:, s % 2, :],
                lambda s: a_mv[:, s % 2, :], lambda s: a_sd[:, s % 2, :])

            def a_moments(i, s):
                eng.wait_ge(a_add, i * TS + s + 1)
                moments(i, s)

            def a_split_lo(i, s):
                g = A0 + i * TS + s
                eng.wait_ge(nhi, g + 1)
                eng.tensor_tensor(a_lo[:, s % 2, :], bank[s % 2][:, :], a_hi[:, s % 2, :].bitcast(F32), ALU.subtract).then_inc(nlo, 1)

            def take_k(i, s):
                g = i * TS + s
                eng.wait_ge(mm_done, A0 + g + 1)
                wait(eng, qk_out[s % 4], 32 * (2 * i + s // 4))
                eng.tensor_copy(a_k[:, s % 4, :], bank[4 + s % 2][:, :]).then_inc(k_ev, 1)

            in_turns(eng, TS, [(invert, 2), (take_k, 6), (shift, 2), (a_moments, 1), (mean_variance, 1), (a_split_lo, 4)])

            def score(i, s):
                g = i * CB + s
                eng.wait_ge(kq_in[s % CS], 32 * (CU * i + s // CS + 1))
                eng.tensor_tensor(b_kq[:, s % 2, :], b_k[:, s % CS, :], b_q[:, s % CS, :], ALU.mult).then_inc(b_mul, 1)
                eng.wait_ge(b_mul, g + 1)
                eng.sem_inc(dve_go, 1)
                eng.tensor_reduce(e_all[:, bass.ds(g, 1), :].rearrange("p c h -> p (c h)"),
                                  b_kq[:, s % 2, :].rearrange("p (h d) -> p h d", h=HEADS), AX.X, ALU.add).then_inc(b_red, 1)

            def v_split_lo(i, s):
                eng.wait_ge(v_hid, i * TS + s + 1)
                eng.tensor_tensor(v_lo[:, s % 2, :], bank[s % 2][:, :], v_hi[:, s % 2, :].bitcast(F32), ALU.subtract).then_inc(v_lod, 1)

            weights_lo(2 * LAYERS + 2, (0,))
            in_turns(eng, 4, [(score, 0, 3), (v_split_lo, 1, 2)])

            eng.wait_ge(v_mm, TILES)
            eng.memset(m_row[:, :, :], 0.0).then_inc(m_step, 1)
            eng.wait_ge(m_step, 6)
            eng.tensor_tensor(m_row[:, 0, 1:P], drow[:, 1:P], drow[:, 0:P - 1], ALU.is_equal)
            eng.tensor_tensor(m_row[:, 1, 0:P - 1], drow[:, 1:P], drow[:, 0:P - 1], ALU.is_equal).then_inc(m_step, 1)
            eng.wait_ge(m_step, 7)
            for k, tile in enumerate((m_new, m_end)):
                eng.tensor_scalar(tile[:, :, :], m_row[:, k:k + 1, :].broadcast_to([CHUNKS, HEADS, P]), -1.0, FAR, ALU.add, ALU.mult)
            for k, tile in enumerate((m_first, m_last)):
                eng.tensor_scalar(m_t[:, k, :], drow[:, :], ends_f[:, k:k + 1], None, ALU.is_equal).then_inc(m_step, 1)
                eng.wait_ge(m_step, 8 + k)
                eng.tensor_scalar(tile[:, :], m_t[:, k, :], -1.0, FAR, ALU.add, ALU.mult)
            eng.tensor_scalar(m_prev[:, :], back_m[:, :], -1.0, FAR, ALU.add, ALU.mult)
            eng.tensor_scalar(m_next[:, :], carry_m[:, :], -1.0, FAR, ALU.add, ALU.mult).then_inc(m_step, 1)
            eng.wait_ge(m_pe, HEADS)
            eng.tensor_copy(m_e[:, 0:4, :].rearrange("p h e -> p (h e)"), bank[4][0:CHUNKS, :])
            eng.tensor_copy(m_e[:, 4:8, :].rearrange("p h e -> p (h e)"), bank[5][0:CHUNKS, :]).then_inc(m_step, 1)
            eng.wait_ge(m_step, 11)
            flat = [x[:, :, :].rearrange("p h e -> p (h e)") for x in (m_new, m_e, m_f, m_end)]
            eng.tensor_tensor_scan(flat[2], flat[0], flat[1], -FAR, ALU.add, ALU.max).then_inc(m_step, 1)
            eng.wait_ge(m_step, 12)
            eng.tensor_tensor_scan(flat[1][:, ::-1], flat[3][:, ::-1], flat[2][:, ::-1], -FAR, ALU.add, ALU.max).then_inc(m_step, 1)
            eng.wait_ge(m_step, 13)
            eng.tensor_copy(m_ce[:, 0, :], m_f[:, :, P - 1])
            eng.tensor_copy(m_ce[:, 1, :], m_e[:, :, 0]).then_inc(m_step, 1)
            eng.wait_ge(ends_in, 16)
            for k, mask in enumerate((m_prev, m_next)):
                eng.tensor_tensor(m_ends[:, :, k], m_ends[:, :, k], mask[:, :].unsqueeze(2).broadcast_to([CHUNKS, CHUNKS, HEADS]),
                                  ALU.add).then_inc(m_step, 1)
                eng.wait_ge(m_step, 15 + 2 * k)
                eng.tensor_reduce(m_c[:, k, :], m_ends[:, :, k].rearrange("p c h -> p h c"), AX.X, ALU.max).then_inc(m_step, 1)
            eng.wait_ge(m_step, 18)
            for k, mask in enumerate((m_first, m_last)):
                eng.tensor_tensor(m_t[:, :, :], mask[:, :].unsqueeze(1).broadcast_to([CHUNKS, HEADS, P]),
                                  m_c[:, k, :].unsqueeze(2).broadcast_to([CHUNKS, HEADS, P]), ALU.add).then_inc(m_step, 1)
                eng.wait_ge(m_step, 19 + 2 * k)
                eng.tensor_tensor(m_e[:, :, :], m_e[:, :, :], m_t[:, :, :], ALU.max).then_inc(m_step, 1)
                eng.wait_ge(m_step, 20 + 2 * k)
            eng.wait_ge(m_pe, 2 * HEADS)
            for k in range(2):
                half = e_all[:, :, 4 * k:4 * k + 4].rearrange("p c h -> p h c")
                eng.tensor_tensor(half, half, bank[6 + k][:, 0:4 * CHUNKS].rearrange("p (h c) -> p h c", h=4), ALU.subtract).then_inc(m_step, 1)
            eng.wait_ge(m_act, 2)
            eng.tensor_tensor(ex_lo[:, :, :], ex[:, :, :], ex_hi[:, :, :].bitcast(F32), ALU.subtract).then_inc(ex_split, 1)
            in_turns(eng, CB, [(weigh, 0), (lambda i, s: equal_edges(3, i, s), 1), (lambda i, s: split_lo(3, i, s), 1),
                               (lambda i, s: take_extra(3, i, s), 2)])
            fix(3)
            eng.wait_ge(r_in, 16 * (2 * LAYERS + 8))
            weights_lo(2 * LAYERS + 3, (0,))
            eng.wait_ge(b2_split, 1)
            eng.tensor_tensor(b2_lo[:, :], rows_bc[0:1, 4, :], b2_hi[:, :].bitcast(F32), ALU.subtract).then_inc(b2_split, 1)

            def inverse_weight(i, s):
                g = TILES + i * TS + s
                eng.wait_ge(ring4[s % 4], R4_D + 16 * (2 * i + s // 4 + 1))
                eng.tensor_scalar(d_z[:, s % 4, 0, :], d_a[:, s % 4, D:AW], 1e-30, None, ALU.max).then_inc(inv_max, 1)
                eng.wait_ge(inv_max, g + 1)
                eng.reciprocal(d_z[:, s % 4, 1, :], d_z[:, s % 4, 0, :]).then_inc(inv_done, 1)

            def d_split_lo(i, s):
                eng.wait_ge(nhi, D0 + i * TS + s + 1)
                eng.tensor_tensor(d_lo[:, s % 2, :], bank[s % 2][:, :], d_hi[:, s % 2, :].bitcast(F32), ALU.subtract).then_inc(nlo, 1)

            def add1(i, s):
                g = i * TS + s
                o = s % 2
                eng.wait_ge(mm_done, D0 + g + 1)
                eng.wait_ge(xr_in[s % 4], 16 * (XR_D + 2 * i + s // 4 + 1))
                wait(eng, nrm, D0 + g - 1)
                eng.tensor_tensor(d_s1[:, o, :], bank[2 + o][:, :], d_h[:, s % 4, :], ALU.add).then_inc(h_done, 1)

            def add2(i, s):
                g = i * TS + s
                o = s % 2
                eng.wait_ge(f_2, g + 1)
                wait(eng, nrm2, g - 1)
                eng.tensor_tensor(d_s2[:, o, :], bank[6 + o][:, :], d_y[:, s, :], ALU.add).then_inc(s2_done, 1)

            def add3(i, s):
                g = i * TS + s
                eng.wait_ge(g_add2, g + 1)
                eng.wait_ge(h2_in[s % 4], 16 * (2 * i + s // 4 + 1))
                wait(eng, o_done, g - 1)
                eng.tensor_tensor(d_s3[:, s % 2, :], d_n2[:, s % 4, :], d_h2[:, s % 4, :], ALU.add).then_inc(s3_done, 1)

            moments1, mean_variance1, invert1, shift1 = norm_steps(
                D0, ln1, lambda s: d_s1[:, s % 2, :], lambda s: d_st[:, s % 2, :],
                lambda s: d_mv[:, s % 2, :], lambda s: d_sd[:, s % 2, :])
            moments2, mean_variance2, invert2, shift2 = norm_steps(
                0, ln2, lambda s: d_s2[:, s % 2, :], lambda s: d_st[:, 2 + s % 2, :],
                lambda s: d_mv[:, 2 + s % 2, :], lambda s: d_sd[:, 2 + s % 2, :])
            moments3, mean_variance3, invert3, shift3 = norm_steps(
                0, ln3, lambda s: d_s3[:, s % 2, :], lambda s: d_st[:, 4 + s % 2, :],
                lambda s: d_mv[:, 4 + s % 2, :], lambda s: d_sd[:, 4 + s % 2, :])

            def moments_of_sum1(i, s):
                eng.wait_ge(h_done, A0 + i * TS + s + 1)
                moments1(i, s)

            def moments_of_sum2(i, s):
                eng.wait_ge(s2_done, i * TS + s + 1)
                moments2(i, s)

            def moments_of_sum3(i, s):
                eng.wait_ge(s3_done, i * TS + s + 1)
                moments3(i, s)

            in_turns(eng, TS, [
                (invert1, 6), (invert2, 14), (invert3, 17), (shift1, 6), (shift2, 14), (shift3, 17),
                (add1, 5), (add2, 13), (moments_of_sum1, 5), (add3, 16), (moments_of_sum2, 13), (mean_variance1, 5),
                (moments_of_sum3, 16), (mean_variance2, 13), (mean_variance3, 16), (inverse_weight, 0), (d_split_lo, 3)])


_SAME = ["L0_gnn_b", "L0_gnn_ln_g", "L0_gnn_ln_b", "L1_gnn_Wq", "L1_gnn_Wk", "L1_gnn_Wv", "L1_gnn_Wo",
         "L1_gnn_W1", "L1_gnn_W2"]
_ROWS = ["L1_gnn_ln1_g", "L1_gnn_ln1_b", "L1_gnn_ln2_g", "L1_gnn_ln2_b", "L1_gnn_b2"]


def kernel(**inputs):
    import concourse.bacc as bacc
    from concourse.bass_utils import run_bass_kernel_spmd

    a = {k: np.asarray(v) for k, v in inputs.items()}
    x = np.zeros((NP, D), np.float32)
    x[:NODES] = a["x"]
    src = np.zeros(EP, np.int32)
    src[:EDGES] = a["src"]
    dst = np.full(EP, NODES, np.int32)
    dst[:EDGES] = a["dst"]
    around = np.full(EP + 2, -1, np.int32)
    around[1:-1] = dst
    first = np.arange(CHUNKS) * P
    last = first + P - 1
    arrays = {
        "x": x,
        "src_cols": np.ascontiguousarray(src.reshape(CHUNKS, P).T),
        "dst_cols": np.ascontiguousarray(dst.reshape(CHUNKS, P).T),
        "next_cols": np.ascontiguousarray(around[2:].reshape(CHUNKS, P).T),
        "dst_rows": dst.reshape(CHUNKS, P),
        "dst_row": dst.reshape(1, EP),
        "first_row": np.ascontiguousarray(dst[first]).reshape(1, CHUNKS),
        "last_row": np.ascontiguousarray(dst[last]).reshape(1, CHUNKS),
        "ends": np.ascontiguousarray(np.stack([dst[first], dst[last], around[first], around[last + 2]], 1)),
        "L0_WlT": np.ascontiguousarray(a["L0_gnn_W_l"].transpose(0, 2, 1)),
        "L0_WrT": np.ascontiguousarray(a["L0_gnn_W_r"].transpose(0, 2, 1)),
        "b1_col": np.ascontiguousarray(a["L1_gnn_b1"]).reshape(DFF, 1),
    }
    for name in _SAME:
        arrays[name] = np.ascontiguousarray(a[name])
    for name in _ROWS:
        arrays[name] = np.ascontiguousarray(a[name]).reshape(1, D)
    nc = bacc.Bacc("TRN2", target_bir_lowering=False, num_devices=1)
    t = {n: nc.dram_tensor("in_" + n, v.shape, mybir.dt.from_np(v.dtype), kind="ExternalInput").ap()
         for n, v in arrays.items()}
    out = nc.dram_tensor("out", (NP, D), F32, kind="ExternalOutput").ap()
    build(nc, t, out)
    r = run_bass_kernel_spmd(nc, [{"in_" + n: v for n, v in arrays.items()}], core_ids=[0])
    return np.ascontiguousarray(r.results[0]["out"][:NODES])
```

```python
import numpy as np
import concourse.bass as bass
from concourse import mybir
from contextlib import ExitStack

F32 = mybir.dt.float32
F32R = mybir.dt.float32r
I32 = mybir.dt.int32
ALU = mybir.AluOpType
ACT = mybir.ActivationFunctionType
AX = mybir.AxisListType

P = 128
D = 512
KC = D // P
NODES, EDGES = 10000, 15000
LAYERS, HEADS, DFF = 3, 8, 64
DK = D // HEADS
TS, CB = 8, 12
CS = 6
HS = 3
QS = 6
CU = CB // CS
TT = max(-(-NODES // (P * TS)), -(-EDGES // (P * CB)))
TILES, CHUNKS = TT * TS, TT * CB
NP, EP = TILES * P, CHUNKS * P
AW = D + HEADS
SKIP = 1 << 15
EPS = 1e-5
AHEAD = 3
FAR = 1.0e38


def in_turns(eng, units, stages):
    stages = [(stage, lag, rate[0] if rate else 1) for stage, lag, *rate in stages]
    late = max(-(-lag // (units * rate)) for _, lag, rate in stages)

    def turn(i, guard):
        for unit in range(units):
            for j in range(max(rate for _, _, rate in stages)):
                for stage, lag, rate in stages:
                    at, item = divmod(unit * rate + j - lag, units * rate)
                    if j >= rate or (guard and not 0 <= i + at < TT):
                        continue
                    stage(i + at if guard or at else i, item)

    for i in range(1 + late):
        turn(i, True)
    with eng.Fori(1 + late, TT) as i:
        turn(i, False)
    for i in range(TT, TT + late):
        turn(i, True)


def wait(eng, semaphore, count):
    if not isinstance(count, int) or count > 0:
        eng.wait_ge(semaphore, count)


def build(nc, t, out):
    ctx = ExitStack()
    with ctx:
        def sem(name):
            return ctx.enter_context(nc.semaphore(name))

        def ring(name, n):
            return [sem(f"{name}{i}") for i in range(n)]

        def dram(name, shape, dt=F32):
            return nc.dram_tensor(name, shape, dt, kind="Internal").ap()

        xs = dram("xs", [NP, D])
        agg = dram("agg", [NP, AW])
        ends_s = dram("ends_s", [CHUNKS, 2, AW])
        hs = dram("hs", [NP, D])
        qs = dram("qs", [NP, D])
        ks = dram("ks", [NP, D])
        vs = dram("vs", [NP, D])
        zs = dram("zs", [NP, D])
        ends_m = dram("ends_m", [CHUNKS, 2 * HEADS])

        top = [nc.sbuf_base]

        def sb(name, shape, dt=F32):
            size = int(np.prod(shape[1:])) * mybir.dt.size(dt)
            top[0] = -(-top[0] // 32) * 32
            tensor = nc.alloc_sbuf_tensor_at(name, shape, dt, offset=top[0])
            top[0] += size
            return tensor

        ident = sb("ident", [P, P])
        dst_bc = sb("dst_bc", [P, EP], I32)
        src_i = sb("src_i", [P, CHUNKS], I32)
        dst_i = sb("dst_i", [P, CHUNKS], I32)
        dst_f = sb("dst_f", [P, CHUNKS])
        nxt_i = sb("nxt_i", [P, CHUNKS], I32)
        same = sb("same", [P, CHUNKS])
        put_i = sb("put_i", [P, CHUNKS], I32)
        get_now = sb("get_now", [P, CB], I32)
        get_now2 = sb("get_now2", [P, CB], I32)
        put_now = sb("put_now", [P, CB], I32)
        inv_n = sb("inv_n", [P, TILES])
        eps = sb("eps", [P, 1])
        ends_i = sb("ends_i", [CHUNKS, 4], I32)
        ends_f = sb("ends_f", [CHUNKS, 4])
        first_bc = sb("first_bc", [CHUNKS, CHUNKS], I32)
        last_bc = sb("last_bc", [CHUNKS, CHUNKS], I32)
        carry_m = sb("carry_m", [CHUNKS, CHUNKS])
        back_m = sb("back_m", [CHUNKS, CHUNKS])
        fixt = sb("fixt", [CHUNKS, 2])
        fix_i = sb("fix_i", [CHUNKS, 1], I32)
        ones_r = sb("ones_r", [P, HEADS], F32R)
        onesf = sb("onesf", [P, HEADS])
        drow = sb("drow", [CHUNKS, P], I32)
        e_all = sb("e_all", [P, CHUNKS, HEADS])
        shared = top[0]

        G = sb("G", [P, CS, D])
        Ghi = sb("Ghi", [P, HS, D], F32R)
        Glo = sb("Glo", [P, HS, D], F32R)
        E = sb("E", [P, HS, P], F32R)
        O = sb("O", [P, CS, AW])
        edges_end = top[0]
        es = sb("es", [CHUNKS, 2, AW])
        fy = sb("fy", [CHUNKS, AW])
        carries_end = top[0]
        top[0] = edges_end
        zx = sb("zx", [P, 4, D])
        zhi = sb("zhi", [P, 2, D], F32R)
        zlo = sb("zlo", [P, 2, D], F32R)
        zo = sb("zo", [P, 4, D])
        weights = shared + 66 * 1024
        assert top[0] <= weights

        top[0] = shared
        y = sb("y", [P, 4, D])
        hn = sb("hn", [P, 4, D])
        xin = sb("xin", [P, 4, D])
        ahi = sb("ahi", [P, 2, D], F32R)
        alo = sb("alo", [P, 2, D], F32R)
        h = sb("h", [P, 2, D])
        assert top[0] <= edges_end
        an = sb("an", [P, 2, D])
        ain = sb("ain", [P, 4, AW])
        zin = sb("zin", [P, 4, D])
        inv = sb("inv", [P, 2])
        st = sb("st", [P, 2, 6])
        mv = sb("mv", [P, 2, 2])
        sd = sb("sd", [P, 2, 3])
        assert top[0] <= weights, top
        top[0] = weights
        wraw = sb("wraw", [P, 2, KC, D])
        whi = sb("whi", [P, 2, KC, D], F32R)
        wlo = sb("wlo", [P, 2, KC, D], F32R)
        rows_bc = sb("rows_bc", [P, 5, D])
        rows_end = top[0]

        top[0] = shared
        a_q = sb("a_q", [P, 4, D])
        a_k = sb("a_k", [P, 4, D])
        a_h = sb("a_h", [P, 4, D])
        a_hi = sb("a_hi", [P, 2, D], F32R)
        a_lo = sb("a_lo", [P, 2, D], F32R)
        top[0] = max(top[0], edges_end)
        a_x3 = sb("a_x3", [P, 4, D])
        a_x0 = sb("a_x0", [P, 4, D])
        a_sum = sb("a_sum", [P, 4, D])
        a_st = sb("a_st", [P, 2, 6])
        a_mv = sb("a_mv", [P, 2, 2])
        a_sd = sb("a_sd", [P, 2, 3])
        assert top[0] <= weights

        top[0] = shared
        b_k = sb("b_k", [P, QS, D])
        b_q = sb("b_q", [P, QS, D])
        v_h = sb("v_h", [P, 4, D])
        b_kq = sb("b_kq", [P, 2, D])
        v_hi = sb("v_hi", [P, 2, D], F32R)
        v_lo = sb("v_lo", [P, 2, D], F32R)
        v_o = sb("v_o", [P, 4, D])
        values_end = top[0]
        top[0] = weights + 4 * KC * D * 2
        m_e = sb("m_e", [CHUNKS, HEADS, P])
        m_f = sb("m_f", [CHUNKS, HEADS, P])
        m_new = sb("m_new", [CHUNKS, HEADS, P])
        m_end = sb("m_end", [CHUNKS, HEADS, P])
        m_t = sb("m_t", [CHUNKS, HEADS, P])
        m_row = sb("m_row", [CHUNKS, 3, P])
        m_first = sb("m_first", [CHUNKS, P])
        m_last = sb("m_last", [CHUNKS, P])
        m_prev = sb("m_prev", [CHUNKS, CHUNKS])
        m_next = sb("m_next", [CHUNKS, CHUNKS])
        m_ends = sb("m_ends", [CHUNKS, CHUNKS, 2, HEADS])
        m_ce = sb("m_ce", [CHUNKS, 2, HEADS])
        m_c = sb("m_c", [CHUNKS, 2, HEADS])
        assert top[0] <= weights + 24 * KC * D
        top[0] = weights + 8 * KC * D
        Gx = sb("Gx", [P, CS, D])
        top[0] = max(carries_end, values_end)
        ex = sb("ex", [P, CHUNKS, HEADS])
        ex_hi = sb("ex_hi", [P, CHUNKS, HEADS], F32R)
        ex_lo = sb("ex_lo", [P, CHUNKS, HEADS], F32R)
        assert top[0] <= weights
        assert top[0] <= nc.sbuf_usable_end, (top, nc.sbuf_usable_end)

        top[0] = shared
        d_a = sb("d_a", [P, 4, AW])
        d_z = sb("d_z", [P, 4, 2, HEADS])
        d_h = sb("d_h", [P, 4, D])
        d_n = sb("d_n", [P, 2, D])
        d_hi = sb("d_hi", [P, 2, D], F32R)
        d_lo = sb("d_lo", [P, 2, D], F32R)
        d_s1 = sb("d_s1", [P, 2, D])
        d_y = sb("d_y", [P, TS, D])
        d_yt = sb("d_yt", [P, 2, D])
        d_f = sb("d_f", [DFF + 1, 2, P])
        d_st = sb("d_st", [P, 6, 6])
        d_mv = sb("d_mv", [P, 6, 2])
        d_sd = sb("d_sd", [P, 6, 3])
        d_n2 = sb("d_n2", [P, 4, D])
        d_end = top[0]
        top[0] = weights + 4 * KC * D
        d_s2 = sb("d_s2", [P, 2, D])
        assert top[0] <= weights + 8 * KC * D
        top[0] = weights + 12 * KC * D
        d_s3 = sb("d_s3", [P, 2, D])
        w1 = sb("w1", [P, KC, DFF])
        w2 = sb("w2", [DFF + 1, D])
        b1c = sb("b1c", [DFF, 1])
        b1s = sb("b1s", [DFF, 1])
        ln1_b = sb("ln1_b", [P, KC])
        assert top[0] <= weights + 16 * KC * D
        top[0] = weights + 20 * KC * D
        d_o = sb("d_o", [P, 4, D])
        assert top[0] <= weights + 24 * KC * D
        assert d_end <= weights, (d_end, weights)
        top[0] = rows_end
        d_h2 = sb("d_h2", [P, 4, D])
        top[0] = rows_end
        zero = sb("zero", [P, 4, AW])
        assert top[0] <= nc.sbuf_usable_end

        bank = [ctx.enter_context(nc.psum_tensor(f"bank{i}", [P, 512], F32)) for i in range(8)]

        idx_in, tables, zero_set, zeroed, prep = map(sem, ("idx_in", "tables", "zero_set", "zeroed", "prep"))
        src_in, eps_set, dst_bc_in, dst_bc_rest_in = map(sem, ("src_in", "eps_set", "dst_bc_in", "dst_bc_rest_in"))
        pool_go, dve_go = sem("pool_go"), sem("dve_go")
        weights_in, w_hi, w_lo = map(sem, ("weights_in", "w_hi", "w_lo"))
        vectors_in = sem("vectors_in")
        gathered, scattered, ends_saved = ring("gathered", CS), ring("scattered", CS), ring("ends_saved", CS)
        z_in, z_out, z_back_in = ring("z_in", 4), ring("z_out", 4), ring("z_back_in", 4)
        bias_in, z_transposed, z_hi, z_lo, z_products_done, z_taken, get_dst_rows_set = map(
            sem, ("bias_in", "z_transposed", "z_hi", "z_lo", "z_products_done", "z_taken", "get_dst_rows_set"))
        get_rows_set, put_rows_set, hi_done, lo_done, eq_done, summed, out_main, out_extra = map(
            sem, ("get_rows_set", "put_rows_set", "hi_done", "lo_done", "eq_done", "summed", "out_main", "out_extra"))
        ends_back, carried, fixed, fix_out = map(sem, ("ends_back", "carried", "fixed", "fix_out"))
        v_in, rows_in, rows_out = ring("v_in", 4), ring("rows_in", 4), ring("rows_out", 4)
        x_again_in = ring("x_again_in", 4)
        inv_max, inv_done, mean_done, transposed, rows_hi_done, rows_lo_done, products_done, h_done = map(
            sem, ("inv_max", "inv_done", "mean_done", "transposed", "rows_hi_done", "rows_lo_done", "products_done", "h_done"))
        moments_done, variance_done, sd_done, inverted, shift_done, normed, gained, offset_done, y_done = map(
            sem, ("moments_done", "variance_done", "sd_done", "inverted", "shift_done", "normed", "gained", "offset_done", "y_done"))
        h_out, qk_out = ring("h_out", 4), ring("qk_out", 4)
        a_add, q_taken, k_taken = map(sem, ("a_add", "q_taken", "k_taken"))
        kq_in = ring("kq_in", QS)
        v_transposed, v_hi_done, v_lo_done, v_products_done, v_taken, kq_multiplied, scores_done = map(sem, ("v_transposed", "v_hi_done", "v_lo_done", "v_products_done", "v_taken", "kq_multiplied", "scores_done"))
        m_step, m_transposed, exp_done, ends_out, ends_in = map(sem, ("m_step", "m_transposed", "exp_done", "ends_out", "ends_in"))
        weighed, ex_split, b2_sum, b1_mm, b1_sum = map(sem, ("weighed", "ex_split", "b2_sum", "b1_mm", "b1_sum"))
        f_transposed, f_copied, ffn1_done, relu_done, ffn2_done = map(sem, ("f_transposed", "f_copied", "ffn1_done", "relu_done", "ffn2_done"))
        s2_done, s3_done, o_done, normed2, gained2, offset2_done = map(
            sem, ("s2_done", "s3_done", "o_done", "normed2", "gained2", "offset2_done"))
        ln2 = [sem(f"ln2_{n}") for n in ("moments_done", "variance_done", "sd", "inverted", "rs")]
        ln3 = [sem(f"ln3_{n}") for n in ("moments_done", "variance_done", "sd", "inverted", "rs")]
        ln1 = [moments_done, variance_done, sd_done, inverted, shift_done]

        A0, D0 = LAYERS * TILES, (LAYERS + 1) * TILES
        XR_D = LAYERS * 2 * TT
        R4_A = LAYERS * 2 * TT * 16
        R4_D = R4_A + 2 * TT * 32
        ST_V, ST_D = LAYERS * 2 * TT, (LAYERS + 1) * 2 * TT

        def rows(i, s):
            return bass.ds((i * TS + s) * P, P)

        block = ctx.enter_context(nc.Block())

        @block.sync
        def _(eng):
            def save_ends(a, i, s):
                g = (a * TT + i) * CB + s
                eng.wait_ge(out_main, g + 1)
                eng.wait_ge(out_extra, g + 1)
                eng.dma_start(ends_s[bass.ds(i * CB + s, 1), :, :].rearrange("c k w -> (c k) w"), O[0:P:P - 1, s % CS, :]).then_inc(ends_saved[s % CS], 16)

            def carries(a):
                if a < LAYERS:
                    eng.wait_ge(z_lo, TILES * (a + 1))
                for s in range(CS):
                    eng.wait_ge(ends_saved[s], 16 * CU * TT * (a + 1))
                eng.dma_start(es[:, :, :], ends_s).then_inc(ends_back, 16)
                eng.wait_ge(fix_out, 16 * (a + 1))

            second = [t["L0_WrT"][l] for l in range(LAYERS)] + [t["L1_gnn_Wk"]]
            first = [t["L0_WlT"][l] for l in range(LAYERS)] + [t["L1_gnn_Wq"]]

            def load_weights(half, source):
                eng.dma_start(wraw[:, half], source.rearrange("(k p) n -> p k n", p=P)).then_inc(weights_in, 16)

            load_weights(1, second[0])
            load_weights(0, first[0])
            eng.dma_start(src_i[:, :], t["src_cols"]).then_inc(src_in, 16)
            for tile, name in ((dst_i, "dst_cols"), (nxt_i, "next_cols"), (ends_i, "ends"),
                               (drow, "dst_rows")):
                eng.dma_start(tile[:, :], t[name]).then_inc(idx_in, 16)
            eng.dma_start(first_bc[:, :], t["first_row"].broadcast_to([CHUNKS, CHUNKS])).then_inc(idx_in, 16)
            eng.dma_start(last_bc[:, :], t["last_row"].broadcast_to([CHUNKS, CHUNKS])).then_inc(idx_in, 16)
            for l in range(LAYERS):
                x_now = t["x"] if l == 0 else xs
                eng.dma_start(rows_bc[:, 0], t["L0_gnn_b"][l:l + 1, :].broadcast_to([P, D])).then_inc(bias_in, 16)
                eng.wait_ge(w_lo, 2 * l + 1)
                load_weights(1, second[l + 1])
                wait(eng, transposed, l * TILES)

                def z_load(i, s):
                    g = (l * TT + i) * TS + s
                    wait(eng, z_transposed if l else z_lo, g - 3 - (TILES if l else 0))
                    if l:
                        eng.wait_ge(rows_out[s % 4], 16 * (2 * ((l - 1) * TT + i) + s // 4 + 1))
                    eng.dma_start(zx[:, s % 4, :], (xs if l else t["x_blocks"])[rows(i, s), :]).then_inc(z_in[s % 4], 16)

                def z_store(i, s):
                    eng.wait_ge(z_taken, (l * TT + i) * TS + s + 1)
                    eng.dma_start(zs[rows(i, s), :], zo[:, s % 4, :]).then_inc(z_out[s % 4], 16)

                in_turns(eng, 4, [(lambda i, s: save_ends(l, i, s), 6 + AHEAD, 3), (z_load, 0, 2), (z_store, 7, 2)])
                for k, name in ((1, "L0_gnn_ln_g"), (2, "L0_gnn_ln_b")):
                    eng.dma_start(rows_bc[:, k], t[name][l:l + 1, :].broadcast_to([P, D])).then_inc(vectors_in, 16)
                carries(l)
                for s in range(4):
                    eng.wait_ge(z_out[s], 16 * 2 * TT * (l + 1))
                eng.wait_ge(w_lo, 2 * l + 2)
                load_weights(0, first[l + 1])

                def load(i, s):
                    g = (l * TT + i) * TS + s
                    wait(eng, mean_done, g - 3)
                    eng.dma_start(ain[:, s % 4, :], agg[rows(i, s), :]).then_inc(rows_in[s % 4], 16)

                def load_x(i, s):
                    wait(eng, y_done, (l * TT + i) * TS + s - 3)
                    eng.dma_start(xin[:, s % 4, :], x_now[rows(i, s), :]).then_inc(x_again_in[s % 4], 16)

                def load_z(i, s):
                    wait(eng, h_done, (l * TT + i) * TS + s - 3)
                    eng.dma_start(zin[:, s % 4, :], zs[rows(i, s), :]).then_inc(z_back_in[s % 4], 16)

                in_turns(eng, TS, [(load, 0), (load_z, 5), (load_x, 8)])

            eng.wait_ge(h_done, A0)

            def a_load(i, s):
                g = i * TS + s
                wait(eng, a_add, g - 3)
                eng.wait_ge(rows_out[s % 4], 16 * (2 * ((LAYERS - 1) * TT + i) + s // 4 + 1))
                if isinstance(i, int) and i == 0 and s == 4:
                    eng.wait_ge(w_lo, 2 * LAYERS + 2)
                    load_weights(0, t["L1_gnn_Wv"])
                    load_weights(1, t["L1_gnn_Wo"])
                eng.dma_start(a_x3[:, s % 4, :], xs[rows(i, s), :]).then_inc(rows_in[s % 4], 16)
                eng.dma_start(a_x0[:, s % 4, :], t["x"][rows(i, s), :]).then_inc(rows_in[s % 4], 16)

            def a_store_h(i, s):
                eng.wait_ge(normed, A0 + i * TS + s + 1)
                eng.dma_start(hs[rows(i, s), :], a_h[:, s % 4, :]).then_inc(h_out[s % 4], 16)

            def a_store_qk(i, s):
                g = i * TS + s
                eng.wait_ge(q_taken, g + 1)
                eng.dma_start(qs[rows(i, s), :], a_q[:, s % 4, :]).then_inc(qk_out[s % 4], 16)
                eng.wait_ge(k_taken, g + 1)
                eng.dma_start(ks[rows(i, s), :], a_k[:, s % 4, :]).then_inc(qk_out[s % 4], 16)

            in_turns(eng, TS, [(a_load, 0), (a_store_h, 6), (a_store_qk, 11)])
            def v_load(i, s):
                wait(eng, v_transposed, i * TS + s - 3)
                eng.wait_ge(h_out[s % 4], 16 * (2 * i + s // 4 + 1))
                eng.dma_start(v_h[:, s % 4, :], hs[rows(i, s), :]).then_inc(v_in[s % 4], 16)

            def v_store(i, s):
                eng.wait_ge(v_taken, i * TS + s + 1)
                eng.dma_start(vs[rows(i, s), :], v_o[:, s % 4, :]).then_inc(rows_out[s % 4], 16)

            in_turns(eng, TS, [(v_load, 0), (v_store, 8)])

            eng.wait_ge(m_step, 14)
            eng.dma_start(ends_m, m_ce[:, :, :].rearrange("p a h -> p (a h)")).then_inc(ends_out, 16)
            eng.wait_ge(ends_out, 16)
            eng.dma_start(m_ends[:, :, :, :].rearrange("p c a h -> p (c a h)"),
                          ends_m.rearrange("c w -> (c w)").unsqueeze(0).broadcast_to([CHUNKS, 2 * CHUNKS * HEADS])
                          ).then_inc(ends_in, 16)

            for k, name in enumerate(("L1_gnn_ln1_g", "L1_gnn_ln1_b", "L1_gnn_ln2_g", "L1_gnn_ln2_b", "L1_gnn_b2")):
                eng.dma_start(rows_bc[:, k], t[name].broadcast_to([P, D])).then_inc(vectors_in, 16)
            in_turns(eng, CB, [(lambda i, s: save_ends(3, i, s), 0)])
            carries(3)
            eng.dma_start(w1[:, :, :], t["L1_gnn_W1"].rearrange("(k p) n -> p k n", p=P)).then_inc(vectors_in, 16)
            eng.dma_start(w2[0:DFF, :], t["L1_gnn_W2"]).then_inc(vectors_in, 16)
            eng.dma_start(b1c[:, :], t["b1_col"]).then_inc(vectors_in, 16)
            eng.dma_start(ln1_b[:, :], t["ln1_b_cols"]).then_inc(vectors_in, 16)

            def d_load(i, s):
                g = i * TS + s
                wait(eng, mean_done, A0 + g - 3)
                eng.dma_start(d_a[:, s % 4, :], agg[rows(i, s), :]).then_inc(rows_in[s % 4], 16)

            def d_load_h(i, s):
                wait(eng, h_done, A0 + i * TS + s - 3)
                eng.dma_start(d_h[:, s % 4, :], hs[rows(i, s), :]).then_inc(x_again_in[s % 4], 16)

            def d_load_again(i, s):
                wait(eng, s3_done, i * TS + s - 3)
                eng.dma_start(d_h2[:, s % 4, :], hs[rows(i, s), :]).then_inc(z_back_in[s % 4], 16)

            def d_store(i, s):
                eng.wait_ge(o_done, i * TS + s + 1)
                eng.dma_start(out[rows(i, s), :], d_o[:, s % 4, :]).then_inc(rows_out[s % 4], 16)

            in_turns(eng, TS, [(d_load, 0), (d_load_h, 5), (d_load_again, 16), (d_store, 21)])
            for s in range(4):
                eng.wait_ge(rows_out[s], 16 * (ST_D + 2 * TT))

        @block.gpsimd
        def _(eng):
            last_row = eng.to_reg(NP - 1)
            eng.memset(zero[:, :, :], 0.0).then_inc(zero_set, 1)
            eng.memset(ident[:, :], 0.0).then_inc(prep, 1)
            eng.wait_ge(src_in, 16)
            eng.wait_ge(prep, 1)
            eng.affine_select(out=ident[:, :], in_=ident[:, :], compare_op=ALU.not_equal, fill=1.0,
                              base=0, pattern=[[-1, P]], channel_multiplier=1).then_inc(prep, 1)
            eng.memset(onesf[:, :], 1.0).then_inc(prep, 1)
            eng.wait_ge(tables, 7)
            eng.affine_select(out=carry_m[:, :], in_=carry_m[:, :], compare_op=ALU.is_gt, fill=0.0,
                              base=0, pattern=[[1, CHUNKS]], channel_multiplier=-1).then_inc(prep, 1)
            eng.affine_select(out=back_m[:, :], in_=back_m[:, :], compare_op=ALU.is_gt, fill=0.0,
                              base=0, pattern=[[-1, CHUNKS]], channel_multiplier=1).then_inc(prep, 1)

            def aggregate(a, source):
                def gather(i, s):
                    g = (a * TT + i) * CB + s
                    n = (LAYERS + 1 if a == 3 else a) * TT + i
                    free = weighed if a == 3 else lo_done
                    wait(eng, free, (i * CB + s if a == 3 else g) - CS + 1)
                    if s % CS == 0:
                        eng.tensor_copy(get_now[:, s:s + CS], src_i[:, bass.ds(i * CB + s, CS)]).then_inc(get_rows_set, 1)
                        eng.wait_ge(get_rows_set, n * CU + s // CS + 1)
                    eng.sem_inc(pool_go, 1)
                    eng.indirect_dma_start(
                        out=G[:, s % CS, :], out_offset=None, in_=source,
                        in_offset=bass.IndirectOffsetOnAxis(ap=get_now[:, s:s + 1], axis=0),
                    ).then_inc(gathered[s % CS], 16)

                def scatter(i, s):
                    g = (a * TT + i) * CB + s
                    if a == 0 and isinstance(i, int) and i + s == 0:
                        eng.wait_ge(zeroed, 16 * (TILES // 4))
                    if s % CS == 0:
                        for k in range(CS):
                            wait(eng, scattered[k], 16 * ((a * TT + i) * CU + s // CS - CU + 1))
                        eng.tensor_copy(put_now[:, s:s + CS], put_i[:, bass.ds(i * CB + s, CS)]).then_inc(put_rows_set, 1)
                        eng.wait_ge(put_rows_set, (a * TT + i) * CU + s // CS + 1)
                    eng.wait_ge(out_main, g + 1)
                    eng.wait_ge(out_extra, g + 1)
                    eng.sem_inc(pool_go, 1)
                    eng.indirect_dma_start(
                        out=agg, out_offset=bass.IndirectOffsetOnAxis(ap=put_now[:, s:s + 1], axis=0),
                        in_=O[:, s % CS, :], in_offset=None, bounds_check=last_row, oob_is_err=False,
                    ).then_inc(scattered[s % CS], 16)

                in_turns(eng, CB, [(gather, 0), (scatter, CS)])
                for s in range(CS):
                    eng.wait_ge(scattered[s], 16 * CU * TT * (a + 1))
                eng.wait_ge(fixed, 2 * (a + 1))
                eng.indirect_dma_start(
                    out=agg, out_offset=bass.IndirectOffsetOnAxis(ap=fix_i[:, 0:1], axis=0),
                    in_=fy[:, :], in_offset=None, bounds_check=last_row, oob_is_err=False).then_inc(fix_out, 16)
                eng.wait_ge(fix_out, 16 * (a + 1))

            for l in range(LAYERS):
                for s in range(4):
                    wait(eng, rows_out[s], 16 * 2 * TT * l)
                aggregate(l, t["x"] if l == 0 else xs)
                eng.wait_ge(vectors_in, 16 * 2 * (l + 1))

                def affine(i, s):
                    g = (l * TT + i) * TS + s
                    eng.wait_ge(normed, g + 1)
                    eng.tensor_tensor(hn[:, s % 4, :], hn[:, s % 4, :], rows_bc[:, 1, :], ALU.mult).then_inc(gained, 1)
                    eng.wait_ge(gained, g + 1)
                    eng.tensor_tensor(hn[:, s % 4, :], hn[:, s % 4, :], rows_bc[:, 2, :], ALU.add).then_inc(offset_done, 1)

                in_turns(eng, TS, [(affine, 0)])

            for s in range(4):
                eng.wait_ge(rows_out[s], 16 * 2 * TT * LAYERS)

            def a_sums(i, s):
                g = i * TS + s
                eng.wait_ge(rows_in[s % 4], R4_A + 32 * (2 * i + s // 4 + 1))
                wait(eng, normed, A0 + g - 3)
                eng.tensor_tensor(a_sum[:, s % 4, :], a_x3[:, s % 4, :], a_x0[:, s % 4, :], ALU.add).then_inc(a_add, 1)

            in_turns(eng, TS, [(a_sums, 0)])

            for s in range(4):
                eng.wait_ge(qk_out[s], 32 * 2 * TT)
                eng.wait_ge(h_out[s], 16 * 2 * TT)

            def gather_kq(i, s):
                g = i * CB + s
                wait(eng, kq_multiplied, g - QS + 1)
                if s % CS == 0:
                    eng.tensor_copy(get_now[:, s:s + CS], src_i[:, bass.ds(g, CS)]).then_inc(get_rows_set, 1)
                    eng.tensor_copy(get_now2[:, s:s + CS], dst_i[:, bass.ds(g, CS)]).then_inc(get_dst_rows_set, 1)
                    eng.wait_ge(get_rows_set, (LAYERS * TT + i) * CU + s // CS + 1)
                    eng.wait_ge(get_dst_rows_set, i * CU + s // CS + 1)
                eng.sem_inc(pool_go, 1)
                for tile, row, source in ((b_k, get_now, ks), (b_q, get_now2, qs)):
                    eng.indirect_dma_start(
                        out=tile[:, s % QS, :], out_offset=None, in_=source,
                        in_offset=bass.IndirectOffsetOnAxis(ap=row[:, s:s + 1], axis=0)).then_inc(kq_in[s % QS], 16)

            in_turns(eng, CB, [(gather_kq, 0)])
            for s in range(4):
                eng.wait_ge(rows_out[s], 16 * (ST_V + 2 * TT))
            eng.wait_ge(kq_multiplied, CHUNKS)
            aggregate(3, vs)
            eng.wait_ge(vectors_in, 16 * (2 * LAYERS + 9))

            def attention(i, s):
                g = i * TS + s
                eng.wait_ge(inv_done, TILES + g + 1)
                wait(eng, transposed, D0 + g - 1)
                eng.tensor_tensor(d_n[:, s % 2, :].rearrange("p (h d) -> p h d", h=HEADS),
                                  d_a[:, s % 4, 0:D].rearrange("p (h d) -> p h d", h=HEADS),
                                  d_z[:, s % 4, 1, :].unsqueeze(2).broadcast_to([P, HEADS, DK]),
                                  ALU.mult).then_inc(mean_done, 1)

            def gain1(i, s):
                eng.wait_ge(normed, D0 + i * TS + s + 1)
                eng.tensor_tensor(d_y[:, s, :], d_y[:, s, :], rows_bc[:, 0, :], ALU.mult).then_inc(gained, 1)

            def gain2(i, s):
                eng.wait_ge(normed2, i * TS + s + 1)
                eng.tensor_tensor(d_n2[:, s % 4, :], d_n2[:, s % 4, :], rows_bc[:, 2, :], ALU.mult).then_inc(gained2, 1)

            def offset2(i, s):
                eng.wait_ge(gained2, i * TS + s + 1)
                eng.tensor_tensor(d_n2[:, s % 4, :], d_n2[:, s % 4, :], rows_bc[:, 3, :], ALU.add).then_inc(offset2_done, 1)

            in_turns(eng, TS, [(gain1, 7), (gain2, 15), (attention, 1), (offset2, 15)])

        @block.tensor
        def _(eng):
            eng.wait_ge(prep, 3)

            def segment_sums(a, i, s):
                g = (a * TT + i) * CB + s
                o = s % 2
                eng.wait_ge(eq_done, g + 1)
                eng.wait_ge(hi_done, g + 1)
                wait(eng, out_main, g - 1)
                eng.matmul(bank[o][:, 0:D], E[:, s % HS, :], Ghi[:, s % HS, :], start=True, stop=False)
                eng.wait_ge(lo_done, g + 1)
                eng.matmul(bank[o][:, 0:D], E[:, s % HS, :], Glo[:, s % HS, :], start=False, stop=True)
                wait(eng, out_extra, g - 1)
                if a < 3:
                    last = eng.matmul(bank[2 + o][:, 0:HEADS], E[:, s % HS, :], ones_r[:, :], start=True, stop=True)
                else:
                    c = bass.ds(i * CB + s, 1)
                    eng.matmul(bank[2 + o][:, 0:HEADS], E[:, s % HS, :], ex_hi[:, c, :].rearrange("p c h -> p (c h)"), start=True, stop=False)
                    last = eng.matmul(bank[2 + o][:, 0:HEADS], E[:, s % HS, :], ex_lo[:, c, :].rearrange("p c h -> p (c h)"), start=False, stop=True)
                last.then_inc(summed, 1)

            def carry(a):
                eng.wait_ge(prep, 5)
                eng.wait_ge(out_main, CHUNKS * (a + 1))
                eng.wait_ge(out_extra, CHUNKS * (a + 1))
                eng.wait_ge(ends_back, 16 * (a + 1))
                eng.matmul(bank[0][0:CHUNKS, 0:D], carry_m[:, :], es[:, 1, 0:D], start=True, stop=True).then_inc(carried, 1)
                eng.matmul(bank[2][0:CHUNKS, 0:HEADS], carry_m[:, :], es[:, 1, D:AW], start=True, stop=True).then_inc(carried, 1)
                eng.wait_ge(fixed, 2 * (a + 1))

            def transpose4(into, tile):
                for k in range(KC):
                    last = eng.transpose(into[:, k * P:(k + 1) * P], tile[:, k * P:(k + 1) * P], ident[:, :])
                return last

            def product3(into, terms):
                step, steps = 0, len(terms) * KC * 3
                for hi, lo, w in terms:
                    for k in range(KC):
                        b = slice(k * P, (k + 1) * P)
                        for left, right in ((hi, whi), (hi, wlo), (lo, whi)):
                            last = eng.matmul(into, left[:, b], right[:, w, k, :], start=step == 0, stop=step == steps - 1)
                            step += 1
                return last

            for l in range(LAYERS):
                eng.wait_ge(w_hi, 2 * l + 1)
                eng.wait_ge(w_lo, 2 * l + 1)

                def z_transposes(i, s):
                    g = (l * TT + i) * TS + s
                    wait(eng, z_lo, g - 1)
                    eng.wait_ge(z_in[s % 4], 16 * (2 * (l * TT + i) + s // 4 + 1))
                    transpose4(bank[4 + s % 2], zx[:, s % 4, :]).then_inc(z_transposed, 1)

                def z_products(i, s):
                    g = (l * TT + i) * TS + s
                    o = s % 2
                    wait(eng, z_taken, g - 1)
                    eng.wait_ge(z_lo, g + 1)
                    product3(bank[6 + o][:, :], [(zhi[:, o, :], zlo[:, o, :], 1)]).then_inc(z_products_done, 1)

                in_turns(eng, 4, [(lambda i, s: segment_sums(l, i, s), 1 + AHEAD, 3)] + [(z_transposes, 0, 2)] * (l > 0)
                         + [(z_products, 2, 2)])
                carry(l)
                eng.wait_ge(w_hi, 2 * l + 2)
                eng.wait_ge(w_lo, 2 * l + 2)

                def transposes(i, s):
                    g = (l * TT + i) * TS + s
                    o = s % 2
                    wait(eng, rows_lo_done, g - 1)
                    eng.wait_ge(mean_done, g + 1)
                    transpose4(bank[2 + o], an[:, o, :]).then_inc(transposed, 1)

                def products(i, s):
                    g = (l * TT + i) * TS + s
                    o = s % 2
                    wait(eng, h_done, g - 1)
                    eng.wait_ge(rows_lo_done, g + 1)
                    product3(bank[o][:, :], [(ahi[:, o, :], alo[:, o, :], 0)]).then_inc(products_done, 1)

                in_turns(eng, TS, [(transposes, 2), (products, 4)])

            eng.wait_ge(w_hi, 2 * LAYERS + 2)
            eng.wait_ge(w_lo, 2 * LAYERS + 2)

            def a_transposes(i, s):
                g = A0 + i * TS + s
                wait(eng, rows_lo_done, g - 1)
                eng.wait_ge(normed, g + 1)
                transpose4(bank[s % 2], a_h[:, s % 4, :]).then_inc(transposed, 1)

            def a_products(i, s):
                g = i * TS + s
                o = s % 2
                eng.wait_ge(rows_lo_done, A0 + g + 1)
                wait(eng, q_taken, g - 1)
                product3(bank[2 + o][:, :], [(a_hi[:, o, :], a_lo[:, o, :], 0)])
                wait(eng, k_taken, g - 1)
                product3(bank[4 + o][:, :], [(a_hi[:, o, :], a_lo[:, o, :], 1)]).then_inc(products_done, 1)

            in_turns(eng, TS, [(a_transposes, 3), (a_products, 5)])

            eng.wait_ge(w_lo, 2 * LAYERS + 3)
            eng.wait_ge(k_taken, TILES)
            eng.wait_ge(q_taken, TILES)

            def v_transposes(i, s):
                g = i * TS + s
                wait(eng, v_lo_done, g - 1)
                eng.wait_ge(v_in[s % 4], 16 * (2 * i + s // 4 + 1))
                transpose4(bank[s % 2], v_h[:, s % 4, :]).then_inc(v_transposed, 1)

            def v_products(i, s):
                g = i * TS + s
                wait(eng, v_taken, g - 1)
                eng.wait_ge(v_lo_done, g + 1)
                product3(bank[2 + s % 2][:, :], [(v_hi[:, s % 2, :], v_lo[:, s % 2, :], 0)]).then_inc(v_products_done, 1)

            in_turns(eng, TS, [(v_transposes, 0), (v_products, 2)])

            eng.wait_ge(scores_done, CHUNKS)
            for n in range(HEADS):
                eng.transpose(bank[4 + n // 4][0:CHUNKS, (n % 4) * P:(n % 4 + 1) * P], e_all[:, :, n],
                              ident[:, :]).then_inc(m_transposed, 1)
            eng.wait_ge(m_step, 22)
            for n in range(HEADS):
                eng.transpose(bank[6 + n // 4][:, (n % 4) * CHUNKS:(n % 4 + 1) * CHUNKS], m_e[:, n, :],
                              ident[0:CHUNKS, 0:CHUNKS]).then_inc(m_transposed, 1)
            eng.wait_ge(m_step, 24)
            eng.wait_ge(ex_split, 1)

            in_turns(eng, CB, [(lambda i, s: segment_sums(3, i, s), 0)])
            carry(3)

            eng.wait_ge(vectors_in, 16 * (2 * LAYERS + 9))
            for k in range(KC):
                last = eng.matmul(bank[5][0:DFF, 0:1], w1[:, k, :], ln1_b[:, k:k + 1], start=k == 0, stop=k == KC - 1)
            last.then_inc(b1_mm, 1)
            eng.wait_ge(w_hi, 2 * LAYERS + 4)
            eng.wait_ge(w_lo, 2 * LAYERS + 4)

            def d_transposes(i, s):
                g = i * TS + s
                wait(eng, rows_lo_done, D0 + g - 1)
                eng.wait_ge(mean_done, A0 + g + 1)
                transpose4(bank[s % 2], d_n[:, s % 2, :]).then_inc(transposed, 1)

            def d_products(i, s):
                g = i * TS + s
                o = s % 2
                wait(eng, h_done, A0 + g - 1)
                eng.wait_ge(rows_lo_done, D0 + g + 1)
                product3(bank[2 + o][:, :], [(d_hi[:, o, :], d_lo[:, o, :], 0)]).then_inc(products_done, 1)

            def f_transposes(i, s):
                g = i * TS + s
                wait(eng, f_copied, g)
                eng.wait_ge(gained, A0 + g + 1)
                transpose4(bank[4], d_y[:, s, :]).then_inc(f_transposed, 1)

            def f_first(i, s):
                g = i * TS + s
                wait(eng, relu_done, g)
                eng.wait_ge(f_copied, g + 1)
                for k in range(KC):
                    last = eng.matmul(bank[5][0:DFF, 0:P], w1[:, k, :], d_yt[:, s % 2, k * P:(k + 1) * P],
                                      start=k == 0, stop=k == KC - 1)
                last.then_inc(ffn1_done, 1)

            def f_second(i, s):
                g = i * TS + s
                wait(eng, s2_done, g - 1)
                eng.wait_ge(relu_done, g + 1)
                eng.matmul(bank[6 + s % 2][:, :], d_f[:, s % 2, :], w2[:, :], start=True, stop=True).then_inc(ffn2_done, 1)

            eng.wait_ge(b2_sum, 2)
            eng.wait_ge(b1_sum, 1)
            in_turns(eng, TS, [(f_second, 12), (d_transposes, 2), (d_products, 4), (f_first, 10), (f_transposes, 8)])

        @block.scalar
        def _(eng):
            eng.wait_ge(eps_set, 1)
            def split_hi(a, i, s):
                g = (a * TT + i) * CB + s
                if a == 3:
                    eng.wait_ge(weighed, i * CB + s + 1)
                else:
                    eng.wait_ge(gathered[s % CS], 16 * ((a * TT + i) * CU + s // CS + 1))
                wait(eng, summed, g - HS + 1)
                eng.activation(Ghi[:, s % HS, :], (Gx if a == 3 else G)[:, s % CS, :], ACT.Copy).then_inc(hi_done, 1)

            def take_sums(a, i, s):
                g = (a * TT + i) * CB + s
                eng.wait_ge(summed, g + 1)
                wait(eng, scattered[s % CS], 16 * ((a * TT + i) * CU + s // CS))
                wait(eng, ends_saved[s % CS], 16 * ((a * TT + i) * CU + s // CS))
                eng.activation(O[:, s % CS, 0:D], bank[s % 2][:, 0:D], ACT.Copy).then_inc(out_main, 1)

            def deviation(i, s, sems, base, sd_t, mv_t, n):
                eng.wait_ge(sems[1], base + i * TS + s + 1)
                eng.activation(sd_t[:, n, 0:1], mv_t[:, n, 1:2], ACT.Sqrt, bias=eps[:, 0:1]).then_inc(sems[2], 1)

            for l in range(LAYERS):
                if l == 0:
                    eng.wait_ge(weights_in, 32)
                    eng.activation(whi[:, 1], wraw[:, 1], ACT.Copy).then_inc(w_hi, 1)
                    eng.dma_start(dst_bc[:, 0:CB * P], t["dst_row"][:, 0:CB * P].broadcast_to([P, CB * P])).then_inc(dst_bc_in, 16)
                    eng.wait_ge(zero_set, 1)
                    agg_flat = agg.rearrange("(p r) w -> p (r w)", p=P)
                    for r in range(TILES // 4):
                        eng.dma_start(agg_flat[:, r * 4 * AW:(r + 1) * 4 * AW],
                                      zero[:, :, :].rearrange("p s w -> p (s w)")).then_inc(zeroed, 16)
                    eng.dma_start(dst_bc[:, CB * P:EP], t["dst_row"][:, CB * P:EP].broadcast_to([P, EP - CB * P])).then_inc(dst_bc_rest_in, 16)

                def z_split(i, s):
                    g = (l * TT + i) * TS + s
                    if l:
                        eng.wait_ge(z_transposed, g - TILES + 1)
                    else:
                        eng.wait_ge(z_in[s % 4], 16 * (2 * i + s // 4 + 1))
                    wait(eng, z_products_done, g - 1)
                    eng.activation(zhi[:, s % 2, :], bank[4 + s % 2][:, :] if l else zx[:, s % 4, :], ACT.Copy).then_inc(z_hi, 1)

                in_turns(eng, 4, [(lambda i, s: split_hi(l, i, s), AHEAD, 3), (z_split, 1, 2),
                                  (lambda i, s: take_sums(l, i, s), 2 + AHEAD, 3)])
                eng.wait_ge(weights_in, 16 * (2 * l + 3))
                eng.activation(whi[:, 0], wraw[:, 0], ACT.Copy).then_inc(w_hi, 1)
                eng.wait_ge(z_products_done, TILES * (l + 1))
                eng.activation(whi[:, 1], wraw[:, 1], ACT.Copy).then_inc(w_hi, 1)

                def mean(i, s):
                    g = (l * TT + i) * TS + s
                    if l == 0:
                        eng.wait_ge(inv_done, g + 1)
                    eng.wait_ge(rows_in[s % 4], 16 * (2 * (l * TT + i) + s // 4 + 1))
                    wait(eng, transposed, g - 1)
                    eng.activation(an[:, s % 2, :], ain[:, s % 4, 0:D], ACT.Copy, scale=inv_n[:, bass.ds(i * TS + s, 1)]).then_inc(mean_done, 1)

                def split_nodes(i, s):
                    g = (l * TT + i) * TS + s
                    o = s % 2
                    eng.wait_ge(transposed, g + 1)
                    wait(eng, products_done, g - 1)
                    eng.activation(ahi[:, o, :], bank[2 + o][:, :], ACT.Copy).then_inc(rows_hi_done, 1)

                def normalise(i, s):
                    g = (l * TT + i) * TS + s
                    o = s % 2
                    eng.wait_ge(shift_done, g + 1)
                    wait(eng, y_done, g - 3)
                    eng.activation(hn[:, s % 4, :], h[:, o, :], ACT.Identity, bias=sd[:, o, 2:3],
                                   scale=sd[:, o, 1:2]).then_inc(normed, 1)

                def store(i, s):
                    g = (l * TT + i) * TS + s
                    eng.wait_ge(y_done, g + 1)
                    eng.dma_start(xs[rows(i, s), :], y[:, s % 4, :]).then_inc(rows_out[s % 4], 16)

                in_turns(eng, TS, [(store, 9), (split_nodes, 3), (mean, 1), (normalise, 6),
                                   (lambda i, s: deviation(i, s, ln1, l * TILES, sd, mv, s % 2), 5)])

            eng.wait_ge(weights_in, 16 * (2 * LAYERS + 2))
            eng.wait_ge(products_done, A0)
            eng.activation(whi[:, 0], wraw[:, 0], ACT.Copy).then_inc(w_hi, 1)

            def a_normalise(i, s):
                g = i * TS + s
                eng.wait_ge(shift_done, A0 + g + 1)
                wait(eng, transposed, A0 + g - 3)
                wait(eng, h_out[s % 4], 16 * (2 * i + s // 4))
                eng.activation(a_h[:, s % 4, :], a_sum[:, s % 4, :], ACT.Identity, bias=a_sd[:, s % 2, 2:3],
                               scale=a_sd[:, s % 2, 1:2]).then_inc(normed, 1)

            def a_split(i, s):
                g = A0 + i * TS + s
                eng.wait_ge(transposed, g + 1)
                wait(eng, products_done, g - 1)
                eng.activation(a_hi[:, s % 2, :], bank[s % 2][:, :], ACT.Copy).then_inc(rows_hi_done, 1)

            def take_q(i, s):
                g = i * TS + s
                eng.wait_ge(products_done, A0 + g + 1)
                wait(eng, qk_out[s % 4], 32 * (2 * i + s // 4))
                eng.activation(a_q[:, s % 4, :], bank[2 + s % 2][:, :], ACT.Copy).then_inc(q_taken, 1)

            in_turns(eng, TS, [(a_split, 4), (take_q, 6), (a_normalise, 2),
                                   (lambda i, s: deviation(i, s, ln1, A0, a_sd, a_mv, s % 2), 1)])

            eng.wait_ge(weights_in, 16 * (2 * LAYERS + 4))
            eng.wait_ge(products_done, D0)
            for s in range(4):
                eng.wait_ge(h_out[s], 16 * 2 * TT)
            eng.activation(whi[:, 0], wraw[:, 0], ACT.Copy).then_inc(w_hi, 1)

            def v_split(i, s):
                g = i * TS + s
                eng.wait_ge(v_transposed, g + 1)
                wait(eng, v_products_done, g - 1)
                eng.activation(v_hi[:, s % 2, :], bank[s % 2][:, :], ACT.Copy).then_inc(v_hi_done, 1)

            def v_finish(i, s):
                eng.wait_ge(v_products_done, i * TS + s + 1)
                wait(eng, rows_out[s % 4], 16 * (ST_V + 2 * i + s // 4))
                eng.activation(v_o[:, s % 4, :], bank[2 + s % 2][:, :], ACT.Copy).then_inc(v_taken, 1)

            in_turns(eng, TS, [(v_split, 1), (v_finish, 3)])

            eng.wait_ge(m_step, 24)
            eng.activation(ex[:, :, :], e_all[:, :, :], ACT.Exp, scale=1.0 / DK ** 0.5).then_inc(exp_done, 1)
            eng.wait_ge(exp_done, 1)
            eng.activation(ex_hi[:, :, :], ex[:, :, :], ACT.Copy).then_inc(exp_done, 1)
            in_turns(eng, CB, [(lambda i, s: split_hi(3, i, s), 0), (lambda i, s: take_sums(3, i, s), 1)])
            eng.wait_ge(fix_out, 16 * 4)
            eng.wait_ge(vectors_in, 16 * (2 * LAYERS + 9))
            eng.activation(whi[:, 0], wraw[:, 1], ACT.Copy).then_inc(w_hi, 1)

            def d_split(i, s):
                g = D0 + i * TS + s
                eng.wait_ge(transposed, g + 1)
                wait(eng, products_done, g - 1)
                eng.activation(d_hi[:, s % 2, :], bank[s % 2][:, :], ACT.Copy).then_inc(rows_hi_done, 1)

            def d_norm1(i, s):
                g = i * TS + s
                eng.wait_ge(shift_done, D0 + g + 1)
                wait(eng, s2_done, g - 7)
                eng.activation(d_y[:, s, :], d_s1[:, s % 2, :], ACT.Identity, bias=d_sd[:, s % 2, 2:3],
                               scale=d_sd[:, s % 2, 1:2]).then_inc(normed, 1)

            def f_take(i, s):
                g = i * TS + s
                eng.wait_ge(f_transposed, g + 1)
                wait(eng, ffn1_done, g - 1)
                eng.activation(d_yt[:, s % 2, :], bank[4][:, :], ACT.Copy).then_inc(f_copied, 1)

            def f_relu(i, s):
                g = i * TS + s
                eng.wait_ge(ffn1_done, g + 1)
                wait(eng, ffn2_done, g - 1)
                eng.activation(d_f[0:DFF, s % 2, :], bank[5][0:DFF, 0:P], ACT.Relu, bias=b1s[:, 0:1]).then_inc(relu_done, 1)

            def d_norm2(i, s):
                g = i * TS + s
                eng.wait_ge(ln2[4], g + 1)
                wait(eng, s3_done, g - 3)
                eng.activation(d_n2[:, s % 4, :], d_s2[:, s % 2, :], ACT.Identity, bias=d_sd[:, 2 + s % 2, 2:3],
                               scale=d_sd[:, 2 + s % 2, 1:2]).then_inc(normed2, 1)

            def d_norm3(i, s):
                g = i * TS + s
                eng.wait_ge(ln3[4], g + 1)
                wait(eng, rows_out[s % 4], 16 * (ST_D + 2 * i + s // 4))
                eng.activation(d_o[:, s % 4, :], d_s3[:, s % 2, :], ACT.Identity, bias=d_sd[:, 4 + s % 2, 2:3],
                               scale=d_sd[:, 4 + s % 2, 1:2]).then_inc(o_done, 1)

            eng.wait_ge(b1_sum, 1)
            in_turns(eng, TS, [
                (f_take, 9), (f_relu, 11), (d_split, 3), (d_norm1, 6), (d_norm2, 14), (d_norm3, 17),
                (lambda i, s: deviation(i, s, ln1, D0, d_sd, d_mv, s % 2), 5),
                (lambda i, s: deviation(i, s, ln2, 0, d_sd, d_mv, 2 + s % 2), 13),
                (lambda i, s: deviation(i, s, ln3, 0, d_sd, d_mv, 4 + s % 2), 16)])

        @block.vector
        def _(eng):
            eng.memset(eps[:, :], EPS).then_inc(eps_set, 1)
            eng.wait_ge(idx_in, 16 * 6)
            eng.tensor_copy(dst_f[:, :], dst_i[:, :]).then_inc(tables, 1)
            eng.tensor_tensor(same[:, :], dst_i[:, :], nxt_i[:, :], ALU.is_equal).then_inc(tables, 1)
            eng.tensor_copy(ends_f[:, :], ends_i[:, :]).then_inc(tables, 1)
            eng.wait_ge(tables, 3)
            eng.scalar_tensor_tensor(out=put_i[:, :], in0=same[:, :], scalar=float(SKIP), in1=dst_f[:, :],
                                     op0=ALU.mult, op1=ALU.add).then_inc(tables, 1)
            eng.tensor_tensor(fixt[:, 0:1], ends_f[:, 0:1], ends_f[:, 2:3], ALU.is_equal).then_inc(m_step, 1)
            eng.tensor_tensor(fixt[:, 1:2], ends_f[:, 0:1], ends_f[:, 3:4], ALU.is_equal).then_inc(m_step, 1)
            eng.wait_ge(m_step, 2)
            eng.scalar_tensor_tensor(out=fixt[:, 1:2], in0=fixt[:, 1:2], scalar=-1.0, in1=fixt[:, 0:1],
                                     op0=ALU.add, op1=ALU.mult).then_inc(m_step, 1)
            eng.wait_ge(m_step, 3)
            eng.tensor_scalar(fixt[:, 0:1], fixt[:, 1:2], float(SKIP), float(SKIP), ALU.mult, ALU.add).then_inc(m_step, 1)
            eng.wait_ge(m_step, 4)
            eng.tensor_tensor(fix_i[:, :], fixt[:, 0:1], ends_f[:, 0:1], ALU.add).then_inc(tables, 1)
            eng.tensor_scalar(carry_m[:, :], first_bc[:, :], ends_f[:, 1:2], None, ALU.is_equal).then_inc(tables, 1)
            eng.tensor_scalar(back_m[:, :], last_bc[:, :], ends_f[:, 0:1], None, ALU.is_equal).then_inc(tables, 1)
            eng.wait_ge(prep, 3)
            eng.tensor_copy(ones_r[:, :], onesf[:, :]).then_inc(m_step, 1)

            def weights_lo(n, halves, source=None):
                for k, w in enumerate(halves):
                    eng.wait_ge(w_hi, n + k + 1)
                    eng.tensor_tensor(wlo[:, w], wraw[:, w if source is None else source], whi[:, w].bitcast(F32), ALU.subtract).then_inc(w_lo, 1)

            def equal_edges(a, i, s):
                g = (a * TT + i) * CB + s
                c = i * CB + s
                if a == 0 and isinstance(i, int) and i + s == 0:
                    eng.wait_ge(dst_bc_in, 16)
                if a == 0 and isinstance(i, int) and i == 1 and s == 0:
                    eng.wait_ge(dst_bc_rest_in, 16)
                wait(eng, summed, g - HS + 1)
                eng.tensor_scalar(E[:, s % HS, :], dst_bc[:, bass.ds(c * P, P)], dst_f[:, bass.ds(c, 1)], None,
                                  ALU.is_equal).then_inc(eq_done, 1)

            def weigh(i, s):
                c = i * CB + s
                eng.wait_ge(gathered[s % CS], 16 * ((3 * TT + i) * CU + s // CS + 1))
                wait(eng, lo_done, 3 * CHUNKS + c - CS + 1)
                eng.tensor_tensor(Gx[:, s % CS, :].rearrange("p (h d) -> p h d", h=HEADS),
                                  G[:, s % CS, :].rearrange("p (h d) -> p h d", h=HEADS),
                                  ex[:, bass.ds(c, 1), :].rearrange("p c h -> p (c h)").unsqueeze(2).broadcast_to([P, HEADS, DK]),
                                  ALU.mult).then_inc(weighed, 1)

            def split_lo(a, i, s):
                g = (a * TT + i) * CB + s
                eng.wait_ge(hi_done, g + 1)
                eng.tensor_tensor(Glo[:, s % HS, :], (Gx if a == 3 else G)[:, s % CS, :], Ghi[:, s % HS, :].bitcast(F32),
                                  ALU.subtract).then_inc(lo_done, 1)

            def take_extra(a, i, s):
                g = (a * TT + i) * CB + s
                eng.wait_ge(summed, g + 1)
                wait(eng, scattered[s % CS], 16 * ((a * TT + i) * CU + s // CS))
                wait(eng, ends_saved[s % CS], 16 * ((a * TT + i) * CU + s // CS))
                eng.tensor_copy(O[:, s % CS, D:AW], bank[2 + s % 2][:, 0:HEADS]).then_inc(out_extra, 1)

            def fix(a):
                eng.wait_ge(ends_back, 16 * (a + 1))
                eng.wait_ge(carried, 2 * (a + 1))
                eng.tensor_tensor(fy[:, 0:D], es[:, 0, 0:D], bank[0][0:CHUNKS, 0:D], ALU.add).then_inc(fixed, 1)
                eng.tensor_tensor(fy[:, D:AW], es[:, 0, D:AW], bank[2][0:CHUNKS, 0:HEADS], ALU.add).then_inc(fixed, 1)

            def norm_steps(base, sems, tile, st_t, mv_t, sd_t):
                def moments(i, s):
                    eng.bn_stats(st_t(s), tile(s)).then_inc(sems[0], 1)

                def mean_variance(i, s):
                    eng.wait_ge(sems[0], base + i * TS + s + 1)
                    eng.sem_inc(dve_go, 1)
                    eng.bn_aggr(mv_t(s), st_t(s)).then_inc(sems[1], 1)

                def invert(i, s):
                    eng.wait_ge(sems[2], base + i * TS + s + 1)
                    eng.reciprocal(sd_t(s)[:, 1:2], sd_t(s)[:, 0:1]).then_inc(sems[3], 1)

                def shift(i, s):
                    eng.wait_ge(sems[3], base + i * TS + s + 1)
                    eng.tensor_scalar(sd_t(s)[:, 2:3], mv_t(s)[:, 0:1], sd_t(s)[:, 1:2], -1.0, ALU.mult, ALU.mult).then_inc(sems[4], 1)

                return moments, mean_variance, invert, shift

            for l in range(LAYERS):
                if l == 0:
                    weights_lo(0, (1,))

                def z_split_lo(i, s):
                    eng.wait_ge(z_hi, (l * TT + i) * TS + s + 1)
                    eng.tensor_tensor(zlo[:, s % 2, :], bank[4 + s % 2][:, :] if l else zx[:, s % 4, :], zhi[:, s % 2, :].bitcast(F32), ALU.subtract).then_inc(z_lo, 1)

                def z_take(i, s):
                    g = (l * TT + i) * TS + s
                    eng.wait_ge(z_products_done, g + 1)
                    wait(eng, z_out[s % 4], 16 * (2 * (l * TT + i) + s // 4))
                    eng.tensor_tensor(zo[:, s % 4, :], bank[6 + s % 2][:, :], rows_bc[:, 0, :], ALU.add).then_inc(z_taken, 1)

                eng.wait_ge(bias_in, 16 * (l + 1))
                in_turns(eng, 4, [(lambda i, s: equal_edges(l, i, s), AHEAD, 3), (z_take, 3, 2),
                                  (lambda i, s: split_lo(l, i, s), AHEAD, 3),
                                  (lambda i, s: take_extra(l, i, s), 2 + AHEAD, 3),
                                  (z_split_lo, 1, 2)])
                weights_lo(2 * l + 1, (0, 1))
                fix(l)
                eng.wait_ge(vectors_in, 16 * 2 * (l + 1))

                def inverse_count(i, s):
                    g = i * TS + s
                    eng.wait_ge(rows_in[s % 4], 16 * (2 * i + s // 4 + 1))
                    o = s % 2
                    wait(eng, inv_done, g - 1)
                    eng.tensor_scalar(inv[:, o:o + 1], ain[:, s % 4, D:D + 1], 1.0, None, ALU.max).then_inc(inv_max, 1)
                    eng.wait_ge(inv_max, g + 1)
                    eng.reciprocal(inv_n[:, bass.ds(g, 1)], inv[:, o:o + 1]).then_inc(inv_done, 1)

                def split_nodes_lo(i, s):
                    g = (l * TT + i) * TS + s
                    o = s % 2
                    eng.wait_ge(rows_hi_done, g + 1)
                    eng.tensor_tensor(alo[:, o, :], bank[2 + o][:, :], ahi[:, o, :].bitcast(F32), ALU.subtract).then_inc(rows_lo_done, 1)

                def add_right(i, s):
                    g = (l * TT + i) * TS + s
                    o = s % 2
                    eng.wait_ge(products_done, g + 1)
                    eng.wait_ge(z_back_in[s % 4], 16 * (2 * (l * TT + i) + s // 4 + 1))
                    wait(eng, normed, g - 1)
                    eng.tensor_tensor(h[:, o, :], bank[o][:, :], zin[:, s % 4, :], ALU.add).then_inc(h_done, 1)

                moments, mean_variance, invert, shift = norm_steps(
                    l * TILES, ln1, lambda s: h[:, s % 2, :], lambda s: st[:, s % 2, :],
                    lambda s: mv[:, s % 2, :], lambda s: sd[:, s % 2, :])

                def moments_of_sum(i, s):
                    eng.wait_ge(h_done, (l * TT + i) * TS + s + 1)
                    moments(i, s)

                def residual(i, s):
                    g = (l * TT + i) * TS + s
                    eng.wait_ge(offset_done, g + 1)
                    eng.wait_ge(x_again_in[s % 4], 16 * (2 * (l * TT + i) + s // 4 + 1))
                    wait(eng, rows_out[s % 4], 16 * (2 * (l * TT + i) + s // 4))
                    eng.scalar_tensor_tensor(out=y[:, s % 4, :], in0=hn[:, s % 4, :], scalar=0.0, in1=xin[:, s % 4, :],
                                             op0=ALU.max, op1=ALU.add).then_inc(y_done, 1)

                in_turns(eng, TS, [(invert, 6), (add_right, 5), (shift, 6), (moments_of_sum, 5), (residual, 8)]
                         + [(inverse_count, 0)] * (l == 0) + [(mean_variance, 5), (split_nodes_lo, 3)])

            weights_lo(2 * LAYERS + 1, (0,))

            moments, mean_variance, invert, shift = norm_steps(
                A0, ln1, lambda s: a_sum[:, s % 4, :], lambda s: a_st[:, s % 2, :],
                lambda s: a_mv[:, s % 2, :], lambda s: a_sd[:, s % 2, :])

            def a_moments(i, s):
                eng.wait_ge(a_add, i * TS + s + 1)
                moments(i, s)

            def a_split_lo(i, s):
                g = A0 + i * TS + s
                eng.wait_ge(rows_hi_done, g + 1)
                eng.tensor_tensor(a_lo[:, s % 2, :], bank[s % 2][:, :], a_hi[:, s % 2, :].bitcast(F32), ALU.subtract).then_inc(rows_lo_done, 1)

            def take_k(i, s):
                g = i * TS + s
                eng.wait_ge(products_done, A0 + g + 1)
                wait(eng, qk_out[s % 4], 32 * (2 * i + s // 4))
                eng.tensor_copy(a_k[:, s % 4, :], bank[4 + s % 2][:, :]).then_inc(k_taken, 1)

            in_turns(eng, TS, [(invert, 2), (take_k, 6), (shift, 2), (a_moments, 1), (mean_variance, 1), (a_split_lo, 4)])

            def score(i, s):
                g = i * CB + s
                eng.wait_ge(kq_in[s % QS], 32 * (CB // QS * i + s // QS + 1))
                eng.tensor_tensor(b_kq[:, s % 2, :], b_k[:, s % QS, :], b_q[:, s % QS, :], ALU.mult).then_inc(kq_multiplied, 1)
                eng.wait_ge(kq_multiplied, g + 1)
                eng.sem_inc(dve_go, 1)
                eng.tensor_reduce(e_all[:, bass.ds(g, 1), :].rearrange("p c h -> p (c h)"),
                                  b_kq[:, s % 2, :].rearrange("p (h d) -> p h d", h=HEADS), AX.X, ALU.add).then_inc(scores_done, 1)

            def v_split_lo(i, s):
                eng.wait_ge(v_hi_done, i * TS + s + 1)
                eng.tensor_tensor(v_lo[:, s % 2, :], bank[s % 2][:, :], v_hi[:, s % 2, :].bitcast(F32), ALU.subtract).then_inc(v_lo_done, 1)

            weights_lo(2 * LAYERS + 2, (0,))
            in_turns(eng, 4, [(score, 0, 3), (v_split_lo, 1, 2)])

            eng.wait_ge(v_products_done, TILES)
            eng.memset(m_row[:, :, :], 0.0).then_inc(m_step, 1)
            eng.wait_ge(m_step, 6)
            eng.tensor_tensor(m_row[:, 0, 1:P], drow[:, 1:P], drow[:, 0:P - 1], ALU.is_equal)
            eng.tensor_tensor(m_row[:, 1, 0:P - 1], drow[:, 1:P], drow[:, 0:P - 1], ALU.is_equal).then_inc(m_step, 1)
            eng.wait_ge(m_step, 7)
            for k, tile in enumerate((m_new, m_end)):
                eng.tensor_scalar(tile[:, :, :], m_row[:, k:k + 1, :].broadcast_to([CHUNKS, HEADS, P]), -1.0, FAR, ALU.add, ALU.mult)
            for k, tile in enumerate((m_first, m_last)):
                eng.tensor_scalar(m_t[:, k, :], drow[:, :], ends_f[:, k:k + 1], None, ALU.is_equal).then_inc(m_step, 1)
                eng.wait_ge(m_step, 8 + k)
                eng.tensor_scalar(tile[:, :], m_t[:, k, :], -1.0, FAR, ALU.add, ALU.mult)
            eng.tensor_scalar(m_prev[:, :], back_m[:, :], -1.0, FAR, ALU.add, ALU.mult)
            eng.tensor_scalar(m_next[:, :], carry_m[:, :], -1.0, FAR, ALU.add, ALU.mult).then_inc(m_step, 1)
            eng.wait_ge(m_transposed, HEADS)
            eng.tensor_copy(m_e[:, 0:4, :].rearrange("p h e -> p (h e)"), bank[4][0:CHUNKS, :])
            eng.tensor_copy(m_e[:, 4:8, :].rearrange("p h e -> p (h e)"), bank[5][0:CHUNKS, :]).then_inc(m_step, 1)
            eng.wait_ge(m_step, 11)
            flat = [x[:, :, :].rearrange("p h e -> p (h e)") for x in (m_new, m_e, m_f, m_end)]
            eng.tensor_tensor_scan(flat[2], flat[0], flat[1], -FAR, ALU.add, ALU.max).then_inc(m_step, 1)
            eng.wait_ge(m_step, 12)
            eng.tensor_tensor_scan(flat[1][:, ::-1], flat[3][:, ::-1], flat[2][:, ::-1], -FAR, ALU.add, ALU.max).then_inc(m_step, 1)
            eng.wait_ge(m_step, 13)
            eng.tensor_copy(m_ce[:, 0, :], m_f[:, :, P - 1])
            eng.tensor_copy(m_ce[:, 1, :], m_e[:, :, 0]).then_inc(m_step, 1)
            eng.wait_ge(ends_in, 16)
            for k, mask in enumerate((m_prev, m_next)):
                eng.tensor_tensor(m_ends[:, :, k], m_ends[:, :, k], mask[:, :].unsqueeze(2).broadcast_to([CHUNKS, CHUNKS, HEADS]),
                                  ALU.add).then_inc(m_step, 1)
                eng.wait_ge(m_step, 15 + 2 * k)
                eng.tensor_reduce(m_c[:, k, :], m_ends[:, :, k].rearrange("p c h -> p h c"), AX.X, ALU.max).then_inc(m_step, 1)
            eng.wait_ge(m_step, 18)
            for k, mask in enumerate((m_first, m_last)):
                eng.tensor_tensor(m_t[:, :, :], mask[:, :].unsqueeze(1).broadcast_to([CHUNKS, HEADS, P]),
                                  m_c[:, k, :].unsqueeze(2).broadcast_to([CHUNKS, HEADS, P]), ALU.add).then_inc(m_step, 1)
                eng.wait_ge(m_step, 19 + 2 * k)
                eng.tensor_tensor(m_e[:, :, :], m_e[:, :, :], m_t[:, :, :], ALU.max).then_inc(m_step, 1)
                eng.wait_ge(m_step, 20 + 2 * k)
            eng.wait_ge(m_transposed, 2 * HEADS)
            for k in range(2):
                half = e_all[:, :, 4 * k:4 * k + 4].rearrange("p c h -> p h c")
                eng.tensor_tensor(half, half, bank[6 + k][:, 0:4 * CHUNKS].rearrange("p (h c) -> p h c", h=4), ALU.subtract).then_inc(m_step, 1)
            eng.wait_ge(exp_done, 2)
            eng.tensor_tensor(ex_lo[:, :, :], ex[:, :, :], ex_hi[:, :, :].bitcast(F32), ALU.subtract).then_inc(ex_split, 1)
            in_turns(eng, CB, [(weigh, 0), (lambda i, s: equal_edges(3, i, s), 1), (lambda i, s: split_lo(3, i, s), 1),
                               (lambda i, s: take_extra(3, i, s), 2)])
            fix(3)
            eng.wait_ge(vectors_in, 16 * (2 * LAYERS + 9))
            eng.tensor_tensor(w2[DFF:DFF + 1, :], rows_bc[DFF:DFF + 1, 4, :], rows_bc[DFF:DFF + 1, 1, :], ALU.add).then_inc(b2_sum, 1)
            eng.memset(d_f[DFF:DFF + 1, :, :], 1.0).then_inc(b2_sum, 1)
            eng.wait_ge(b1_mm, 1)
            eng.tensor_tensor(b1s[:, :], b1c[:, :], bank[5][0:DFF, 0:1], ALU.add).then_inc(b1_sum, 1)
            weights_lo(2 * LAYERS + 3, (0,), 1)

            def inverse_weight(i, s):
                g = TILES + i * TS + s
                eng.wait_ge(rows_in[s % 4], R4_D + 16 * (2 * i + s // 4 + 1))
                eng.tensor_scalar(d_z[:, s % 4, 0, :], d_a[:, s % 4, D:AW], 1e-30, None, ALU.max).then_inc(inv_max, 1)
                eng.wait_ge(inv_max, g + 1)
                eng.reciprocal(d_z[:, s % 4, 1, :], d_z[:, s % 4, 0, :]).then_inc(inv_done, 1)

            def d_split_lo(i, s):
                eng.wait_ge(rows_hi_done, D0 + i * TS + s + 1)
                eng.tensor_tensor(d_lo[:, s % 2, :], bank[s % 2][:, :], d_hi[:, s % 2, :].bitcast(F32), ALU.subtract).then_inc(rows_lo_done, 1)

            def add1(i, s):
                g = i * TS + s
                o = s % 2
                eng.wait_ge(products_done, D0 + g + 1)
                eng.wait_ge(x_again_in[s % 4], 16 * (XR_D + 2 * i + s // 4 + 1))
                wait(eng, normed, D0 + g - 1)
                eng.tensor_tensor(d_s1[:, o, :], bank[2 + o][:, :], d_h[:, s % 4, :], ALU.add).then_inc(h_done, 1)

            def add2(i, s):
                g = i * TS + s
                o = s % 2
                eng.wait_ge(ffn2_done, g + 1)
                wait(eng, normed2, g - 1)
                eng.tensor_tensor(d_s2[:, o, :], bank[6 + o][:, :], d_y[:, s, :], ALU.add).then_inc(s2_done, 1)

            def add3(i, s):
                g = i * TS + s
                eng.wait_ge(offset2_done, g + 1)
                eng.wait_ge(z_back_in[s % 4], 16 * (XR_D + 2 * i + s // 4 + 1))
                wait(eng, o_done, g - 1)
                eng.tensor_tensor(d_s3[:, s % 2, :], d_n2[:, s % 4, :], d_h2[:, s % 4, :], ALU.add).then_inc(s3_done, 1)

            moments1, mean_variance1, invert1, shift1 = norm_steps(
                D0, ln1, lambda s: d_s1[:, s % 2, :], lambda s: d_st[:, s % 2, :],
                lambda s: d_mv[:, s % 2, :], lambda s: d_sd[:, s % 2, :])
            moments2, mean_variance2, invert2, shift2 = norm_steps(
                0, ln2, lambda s: d_s2[:, s % 2, :], lambda s: d_st[:, 2 + s % 2, :],
                lambda s: d_mv[:, 2 + s % 2, :], lambda s: d_sd[:, 2 + s % 2, :])
            moments3, mean_variance3, invert3, shift3 = norm_steps(
                0, ln3, lambda s: d_s3[:, s % 2, :], lambda s: d_st[:, 4 + s % 2, :],
                lambda s: d_mv[:, 4 + s % 2, :], lambda s: d_sd[:, 4 + s % 2, :])

            def moments_of_sum1(i, s):
                eng.wait_ge(h_done, A0 + i * TS + s + 1)
                moments1(i, s)

            def moments_of_sum2(i, s):
                eng.wait_ge(s2_done, i * TS + s + 1)
                moments2(i, s)

            def moments_of_sum3(i, s):
                eng.wait_ge(s3_done, i * TS + s + 1)
                moments3(i, s)

            in_turns(eng, TS, [
                (invert1, 6), (invert2, 14), (invert3, 17), (shift1, 6), (shift2, 14), (shift3, 17),
                (add1, 5), (add2, 13), (moments_of_sum1, 5), (add3, 16), (moments_of_sum2, 13), (mean_variance1, 5),
                (moments_of_sum3, 16), (mean_variance2, 13), (mean_variance3, 16), (inverse_weight, 0), (d_split_lo, 3)])


_SAME = ["L0_gnn_b", "L0_gnn_ln_g", "L0_gnn_ln_b", "L1_gnn_Wq", "L1_gnn_Wk", "L1_gnn_Wv", "L1_gnn_Wo",
         "L1_gnn_W1", "L1_gnn_W2"]
_ROWS = ["L1_gnn_ln1_g", "L1_gnn_ln1_b", "L1_gnn_ln2_g", "L1_gnn_ln2_b", "L1_gnn_b2"]


def kernel(**inputs):
    import concourse.bacc as bacc
    from concourse.bass_utils import run_bass_kernel_spmd

    a = {k: np.asarray(v) for k, v in inputs.items()}
    x = np.zeros((NP, D), np.float32)
    x[:NODES] = a["x"]
    src = np.zeros(EP, np.int32)
    src[:EDGES] = a["src"]
    dst = np.full(EP, NODES, np.int32)
    dst[:EDGES] = a["dst"]
    around = np.full(EP + 2, -1, np.int32)
    around[1:-1] = dst
    first = np.arange(CHUNKS) * P
    last = first + P - 1
    arrays = {
        "x": x,
        "x_blocks": np.ascontiguousarray(x.reshape(TILES, P, KC, P).transpose(0, 3, 2, 1)).reshape(NP, D),
        "src_cols": np.ascontiguousarray(src.reshape(CHUNKS, P).T),
        "dst_cols": np.ascontiguousarray(dst.reshape(CHUNKS, P).T),
        "next_cols": np.ascontiguousarray(around[2:].reshape(CHUNKS, P).T),
        "dst_rows": dst.reshape(CHUNKS, P),
        "dst_row": dst.reshape(1, EP),
        "first_row": np.ascontiguousarray(dst[first]).reshape(1, CHUNKS),
        "last_row": np.ascontiguousarray(dst[last]).reshape(1, CHUNKS),
        "ends": np.ascontiguousarray(np.stack([dst[first], dst[last], around[first], around[last + 2]], 1)),
        "L0_WlT": np.ascontiguousarray(a["L0_gnn_W_l"].transpose(0, 2, 1)),
        "L0_WrT": np.ascontiguousarray(a["L0_gnn_W_r"].transpose(0, 2, 1)),
        "ln1_b_cols": np.ascontiguousarray(a["L1_gnn_ln1_b"].reshape(KC, P).T),
        "b1_col": np.ascontiguousarray(a["L1_gnn_b1"]).reshape(DFF, 1),
    }
    for name in _SAME:
        arrays[name] = np.ascontiguousarray(a[name])
    for name in _ROWS:
        arrays[name] = np.ascontiguousarray(a[name]).reshape(1, D)
    nc = bacc.Bacc("TRN2", target_bir_lowering=False, num_devices=1)
    t = {n: nc.dram_tensor("in_" + n, v.shape, mybir.dt.from_np(v.dtype), kind="ExternalInput").ap()
         for n, v in arrays.items()}
    out = nc.dram_tensor("out", (NP, D), F32, kind="ExternalOutput").ap()
    build(nc, t, out)
    r = run_bass_kernel_spmd(nc, [{"in_" + n: v for n, v in arrays.items()}], core_ids=[0])
    return np.ascontiguousarray(r.results[0]["out"][:NODES])
```
